# Optimizing a Trainium2 kernel written in Bass

```python
import numpy as np
import jax
import jax.numpy as jnp

def _softmax(x, axis=-1):
    return jax.nn.softmax(x, axis=axis)
def _gelu(x):
    return jax.nn.gelu(x, approximate=True)
def _silu(x):
    return jax.nn.silu(x)
def _sigmoid(x):
    return jax.nn.sigmoid(x)
def _layernorm(x, axis=-1, eps=1e-5):
    m = jnp.mean(x, axis=axis, keepdims=True)
    v = jnp.var(x, axis=axis, keepdims=True)
    return (x - m) / jnp.sqrt(v + eps)
def _scatter_add(tgt, idx, src, axis=0):
    return tgt.at[idx].add(src)
def _segment_sum(src, seg, n):
    return jax.ops.segment_sum(src, seg, n)

kernel_name = 'mk_conv_preact_d4_conv_nhwc256_d386ff'

def setup_inputs(seed: int = 0):
    np.random.seed(seed)
    _w = jnp.asarray
    def _rec_inputs():
        import jax
        import jax.numpy as jnp
        _gk = jax.random.key(seed)
        x = -0.0002023 + 1 * jax.random.normal(jax.random.fold_in(_gk, 1), (8, 56, 56, 256), jnp.float32)
        return x
    x = _rec_inputs()
    def _L0_conv_setup():
        import jax, jax.numpy as jnp
        import numpy as np
        NH, NWIN, TOPK = (8, 7, 4)
        key = jax.random.key(seed)
        ks = jax.random.split(key, 7)
        B, H, W, C = (8, 56, 56, 256)
        return {'x': jax.random.normal(ks[0], (B, H, W, C), jnp.float32), 'qkv_w': jax.random.normal(ks[1], (3 * C, C), jnp.float32) * C ** (-0.5), 'qkv_b': jax.random.normal(ks[2], (3 * C,), jnp.float32) * 0.02, 'lepe_w': jax.random.normal(ks[3], (C, 1, 3, 3), jnp.float32) * 0.1, 'lepe_b': jax.random.normal(ks[4], (C,), jnp.float32) * 0.02, 'out_w': jax.random.normal(ks[5], (C, C), jnp.float32) * C ** (-0.5), 'out_b': jax.random.normal(ks[6], (C,), jnp.float32) * 0.02}
    _L0_conv_all = _L0_conv_setup()
    _L0_conv_in = {k: v for k, v in _L0_conv_all.items() if k in ('qkv_w', 'qkv_b', 'lepe_w', 'lepe_b', 'out_w', 'out_b', )}
    del _L0_conv_all

    def _L1_conv_setup():
        import jax, jax.numpy as jnp
        import numpy as np
        B, H, W, C = (8, 128, 128, 256)
        K, DT, EPS = (5, 0.2, 0.001)
        LAM2 = 4.0

        def _dwconv(x, w):
            k = w.reshape(3, 3, 1, C)
            return jax.lax.conv_general_dilated(x, k, (1, 1), 'SAME', dimension_numbers=('NHWC', 'HWIO', 'NHWC'), feature_group_count=C)

        def _bn(x, gamma, beta, mean, var):
            return (x - mean) * jax.lax.rsqrt(var + EPS) * gamma + beta

        def _sobel(x):
            xp = jnp.pad(x, ((0, 0), (1, 1), (1, 1), (0, 0)), mode='reflect')
            top, mid, bot = (xp[:, :-2], xp[:, 1:-1], xp[:, 2:])
            gy = bot[:, :, :-2] + 2 * bot[:, :, 1:-1] + bot[:, :, 2:] - (top[:, :, :-2] + 2 * top[:, :, 1:-1] + top[:, :, 2:])
            gx = top[:, :, 2:] + 2 * mid[:, :, 2:] + bot[:, :, 2:] - (top[:, :, :-2] + 2 * mid[:, :, :-2] + bot[:, :, :-2])
            return (gy, gx)
        key = jax.random.key(seed)
        ks = jax.random.split(key, 6)
        f = jnp.float32
        d = {}
        d['s0'] = jax.random.normal(ks[0], (B, H, W, C), f)
        d['wg'] = jax.random.normal(ks[1], (3, 3, C), f) * 0.1
        d['wg1'] = jax.random.normal(ks[2], (3, 3, C), f) * 0.1
        for i, p in enumerate(['g', 'g1', 'out']):
            k4 = jax.random.split(ks[3 + i], 4)
            d[p + '_gamma'] = 1.0 + 0.1 * jax.random.normal(k4[0], (C,), f)
            d[p + '_beta'] = 0.1 * jax.random.normal(k4[1], (C,), f)
            d[p + '_mean'] = 0.1 * jax.random.normal(k4[2], (C,), f)
            d[p + '_var'] = 0.5 + jax.random.uniform(k4[3], (C,), f)
        return d
    _L1_conv_all = _L1_conv_setup()
    _L1_conv_in = {k: v for k, v in _L1_conv_all.items() if k in ('wg', 'wg1', 'g_gamma', 'g_beta', 'g_mean', 'g_var', 'g1_gamma', 'g1_beta', 'g1_mean', 'g1_var', 'out_gamma', 'out_beta', 'out_mean', 'out_var', )}
    del _L1_conv_all

    def _L2_conv_setup():
        import jax, jax.numpy as jnp
        import numpy as np
        import math
        WS = 7
        TOPK = 4
        NUM_HEADS = 8

        def _dwconv(v_img, kernel, bias):
            out = jax.lax.conv_general_dilated(v_img, kernel, window_strides=(1, 1), padding='SAME', dimension_numbers=('NHWC', 'HWIO', 'NHWC'), feature_group_count=v_img.shape[-1])
            return out + bias
        key = jax.random.key(seed)
        ks = jax.random.split(key, 12)
        B, H, W, C = (8, 56, 56, 256)
        std = 0.02
        return {'x': jax.random.normal(ks[0], (B, H, W, C), jnp.float32), 'w_qkv': jax.random.normal(ks[1], (C, 3 * C), jnp.float32) * std, 'b_qkv': jnp.zeros((3 * C,), jnp.float32), 'w_g1': jax.random.normal(ks[2], (C, C // 4), jnp.float32) * std, 'b_g1': jnp.zeros((C // 4,), jnp.float32), 'w_g2': jax.random.normal(ks[3], (C // 4, 2), jnp.float32) * std, 'b_g2': jnp.zeros((2,), jnp.float32), 'dw_kernel': jax.random.normal(ks[4], (3, 3, 1, C), jnp.float32) * std, 'dw_bias': jnp.zeros((C,), jnp.float32), 'w_proj': jax.random.normal(ks[5], (C, C), jnp.float32) * std, 'b_proj': jnp.zeros((C,), jnp.float32)}
    _L2_conv_all = _L2_conv_setup()
    _L2_conv_in = {k: v for k, v in _L2_conv_all.items() if k in ('w_qkv', 'b_qkv', 'w_g1', 'b_g1', 'w_g2', 'b_g2', 'dw_kernel', 'dw_bias', 'w_proj', 'b_proj', )}
    del _L2_conv_all

    def _L3_conv_setup():
        import jax, jax.numpy as jnp
        import numpy as np
        B, H, W, C, F, K = (64, 56, 56, 256, 256, 3)

        def _conv(x, w, padding):
            return jax.lax.conv_general_dilated(x, w, window_strides=(1, 1), padding=padding, dimension_numbers=('NHWC', 'HWIO', 'NHWC'))
        key = jax.random.key(seed)
        kx, kw = jax.random.split(key)
        x = jax.random.normal(kx, (B, H, W, C), dtype=jnp.float32)
        stdv = 1.0 / np.sqrt(K * K * C)
        w = (jax.random.normal(kw, (K, K, C, F), dtype=jnp.float32) * stdv).astype(jnp.float32)
        return {'x': x, 'w': w}
    _L3_conv_all = _L3_conv_setup()
    _L3_conv_in = {k: v for k, v in _L3_conv_all.items() if k in ('w', )}
    del _L3_conv_all

    return {
        "x": x,
        "L0_conv_qkv_w": _L0_conv_in["qkv_w"],
        "L0_conv_qkv_b": _L0_conv_in["qkv_b"],
        "L0_conv_lepe_w": _L0_conv_in["lepe_w"],
        "L0_conv_lepe_b": _L0_conv_in["lepe_b"],
        "L0_conv_out_w": _L0_conv_in["out_w"],
        "L0_conv_out_b": _L0_conv_in["out_b"],
        "L1_conv_wg": _L1_conv_in["wg"],
        "L1_conv_wg1": _L1_conv_in["wg1"],
        "L1_conv_g_gamma": _L1_conv_in["g_gamma"],
        "L1_conv_g_beta": _L1_conv_in["g_beta"],
        "L1_conv_g_mean": _L1_conv_in["g_mean"],
        "L1_conv_g_var": _L1_conv_in["g_var"],
        "L1_conv_g1_gamma": _L1_conv_in["g1_gamma"],
        "L1_conv_g1_beta": _L1_conv_in["g1_beta"],
        "L1_conv_g1_mean": _L1_conv_in["g1_mean"],
        "L1_conv_g1_var": _L1_conv_in["g1_var"],
        "L1_conv_out_gamma": _L1_conv_in["out_gamma"],
        "L1_conv_out_beta": _L1_conv_in["out_beta"],
        "L1_conv_out_mean": _L1_conv_in["out_mean"],
        "L1_conv_out_var": _L1_conv_in["out_var"],
        "L2_conv_w_qkv": _L2_conv_in["w_qkv"],
        "L2_conv_b_qkv": _L2_conv_in["b_qkv"],
        "L2_conv_w_g1": _L2_conv_in["w_g1"],
        "L2_conv_b_g1": _L2_conv_in["b_g1"],
        "L2_conv_w_g2": _L2_conv_in["w_g2"],
        "L2_conv_b_g2": _L2_conv_in["b_g2"],
        "L2_conv_dw_kernel": _L2_conv_in["dw_kernel"],
        "L2_conv_dw_bias": _L2_conv_in["dw_bias"],
        "L2_conv_w_proj": _L2_conv_in["w_proj"],
        "L2_conv_b_proj": _L2_conv_in["b_proj"],
        "L3_conv_w": _L3_conv_in["w"],
    }

def reference(x, L0_conv_qkv_w, L0_conv_qkv_b, L0_conv_lepe_w, L0_conv_lepe_b, L0_conv_out_w, L0_conv_out_b, L1_conv_wg, L1_conv_wg1, L1_conv_g_gamma, L1_conv_g_beta, L1_conv_g_mean, L1_conv_g_var, L1_conv_g1_gamma, L1_conv_g1_beta, L1_conv_g1_mean, L1_conv_g1_var, L1_conv_out_gamma, L1_conv_out_beta, L1_conv_out_mean, L1_conv_out_var, L2_conv_w_qkv, L2_conv_b_qkv, L2_conv_w_g1, L2_conv_b_g1, L2_conv_w_g2, L2_conv_b_g2, L2_conv_dw_kernel, L2_conv_dw_bias, L2_conv_w_proj, L2_conv_b_proj, L3_conv_w):
    import jax
    import jax.numpy as jnp
    def _L0_conv_ref(x, qkv_w, qkv_b, lepe_w, lepe_b, out_w, out_b):
        import jax, jax.numpy as jnp
        import numpy as np
        NH, NWIN, TOPK = (8, 7, 4)
        B, H, W, C = x.shape
        nh, nwin, topk = (NH, NWIN, TOPK)
        hd = C // nh
        rh, rw = (H // nwin, W // nwin)
        nreg, S = (nwin * nwin, rh * rw)
        scale = C ** (-0.5)
        xc = jnp.transpose(x, (0, 3, 1, 2))
        qkv = jnp.einsum('bchw,oc->bohw', xc, qkv_w) + qkv_b[None, :, None, None]
        q, k, v = jnp.split(qkv, 3, axis=1)

        def pool(t):
            t = t.reshape(B, C, nwin, rh, nwin, rw)
            return t.mean(axis=(3, 5))
        q_r = jax.lax.stop_gradient(pool(q)).transpose(0, 2, 3, 1).reshape(B, nreg, C)
        k_r = jax.lax.stop_gradient(pool(k)).reshape(B, C, nreg)
        a_r = q_r @ k_r
        idx_r = jax.lax.top_k(a_r, topk)[1]

        def g2s(t):
            t = t.reshape(B, nh, hd, nwin, rh, nwin, rw)
            return jnp.einsum('bmdhpwq->bmhwpqd', t).reshape(B, nh, nreg, S, hd)
        qs, ks_, vs = (g2s(q), g2s(k), g2s(v))
        rg = jnp.broadcast_to(idx_r[:, None], (B, nh, nreg, topk))
        bI = jnp.arange(B)[:, None, None, None]
        hI = jnp.arange(nh)[None, :, None, None]
        key_g = ks_[bI, hI, rg]
        val_g = vs[bI, hI, rg]
        TS = topk * S
        attn = jnp.einsum('bhnsd,bhnkd->bhnsk', qs * scale, key_g.reshape(B, nh, nreg, TS, hd))
        k2 = TS // 8
        score, index = jax.lax.top_k(attn, k2)
        vflat = val_g.reshape(B, nh, nreg, TS, hd)
        bI2 = jnp.arange(B)[:, None, None, None, None]
        hI2 = jnp.arange(nh)[None, :, None, None, None]
        nI2 = jnp.arange(nreg)[None, None, :, None, None]
        v_sel = vflat[bI2, hI2, nI2, index]
        a_g = jax.nn.softmax(score, axis=-1)
        out = jnp.einsum('bhnsk,bhnskd->bhnsd', a_g, v_sel)
        out = out.reshape(B, nh, nwin, nwin, rh, rw, hd)
        out = jnp.einsum('bmhwpqd->bmdhpwq', out).reshape(B, C, H, W)
        lepe = jax.lax.conv_general_dilated(v, lepe_w, (1, 1), 'SAME', feature_group_count=C) + lepe_b[None, :, None, None]
        out = out + lepe
        out = jnp.einsum('bchw,oc->bohw', out, out_w) + out_b[None, :, None, None]
        return jnp.transpose(out, (0, 2, 3, 1))

    def _L1_conv_ref(s0, wg, wg1, g_gamma, g_beta, g_mean, g_var, g1_gamma, g1_beta, g1_mean, g1_var, out_gamma, out_beta, out_mean, out_var):
        import jax, jax.numpy as jnp
        import numpy as np
        B, H, W, C = (8, 128, 128, 256)
        K, DT, EPS = (5, 0.2, 0.001)
        LAM2 = 4.0

        def _dwconv(x, w):
            k = w.reshape(3, 3, 1, C)
            return jax.lax.conv_general_dilated(x, k, (1, 1), 'SAME', dimension_numbers=('NHWC', 'HWIO', 'NHWC'), feature_group_count=C)

        def _bn(x, gamma, beta, mean, var):
            return (x - mean) * jax.lax.rsqrt(var + EPS) * gamma + beta

        def _sobel(x):
            xp = jnp.pad(x, ((0, 0), (1, 1), (1, 1), (0, 0)), mode='reflect')
            top, mid, bot = (xp[:, :-2], xp[:, 1:-1], xp[:, 2:])
            gy = bot[:, :, :-2] + 2 * bot[:, :, 1:-1] + bot[:, :, 2:] - (top[:, :, :-2] + 2 * top[:, :, 1:-1] + top[:, :, 2:])
            gx = top[:, :, 2:] + 2 * mid[:, :, 2:] + bot[:, :, 2:] - (top[:, :, :-2] + 2 * mid[:, :, :-2] + bot[:, :, :-2])
            return (gy, gx)
        fsrc = s0
        h = s0
        h0 = fsrc
        g = jax.nn.relu(_bn(_dwconv(h, wg), g_gamma, g_beta, g_mean, g_var))
        g1 = jax.nn.relu(_bn(_dwconv(h, wg1), g1_gamma, g1_beta, g1_mean, g1_var))
        gy, gx = _sobel(h)
        Dx = 1.0 / (gy * gy / LAM2 + 1.0)
        Dy = 1.0 / (gx * gx / LAM2 + 1.0)
        ux = 0.5 * (jnp.roll(g, 1, axis=2) - jnp.roll(g, -1, axis=2))
        vy = 0.5 * (jnp.roll(g1, 1, axis=3) - jnp.roll(g1, -1, axis=3))
        Ax, Ay = (g * DT, g1 * DT)
        Bx, By = (Dx * DT, Dy * DT)
        E = (ux + vy) * DT
        D = 1.0 / (1.0 + 2.0 * Bx + 2.0 * By)
        cm_x, cp_x = (-Ax + 2.0 * Bx, Ax + 2.0 * Bx)
        cm_y, cp_y = (-Ay + 2.0 * By, Ay + 2.0 * By)
        c0 = 1.0 - 2.0 * Bx - 2.0 * By
        for _ in range(K):
            prev = h
            h = D * (c0 * h0 - 2.0 * E * h + cm_x * jnp.roll(h, 1, axis=2) + cp_x * jnp.roll(h, -1, axis=2) + cm_y * jnp.roll(h, 1, axis=3) + cp_y * jnp.roll(h, -1, axis=3))
            h = h + D * (2.0 * DT) * fsrc
            h0 = prev
        return jax.nn.relu(_bn(h, out_gamma, out_beta, out_mean, out_var))

    def _L2_conv_ref(x, w_qkv, b_qkv, w_g1, b_g1, w_g2, b_g2, dw_kernel, dw_bias, w_proj, b_proj):
        import jax, jax.numpy as jnp
        import numpy as np
        import math
        WS = 7
        TOPK = 4
        NUM_HEADS = 8

        def _dwconv(v_img, kernel, bias):
            out = jax.lax.conv_general_dilated(v_img, kernel, window_strides=(1, 1), padding='SAME', dimension_numbers=('NHWC', 'HWIO', 'NHWC'), feature_group_count=v_img.shape[-1])
            return out + bias
        B, H, W, C = x.shape
        ws = WS
        nH, nW = (H // ws, W // ws)
        S, ntok = (nH * nW, ws * ws)
        t = min(TOPK, S)
        scale = (C // NUM_HEADS) ** (-0.5)
        xw = x.reshape(B, nH, ws, nW, ws, C).transpose(0, 1, 3, 2, 4, 5).reshape(B, S, ntok, C)
        x_region = xw.mean(axis=2)
        qkv_r = (x_region @ w_qkv + b_qkv).reshape(B, S, 3, C)
        q_r, k_r = (qkv_r[:, :, 0], qkv_r[:, :, 1])
        A_r = jnp.einsum('bsc,bzc->bsz', q_r, k_r) * scale
        _, topk_idx = jax.lax.top_k(A_r, t)
        gp = jax.nn.relu(q_r @ w_g1 + b_g1) @ w_g2 + b_g2
        sigma = jax.nn.softplus(gp) + 0.5
        s_side = int(round(math.sqrt(S)))
        coords = jnp.arange(s_side, dtype=x.dtype)
        gy, gx = jnp.meshgrid(coords, coords, indexing='ij')
        mu = jnp.stack([gx.ravel(), gy.ravel()], axis=-1)
        d = mu[None, :, :] - mu[:, None, :]
        z = (d[..., 0][None] / sigma[..., 0][:, :, None]) ** 2 + (d[..., 1][None] / sigma[..., 1][:, :, None]) ** 2
        gauss = jnp.exp(-0.5 * z)
        gauss = gauss / (gauss.sum(-1, keepdims=True) + 1e-06)
        gwt = jnp.take_along_axis(gauss, topk_idx, axis=2)
        qkv = (xw @ w_qkv + b_qkv).reshape(B, S, ntok, 3, C)
        q, k, v = (qkv[..., 0, :], qkv[..., 1, :], qkv[..., 2, :])
        gather = jax.vmap(lambda a, i: a[i])
        k_g = (gather(k, topk_idx) * gwt[..., None, None]).reshape(B, S, t * ntok, C)
        v_g = (gather(v, topk_idx) * gwt[..., None, None]).reshape(B, S, t * ntok, C)
        attn = jax.nn.softmax(jnp.einsum('bswc,bskc->bswk', q, k_g) * scale, axis=-1)
        out = jnp.einsum('bswk,bskc->bswc', attn, v_g)
        vdw = _dwconv(v.reshape(B * S, ws, ws, C), dw_kernel, dw_bias).reshape(B, S, ntok, C)
        out = out + vdw
        out = out.reshape(B, nH, nW, ws, ws, C).transpose(0, 1, 3, 2, 4, 5).reshape(B, H, W, C)
        return out @ w_proj + b_proj

    def _L3_conv_ref(x, w):
        import jax, jax.numpy as jnp
        import numpy as np
        B, H, W, C, F, K = (64, 56, 56, 256, 256, 3)

        def _conv(x, w, padding):
            return jax.lax.conv_general_dilated(x, w, window_strides=(1, 1), padding=padding, dimension_numbers=('NHWC', 'HWIO', 'NHWC'))
        wq = w.astype(jnp.float16).astype(jnp.float32)
        wb = jnp.sign(jnp.clip(wq, -1.0, 1.0))
        return _conv(x, wb, 'SAME')

    def _gn(v, G=32, eps=1e-5):
        B_, H_, W_, C_ = v.shape
        g = v.reshape(B_, H_, W_, G, C_ // G)
        m = jnp.mean(g, axis=(1, 2, 4), keepdims=True)
        s = jnp.var(g, axis=(1, 2, 4), keepdims=True)
        return ((g - m) / jnp.sqrt(s + eps)).reshape(v.shape)

    def _ln_c(v, eps=1e-6):
        m = jnp.mean(v, axis=-1, keepdims=True)
        s = jnp.var(v, axis=-1, keepdims=True)
        return (v - m) / jnp.sqrt(s + eps)

    def _ln_t(v, eps=1e-5):
        m = jnp.mean(v, axis=-1, keepdims=True)
        s = jnp.var(v, axis=-1, keepdims=True)
        return (v - m) / jnp.sqrt(s + eps)

    def _to_tokens(v):
        B_, H_, W_, C_ = v.shape
        return v.reshape(B_, H_ * W_, C_)
    def _from_tokens(t, like):
        return t.reshape(like.shape)

    x = x + _L0_conv_ref(_gn(x), L0_conv_qkv_w, L0_conv_qkv_b, L0_conv_lepe_w, L0_conv_lepe_b, L0_conv_out_w, L0_conv_out_b)
    x = x + _L1_conv_ref(_gn(x), L1_conv_wg, L1_conv_wg1, L1_conv_g_gamma, L1_conv_g_beta, L1_conv_g_mean, L1_conv_g_var, L1_conv_g1_gamma, L1_conv_g1_beta, L1_conv_g1_mean, L1_conv_g1_var, L1_conv_out_gamma, L1_conv_out_beta, L1_conv_out_mean, L1_conv_out_var)
    x = x + _L2_conv_ref(_gn(x), L2_conv_w_qkv, L2_conv_b_qkv, L2_conv_w_g1, L2_conv_b_g1, L2_conv_w_g2, L2_conv_b_g2, L2_conv_dw_kernel, L2_conv_dw_bias, L2_conv_w_proj, L2_conv_b_proj)
    x = x + _L3_conv_ref(_gn(x), L3_conv_w)
    return x


_drawn_inputs = setup_inputs


def setup_inputs(seed=0):
    import zlib

    import numpy as np

    out = dict(_drawn_inputs(seed))
    spreads = {'L2_conv_b_qkv': (0.0, 0.8),
     'L2_conv_b_g1': (0.0, 2.0),
     'L2_conv_b_g2': (0.0, 2.0),
     'L2_conv_dw_bias': (0.0, 0.45),
     'L2_conv_b_proj': (0.0, 0.1)}
    factors = {'L0_conv_lepe_b': 2.745,
     'L1_conv_g_gamma': 8.0,
     'L1_conv_g_beta': 3.315,
     'L1_conv_g_mean': 3.076,
     'L1_conv_g_var': 4.311,
     'L1_conv_g1_gamma': 8.0,
     'L1_conv_g1_beta': 3.117,
     'L1_conv_g1_mean': 3.125,
     'L1_conv_g1_var': 5.338,
     'L2_conv_w_qkv': 8.0,
     'L2_conv_w_g1': 8.0,
     'L2_conv_w_g2': 8.0,
     'L2_conv_dw_kernel': 8.0,
     'L2_conv_w_proj': 2.83}
    for name, (base, spread) in spreads.items():
        noise = np.random.default_rng([zlib.crc32(name.encode()), seed]).standard_normal(out[name].shape)
        drawn = base * np.exp(spread * noise) if base else spread * noise
        out[name] = jnp.asarray(drawn.astype(out[name].dtype))
    for name, factor in factors.items():
        out[name] = (out[name] * factor).astype(out[name].dtype)
    return out
```

```python
from contextlib import ExitStack

import numpy as np

import concourse.bass as bass
from concourse import mybir

ALU = mybir.AluOpType
ACT = mybir.ActivationFunctionType
AX = mybir.AxisListType
F32 = mybir.dt.float32
BF16 = mybir.dt.bfloat16
F16 = mybir.dt.float16
U32 = mybir.dt.uint32
SP, POOL = mybir.EngineType.SP, mybir.EngineType.Pool

P = 128
H = W = 56
C = 256
N = H * W
PW = W + 2
PN = (H + 2) * PW
TAPS = 9
CHUNK = 448
CHUNKS = N // CHUNK
TOK = 112

R0, S0 = 7, 8
REG0, TOK0 = R0 * R0, S0 * S0
TOPK = 4
HD = 32
TILES = 4
KEYS0 = TOPK * TOK0
KEPT = KEYS0 // 8
VS = 4
LAPS = (REG0 - 1) // (2 * VS)
SECOND_HALF = {1: range(0, 3), 2: range(3, 6), 3: range(6, 9)}
FIRST_HALF = {4: range(0, 2), 5: range(2, 4), 6: range(4, 6), 7: range(6, 8), 8: range(8, 9)}
REMOVED = -1.0e30
SCALE0 = float(C) ** -0.5
R2, S2 = 8, 7
REG2, TOK2 = R2 * R2, S2 * S2
KEYS2 = TOPK * TOK2
HK2 = 2 * TOK2
SCALE2 = float(C // 8) ** -0.5
VW2 = 64
VOFF2 = 16
DT = 0.2
STEPS = 5
BN_EPS = 0.001
ROWS1 = 14
CH1 = H // ROWS1
E1 = ROWS1 * W


class Stage:

    def __init__(self, sem, per, credit=0):
        self.sem, self.per, self.credit = sem, per, credit

    def at(self, img, k):
        return self.sem, img * self.per + (k + self.credit)


def build_blocks(nc, x, w0_qkv, b0_qkv, w0_lepe, b0_lepe, w0_out, b0_out,
                 w1_g, w1_g1, bn1,
                 w2_qkv, b2_qkv, w2_g1, b2_g1, w2_g2, b2_g2, w2_dw, b2_dw, w2_proj, b2_proj,
                 w3, mats, posd, out, LAYERS=4):
    B = x.shape[0]
    with ExitStack() as ctx:
        stages = []

        def sb(name, shape, dt=F32):
            return ctx.enter_context(nc.sbuf_tensor(name, shape, dt))

        def dram(name, shape, dt=F32):
            return nc.dram_tensor(name, shape, dt, kind="Internal").ap()

        def stage(name, per, credit=0):
            stages.append(Stage(ctx.enter_context(nc.semaphore(name)), per, credit))
            return stages[-1]

        q_dram = dram("q_dram", [P, REG0, 2, TOK0])
        k_dram = dram("k_dram", [P, REG0, 2, TOK0])
        v_dram = dram("v_dram", [REG0, TOK0, C])
        q2_dram = dram("q2_dram", [P, REG2, 2, TOK2])
        k2_dram = dram("k2_dram", [P, REG2, 2, TOK2])
        v2_dram = dram("v2_dram", [REG2, TOK2, C])
        idx0_dram = dram("idx0_dram", [REG0, TOPK], U32)
        idx2_dram = dram("idx2_dram", [REG2, TOPK], U32)
        gw_dram = dram("gw_dram", [REG2, TOPK])

        bank = ctx.enter_context(nc.psum_tensor("bank", [P, 8, 512], F32))

        res = sb("res", [P, 2, N])
        xnp = sb("xnp", [P, 2, H + 2, PW])
        vpad = sb("vpad", [P, 2 * PN + 2 * E1])
        att = sb("att", [P, 2, N])
        w0t = sb("w0t", [P, 2, 3, 2, P])
        o0t = sb("o0t", [P, 2, 2, P])
        w2s = sb("w2s", [P, 2, 3 * C])
        p2s = sb("p2s", [P, 2, C])
        diag = sb("diag", [P, TAPS, 2, P])
        mat = sb("mat", [P, 6, P])
        w3s = sb("w3s", [P, TAPS, 2, C], BF16)
        wg1s = sb("wg1s", [P, 2, REG2])
        wg2s = sb("wg2s", [REG2, 4])
        bg2s = sb("bg2s", [1, 2 + REG2])
        posd_s = sb("posd_s", [REG2, 3, REG2])
        diag_g1 = sb("diag_g1", [P, TAPS, 2, P])
        bias0 = sb("bias0", [P, 3, 2])
        bias2 = sb("bias2", [P, 3, 2])
        small = sb("small", [P, 64])
        lepe_w = sb("lepe_w", [P, 2, TAPS])
        dw2_w = sb("dw2_w", [P, 2, TAPS])
        g_w = sb("g_w", [P, 2, TAPS])
        g1_w = sb("g1_w", [P, 2, TAPS])
        bns = sb("bns", [P, 2, 12])
        bnc = sb("bnc", [P, 3, 2, 2])
        stats = sb("stats", [P, 2, CHUNKS, 6])
        mv = sb("mv", [P, 2, 2])
        ms = sb("ms", [P, 2, 2])
        grp = sb("grp", [P, 2, 2])
        gm = sb("gm", [P, 8])
        SC = 13056
        scratch = sb("scratch", [P, SC])

        ident = mat[:, 0, :]
        lepe_b, out0_b = small[:, 0:2], small[:, 2:4]
        dw2_b, proj_b = small[:, 4:6], small[:, 6:8]

        top = [0]

        def carve(n, **shape):
            assert top[0] + n <= SC, (top[0], n)
            v = scratch[:, top[0]:top[0] + n]
            top[0] += n
            return v

        top[0] = 0
        tok = carve(2 * 4 * C).rearrange("p (s k c) -> p s k c", s=2, k=4)
        top[0] = 0
        qks_flat = carve(2 * R0 * 2 * TOK0)
        qks = [qks_flat[:, 0:2 * R * 2 * T].rearrange("p (k w a t) -> p k w a t", k=2, w=R, a=2) for R, T in ((R0, TOK0), (R2, TOK2))]
        vrow = carve(2 * CHUNK).rearrange("p (a n) -> p a n", a=2)
        vtk = carve(R2 * C).rearrange("p (w c) -> p w c", w=R2)
        pool_flat, mean_flat, qkr_flat = carve(2 * H * R2), carve(2 * REG2), carve(4 * REG2)
        pool_a = [pool_flat[:, 0:2 * H * R].rearrange("p (q y w) -> p q y w", q=2, y=H) for R in (R0, R2)]
        pool_m = [mean_flat[:, 0:2 * R * R].rearrange("p (q r) -> p q r", q=2) for R in (R0, R2)]
        qkr = [qkr_flat[:, 0:4 * R * R].rearrange("p (k a r) -> p k a r", k=2, a=2) for R in (R0, R2)]
        aff = carve(REG2)
        v8 = carve(8)
        i8 = carve(8).bitcast(U32)
        idx_row = carve(REG2 * TOPK).bitcast(U32)
        base_attn = top[0]
        qg = carve(2 * 2 * TOK0).rearrange("p (s a t) -> p s a t", s=2, a=2)
        kg = carve(2 * TOPK * 2 * TOK0).rearrange("p (s t a n) -> p s t a n", s=2, t=TOPK, a=2)
        vg = carve(VS * 2 * C).rearrange("p (s c n) -> p s c n", s=VS, c=2)
        sc_sb = carve(2 * TILES * KEYS0).rearrange("p (s j n) -> p s j n", s=2, j=TILES)
        top[0] = 0
        rem = carve(TILES * KEYS0).rearrange("p (j n) -> p j n", j=TILES)
        ee = carve(TILES * KEYS0).rearrange("p (j n) -> p j n", j=TILES)
        er = carve(TILES * KEYS0).rearrange("p (j n) -> p j n", j=TILES)
        pt = carve(2 * 2 * P).rearrange("p (s c n) -> p s c n", s=2, c=2)
        best = carve(2 * TILES * KEPT).rearrange("p (s j n) -> p s j n", s=2, j=TILES)
        ebest = carve(TILES * KEPT).rearrange("p (j n) -> p j n", j=TILES)
        nmax = carve(2 * TILES).rearrange("p (s j) -> p s j", s=2)
        zsum = carve(2 * TILES).rearrange("p (s j) -> p s j", s=2)
        rz = carve(2 * TILES).rearrange("p (s j) -> p s j", s=2)
        osb = carve(TILES * HD).rearrange("p (j d) -> p j d", j=TILES)
        assert top[0] <= base_attn - REG2 * TOPK, (top[0], base_attn)
        top[0] = base_attn
        hid = carve(REG2)
        sig = carve(16)
        gauss = carve(REG2)
        idx_f = carve(8)
        gsum = carve(2)
        gwt = carve(TOPK)
        gws = carve((REG2 // 2) * TOPK).rearrange("p (u t) -> p u t", t=TOPK)
        q2g_flat = carve(2 * 2 * 2 * 64)
        q2g = q2g_flat.rearrange("p (s i a t) -> p s i a t", s=2, i=2, a=2)
        k2g = carve(2 * 2 * TOPK * 2 * TOK2).rearrange("p (s i t a n) -> p s i t a n", s=2, i=2, t=TOPK, a=2)
        v2g = carve(VS * 2 * 2 * C).rearrange("p (s i c n) -> p s i c n", s=VS, i=2, c=2)
        top[0] = 0
        lg2 = carve(2 * KEYS2).rearrange("p (s n) -> p s n", s=2)
        e2 = carve(2 * KEYS2).rearrange("p (s n) -> p s n", s=2)
        w2p = carve(2 * KEYS2).rearrange("p (s n) -> p s n", s=2)
        pt2 = carve(2 * 2 * P).rearrange("p (s c n) -> p s c n", s=2, c=2)
        max2, z2, rz2 = carve(2), carve(2), carve(2)
        assert top[0] <= base_attn - REG2 * TOPK
        vp16 = vpad[:, 0:2 * PN].bitcast(BF16)
        parts = [v.rearrange("p (q y x) -> p q y x", q=2, y=H + 2) for v in
                 (vp16[:, 0:2 * PN], vp16[:, 2 * PN:4 * PN], att[:, :, :].rearrange("p a n -> p (a n)")[:, 0:PN].bitcast(BF16))]
        w3raw = scratch[:, 0:TAPS * 2 * C]
        w3half = scratch[:, TAPS * 2 * C:TAPS * 3 * C].bitcast(F16)
        top[0] = 0
        otmp = carve(2 * 2 * CHUNK).rearrange("p (s q n) -> p s q n", s=2, q=2)

        top[0] = 0
        A1 = 2 * E1
        arrays1 = [carve(A1) for _ in range(8)] + [att[:, :, :].rearrange("p a n -> p (a n)")[:, k * A1:(k + 1) * A1] for k in range(4)] + [vpad[:, 2 * PN:2 * PN + A1]]
        c0, cE, cmx, cpx, cmy, cpy, cF, hA, hB, acc, prod, ax1, ay1 = [a.rearrange("p (q n) -> p q n", q=2) for a in arrays1]

        V2A = VOFF2 + REG2 * VW2 + 16
        def v2_view(a, shift):
            o = a * V2A + VOFF2 + shift
            return vpad[:, o:o + REG2 * VW2].rearrange("p (w y x) -> p w y x", y=8, x=8)

        VP0 = vpad[:, 0:2 * PN].rearrange("p (a y x) -> p a y x", a=2, y=H + 2)

        passed = ctx.enter_context(nc.semaphore("passed"))
        const_in = stage("const_in", 0)
        wraw_in = stage("wraw_in", 0)
        w_turned = stage("w_turned", 0)
        w_copied = stage("w_copied", 0)
        zeroed = stage("zeroed", 0)
        x_in = [stage(f"x_in{s}", 16 * (4 - s)) for s in range(2)]
        x_turned = stage("x_turned", 2 * CHUNKS)
        x_evac_a = stage("x_evac_a", CHUNKS)
        x_evac_v = stage("x_evac_v", CHUNKS)
        gn_ms = stage("gn_ms", LAYERS)
        gn_grp = stage("gn_grp", LAYERS)
        gn_var = stage("gn_var", LAYERS)
        gn_sqrt = stage("gn_sqrt", LAYERS)
        gn_coef = stage("gn_coef", LAYERS)
        xn_a = stage("xn_a", LAYERS)
        xn_v = stage("xn_v", LAYERS)
        res_done = stage("res_done", LAYERS, 1)
        bn_sqrt = stage("bn_sqrt", 0)
        bn_ready = stage("bn_ready", 0)
        bn_var = stage("bn_var", 0)
        mirror_in = stage("mirror_in", 1)
        mirrored = stage("mirrored", 1)
        g_mm = stage("g_mm", 2 * CH1)
        g1_mm = stage("g1_mm", 2 * CH1)
        ax_evac = stage("ax_evac", 2 * CH1)
        ay_evac = stage("ay_evac", 2 * CH1)
        sobel_done = stage("sobel_done", 2 * CH1)
        squared = stage("squared", 2 * CH1)
        e_diff = stage("e_diff", CH1)
        coef_done = stage("coef_done", CH1)
        h_set = stage("h_set", CH1)
        h_ready = stage("h_ready", CH1 * STEPS)
        shifted = stage("shifted", CH1 * STEPS)
        own_part = stage("own_part", CH1 * STEPS)
        y1_ready = stage("y1_ready", CH1)
        y1_added = stage("y1_added", CH1, 1)
        NR = (R0, R2)
        qkv_mm = [stage(f"qkv_mm{l}", 6 * NR[l]) for l in range(2)]
        qk_evac_a = [stage(f"qk_evac_a{l}", 3 * NR[l], 4) for l in range(2)]
        qkv_evac_v = [stage(f"qkv_evac_v{l}", 3 * NR[l], 4) for l in range(2)]
        v_padded = [stage(f"v_padded{l}", NR[l], 1) for l in range(2)]
        v_turned = [stage(f"v_turned{l}", 4 * NR[l], 1) for l in range(2)]
        vtk_evac = [stage(f"vtk_evac{l}", 4 * NR[l], 4) for l in range(2)]
        qk_out = [stage(f"qk_out{l}", 32 * NR[l], 1) for l in range(2)]
        v_out = [stage(f"v_out{l}", 16 * NR[l], 1) for l in range(2)]
        pooled = [stage(f"pooled{l}", 1) for l in range(2)]
        qkr_mm = [stage(f"qkr_mm{l}", 1) for l in range(2)]
        qkr_evac = [stage(f"qkr_evac{l}", 1) for l in range(2)]
        aff_mm = [stage(f"aff_mm{l}", 1) for l in range(2)]
        idx_found = [stage(f"idx_found{l}", 1) for l in range(2)]
        idx_out = [stage(f"idx_out{l}", 16) for l in range(2)]
        idx_in = [stage(f"idx_in{l}", 16) for l in range(2)]
        kq_in = [stage(f"kq_in{s}", 16 * 5 * (25 - s)) for s in range(2)]
        v_in = [stage(f"v_in{s}", 16 * 4 * len(range(s, REG0, VS))) for s in range(VS)]
        NT = REG0 * TILES
        scored = stage("scored", NT)
        s_copied = stage("s_copied", NT, 4)
        topk_step = ctx.enter_context(nc.semaphore("topk_step"))
        topped = stage("topped", NT)
        exped = stage("exped", NT, 4)
        kept = stage("kept", NT)
        p_turned = stage("p_turned", NT, 4)
        pt_evac = stage("pt_evac", NT, 4)
        pv_done = stage("pv_done", REG0)
        o_norm = stage("o_norm", REG0, 1)
        o_turned = stage("o_turned", REG0, 1)
        o_evac = stage("o_evac", REG0, 1)
        lepe_mm = stage("lepe_mm", 2 * R0)
        lepe_evac = stage("lepe_evac", 2 * R0, 1)
        hid_mm = stage("hid_mm", 1)
        hid_relu = stage("hid_relu", 1)
        gate_mm = stage("gate_mm", 1)
        gate_neg = stage("gate_neg", 1)
        gate_exp = stage("gate_exp", 1)
        gate_one = stage("gate_one", 1)
        gate_ln = stage("gate_ln", 1)
        dist_done = stage("dist_done", 1)
        gauss_exp = stage("gauss_exp", 1)
        gwt_done = stage("gwt_done", 1)
        gw_out = stage("gw_out", 16)
        gw_in = stage("gw_in", 32)
        q2_zeroed = stage("q2_zeroed", 1)
        vp_zeroed = stage("vp_zeroed", 1)
        NP2 = REG2 // 2
        kq2_in = [stage(f"kq2_in{s}", 16 * 9 * NP2 // 2) for s in range(2)]
        v2_in = [stage(f"v2_in{s}", 16 * 8 * NP2 // VS) for s in range(VS)]
        scored2 = stage("scored2", NP2)
        logit2 = stage("logit2", NP2, 2)
        exped2 = stage("exped2", NP2, 2)
        weighted2 = stage("weighted2", NP2, 2)
        turned2 = stage("turned2", NP2, 2)
        pt2_evac = stage("pt2_evac", NP2, 2)
        pv2_done = stage("pv2_done", NP2)
        out2_evac = stage("out2_evac", NP2, 2)
        w3_half = stage("w3_half", 0)
        w3_made = stage("w3_made", 0)
        part_made = [stage(f"part_made{k}", 2) for k in range(3)]
        rest_made = stage("rest_made", 2)
        c3_mm = stage("c3_mm", CHUNKS)
        c3_added = stage("c3_added", 2 * CHUNKS, 3)
        diag_made = [stage(f"diag_made{k}", 1) for k in range(4)]
        om_mm = [stage(f"om_mm{l}", 2 * NR[l]) for l in range(2)]
        om_evac = [stage(f"om_evac{l}", 2 * NR[l], 4) for l in range(2)]
        om_added = [stage(f"om_added{l}", 2 * NR[l], 4) for l in range(2)]
        y_turned = stage("y_turned", 2 * CHUNKS)
        y_evac = stage("y_evac", 2 * CHUNKS)
        y_out = [stage(f"y_out{s}", 16 * (4 - s)) for s in range(2)]

        wraw = xnp[:, :, :, :].rearrange("p q y x -> p (q y x)")
        w0raw = wraw[:, 0:6 * C].rearrange("p (m c) -> p m c", m=6)
        o0raw = wraw[:, 6 * C:8 * C].rearrange("p (m c) -> p m c", m=2)

        BLK = (S0 * S0 * R0, S2 * S2 * R2)
        SS, RR = (S0, S2), (R0, R2)

        def region_view(img3, l, row):
            s = SS[l]
            return img3[:, bass.ds(row * s, s), :].rearrange("p y (w x) -> p w y x", x=s)

        CREDITS = [st for st in stages if st.credit]
        CONSTS = 16 * (7 + 9 + 10)
        block = ctx.enter_context(nc.Block())

        def sp_project(sp, img, l):
            R, T = RR[l], (TOK0, TOK2)[l]
            qd, kd, vd = ((q_dram, k_dram, v_dram), (q2_dram, k2_dram, v2_dram))[l]
            with sp.Fori(0, R) as i:
                sp.wait_ge(*qk_evac_a[l].at(img, 3 * i + 3))
                sp.sem_inc(passed, 1)
                sp.wait_ge(*qkv_evac_v[l].at(img, 3 * i + 1))
                sp.dma_start(qd[:, bass.ds(i * R, R)], qks[l][:, 0]).then_inc(qk_out[l].sem, 16)
                sp.dma_start(kd[:, bass.ds(i * R, R)], qks[l][:, 1]).then_inc(qk_out[l].sem, 16)
                sp.wait_ge(*vtk_evac[l].at(img, 4 * i + 4))
                sp.dma_start(vd[bass.ds(i * R, R)].rearrange("w t c -> t w c"), vtk[0:T, 0:R]).then_inc(v_out[l].sem, 16)
            idd = (idx0_dram, idx2_dram)[l]
            sp.wait_ge(*idx_found[l].at(img, 1))
            sp.dma_start(idd[:, :], i8[0:R * R, 0:TOPK]).then_inc(idx_out[l].sem, 16)
            sp.wait_ge(*idx_out[l].at(img, 16))
            sp.dma_start(idx_row[0:1, 0:R * R * TOPK], idd.rearrange("(o r) t -> o (r t)", o=1)).then_inc(idx_in[l].sem, 16)
            sp.wait_ge(*idx_in[l].at(img, 16))
            sp.wait_ge(*qk_out[l].at(img, 32 * R))
            sp.wait_ge(*v_out[l].at(img, 16 * R))

        def numbers(engine, at, n, limit):
            return nc.values_load_multi_w_load_instructions(idx_row[0:1, bass.ds(at, n)], engines=(engine,), min_val=0, max_val=limit - 1)[1]

        def sp_gather0(sp, img):
            def gather(r, s, v, wait, wait_v):
                ids = numbers(SP, r * TOPK, TOPK, REG0)
                if wait:
                    sp.wait_ge(*scored.at(img, (r - 1) * TILES))
                sp.dma_start(qg[:, s], q_dram[:, bass.ds(r, 1)].rearrange("p r a t -> p (r a) t")).then_inc(kq_in[s].sem, 16)
                for t in range(TOPK):
                    sp.dma_start(kg[:, s, t], k_dram[:, bass.ds(ids[t], 1)].rearrange("p r a t -> p (r a) t")).then_inc(kq_in[s].sem, 16)
                if wait_v:
                    sp.wait_ge(*pv_done.at(img, r - VS + 1))
                for t in range(TOPK):
                    sp.dma_start(vg[64 * (t % 2):64 * (t % 2) + 64, v, t // 2], v_dram[bass.ds(ids[t], 1)].rearrange("r t c -> (r t) c")).then_inc(v_in[v].sem, 16)
            sp.sem_inc(passed, 1)
            for r in range(VS):
                gather(r, r % 2, r, r >= 2, False)
            with sp.Fori(1, REG0 // VS) as i:
                for v in range(VS):
                    gather(VS * i + v, v % 2, v, True, True)
            gather(REG0 - 1, 0, 0, True, True)

        def sp_gather2(sp, img):
            sp.wait_ge(*gwt_done.at(img, 1))
            sp.dma_start(gw_dram, gwt[0:REG2, :]).then_inc(gw_out.sem, 16)
            sp.wait_ge(*gw_out.at(img, 16))
            for i in range(2):
                sp.dma_start(gws[64 * i:64 * i + 64], gw_dram.rearrange("(o w i) t -> i o w t", i=2, o=1)[i].to_broadcast([64, NP2, TOPK])).then_inc(gw_in.sem, 16)
            sp.wait_ge(*q2_zeroed.at(img, 1))

            def gather(u, s, wait):
                sp.sem_inc(passed, 1)
                ids = numbers(SP, 2 * u * TOPK, 2 * TOPK, REG2)
                if wait:
                    sp.wait_ge(*scored2.at(img, u - 1))
                sp.dma_start(q2g[:, s, :, :, 0:TOK2].rearrange("p i a t -> p (i a) t"), q2_dram[:, bass.ds(2 * u, 2)].rearrange("p r a t -> p (r a) t")).then_inc(kq2_in[s].sem, 16)
                for i in range(2):
                    for t in range(TOPK):
                        sp.dma_start(k2g[:, s, i, t], k2_dram[:, bass.ds(ids[i * TOPK + t], 1)].rearrange("p r a t -> p (r a) t")).then_inc(kq2_in[s].sem, 16)


            gather(0, 0, False)
            gather(1, 1, False)
            with sp.Fori(1, NP2 // 2) as n:
                gather(2 * n, 0, True)
                gather(2 * n + 1, 1, True)

        def pool_gather2(pool, img):
            def gather(u, s, wait):
                ids = numbers(POOL, 2 * u * TOPK, 2 * TOPK, REG2)
                if wait:
                    pool.wait_ge(*pv2_done.at(img, u - VS + 1))
                for i in range(2):
                    for t in range(TOPK):
                        pool.dma_start(v2g[TOK2 * (t % 2):TOK2 * (t % 2) + TOK2, s, i, t // 2],
                                     v2_dram[bass.ds(ids[i * TOPK + t], 1)].rearrange("r t c -> (r t) c")).then_inc(v2_in[s].sem, 16)
            pool.wait_ge(*v_out[1].at(img, 16 * R2))
            pool.wait_ge(*idx_in[1].at(img, 16))
            pool.sem_inc(passed, 1)
            for v in range(VS):
                gather(v, v, False)
            with pool.Fori(1, NP2 // VS) as n:
                for v in range(VS):
                    gather(VS * n + v, v, True)

        def sp_store(sp, img):
            for g in range(CHUNKS):
                s = g % 2
                sp.wait_ge(*y_evac.at(img, 2 * g + 2))
                sp.dma_start(out[img, 8 * g:8 * g + 8].rearrange("(k y) x c -> (y x) k c", k=4), tok[0:TOK, s]).then_inc(y_out[s].sem, 16)
            sp.wait_ge(*y_out[0].at(img, 64))
            sp.sem_inc(passed, 1)
            sp.wait_ge(*y_out[1].at(img, 48))
            sp.sem_inc(passed, 1)

        def pe_gn(pe, img, n):
            pe.wait_ge(*gn_ms.at(img, n + 1))
            pe.matmul(bank[:, 7, 0:4], lhsT=mat[:, 1, :], rhs=ms[:, :, :].rearrange("p q s -> p (q s)"), start=True, stop=True).then_inc(gn_grp.sem, 1)
            pe.wait_ge(*xn_a.at(img, n + 1))
            pe.wait_ge(*xn_v.at(img, n + 1))

        def weight(l, q, kind, a):
            return w0t[:, q, kind, a, :] if l == 0 else w2s[:, q, kind * C + a * P:kind * C + (a + 1) * P]

        def pe_project(pe, img, l):
            R, T, n = RR[l], (TOK0, TOK2)[l], BLK[l]
            pe.wait_ge(*pooled[l].at(img, 1))
            for kind in range(2):
                for a in range(2):
                    o = (2 * kind + a) * 64
                    for q in range(2):
                        m = pe.matmul(bank[:, 6, o:o + R * R], lhsT=weight(l, q, kind, a), rhs=pool_m[l][:, q, :], start=q == 0, stop=q == 1)
            m.then_inc(qkr_mm[l].sem, 1)
            pe.wait_ge(*qkr_evac[l].at(img, 1))
            for a in range(2):
                m = pe.matmul(bank[0:R * R, 7, 0:R * R], lhsT=qkr[l][:, 0, a], rhs=qkr[l][:, 1, a], start=a == 0, stop=a == 1)
            m.then_inc(aff_mm[l].sem, 1)
            if l == 1:
                for a in range(2):
                    m = pe.matmul(bank[0:REG2, 5, 0:REG2], lhsT=wg1s[:, a, :], rhs=qkr[1][:, 0, a], start=a == 0, stop=a == 1)
                m.then_inc(hid_mm.sem, 1)
                pe.wait_ge(*hid_relu.at(img, 1))
                pe.sem_inc(passed, 1)
                pe.matmul(bank[0:REG2, 4, 0:2], lhsT=hid[0:REG2, :], rhs=wg2s[:, 0:2], start=True, stop=False)
                pe.matmul(bank[0:REG2, 4, 0:2], lhsT=bg2s[:, 2:2 + REG2], rhs=bg2s[:, 0:2], start=False, stop=True).then_inc(gate_mm.sem, 1)
                pe.wait_ge(*gwt_done.at(img, 1))
                pe.sem_inc(passed, 1)
            pe.wait_ge(*idx_found[l].at(img, 1))
            pe.sem_inc(passed, 1)
            with pe.Fori(0, R) as i:
                for kind in range(3):
                    for a in range(2):
                        m = 2 * kind + a
                        if m < 3:
                            pe.wait_ge(*qk_evac_a[l].at(img, 3 * i + m - 2))
                        else:
                            pe.wait_ge(*qkv_evac_v[l].at(img, 3 * i + m - 5))
                        for q in range(2):
                            mm = pe.matmul(bank[:, m, 0:n], lhsT=weight(l, q, kind, a),
                                           rhs=region_view(xnp[:, q, 1:H + 1, 1:W + 1], l, i), start=q == 0, stop=q == 1)
                        mm.then_inc(qkv_mm[l].sem, 1)
                pe.wait_ge(*qkv_evac_v[l].at(img, 3 * i + 3))
                for u in range(4):
                    pe.wait_ge(*vtk_evac[l].at(img, 4 * i + u - 1))
                    pe.sem_inc(passed, 1)
                    for w in range(2 * u, min(2 * u + 2, R)):
                        for a in range(2):
                            t = pe.transpose(bank[0:T, 6 + u % 2, (w % 2) * C + a * P:(w % 2) * C + (a + 1) * P],
                                             vrow[:, a, w * T:(w + 1) * T], ident)
                    t.then_inc(v_turned[l].sem, 1)

        def pe_attend0(pe, img):
            def score(r, s, j):
                pe.wait_ge(*s_copied.at(img, r * TILES + j - 3))
                for a in range(2):
                    m = pe.matmul(bank[64 * a:64 * a + 64, j, 0:KEYS0], lhsT=qg[32 * j:32 * j + 32, s, a, :],
                                  rhs=kg[32 * j:32 * j + 32, s, :, a, :], start=True, stop=True)
                m.then_inc(scored.sem, 1)

            def turn(r, j):
                pe.wait_ge(*kept.at(img, r * TILES + j + 1))
                pe.wait_ge(*pt_evac.at(img, r * TILES + j))
                if j == 0:
                    pe.wait_ge(*o_evac.at(img, r - 1))
                for c in range(2):
                    t = pe.transpose(bank[:, 4, c * P:(c + 1) * P], ee[:, j, c * P:(c + 1) * P], ident)
                t.then_inc(p_turned.sem, 1)

            def values(r, s, v, j):
                pe.wait_ge(*pt_evac.at(img, r * TILES + j + 1))
                for a in range(2):
                    for c in range(2):
                        m = pe.matmul(bank[64 * a:64 * a + 64, 5 + s, j * HD:(j + 1) * HD],
                                      lhsT=pt[:, j % 2, c, a * 64:a * 64 + 64],
                                      rhs=vg[:, v, c, a * P + 32 * j:a * P + 32 * j + HD], start=c == 0, stop=c == 1)
                if j == TILES - 1:
                    m.then_inc(pv_done.sem, 1)

            def turn_out(r):
                pe.wait_ge(*o_norm.at(img, r + 1))
                pe.wait_ge(*lepe_evac.at(img, 2 * (r // R0) + 2))
                pe.sem_inc(passed, 1)
                pe.matmul(bank[:, 4, 2 * P:3 * P], lhsT=ident, rhs=att[:, :, bass.ds(r * TOK0, TOK0)], start=True, stop=False)
                pe.matmul(bank[:, 4, 2 * P:3 * P], lhsT=osb[:, :, :].rearrange("p j d -> p (j d)"), rhs=ident, start=False, stop=True).then_inc(o_turned.sem, 1)

            def lepe(row, a, taps, wait=True):
                if taps[0] == 0:
                    pe.wait_ge(*lepe_evac.at(img, 2 * row + a))
                for t in taps:
                    m = pe.matmul(bank[:, 7, 0:BLK[0]], lhsT=diag[:, t, a, :], rhs=region_view(VP0[:, a, t // 3:t // 3 + H, t % 3:t % 3 + W], 0, row),
                                  start=t == 0, stop=t == TAPS - 1)
                if taps[-1] == TAPS - 1:
                    m.then_inc(lepe_mm.sem, 1)

            def region(r, v, nth_next, nth, first=False, second=False, last=False, ahead=None):
                s = v % 2
                if not first:
                    values(r - 1, 1 - s, (v - 1) % VS, TILES - 1)
                if not first and not second:
                    turn_out(r - 2)
                if not last:
                    pe.wait_ge(*kq_in[1 - s].at(img, 80 * nth_next))
                    for j in range(TILES):
                        score(r + 1, 1 - s, j)
                for j in range(TILES):
                    turn(r, j)
                    if j > 0:
                        if j == 1:
                            pe.wait_ge(*v_in[v].at(img, 64 * nth))
                        values(r, s, v, j - 1)
                    if j == 1 and ahead:
                        lepe(*ahead)

            def lap(i, first=False, last=False):
                for n in range(1, 2 * VS + 1):
                    if n in SECOND_HALF:
                        ahead = (i + 1, 1, SECOND_HALF[n])
                    else:
                        ahead = None if last else (i + 2, 0, FIRST_HALF[n])
                    region(2 * VS * i + n, n % VS, VS * i + (n + 1) // 2 + 1, 2 * i + n // VS + 1, second=first and n == 1,
                           last=last and n == 2 * VS, ahead=ahead)

            pe.wait_ge(*diag_made[0].at(img, 1))
            pe.wait_ge(*v_padded[0].at(img, R0))
            pe.wait_ge(*vtk_evac[0].at(img, 4 * R0))
            pe.sem_inc(passed, 1)
            lepe(0, 0, range(TAPS))
            pe.wait_ge(*kq_in[0].at(img, 80))
            for j in range(TILES):
                score(0, 0, j)
            lepe(0, 1, range(TAPS))
            region(0, 0, 1, 1, first=True, ahead=(1, 0, range(TAPS)))
            lap(0, first=True)
            with pe.Fori(1, LAPS - 1) as i:
                lap(i)
            lap(LAPS - 1, last=True)
            values(REG0 - 1, 0, 0, TILES - 1)
            turn_out(REG0 - 2)
            pe.wait_ge(*o_evac.at(img, REG0 - 1))
            turn_out(REG0 - 1)

        def pe_output(pe, img, l):
            R, n = RR[l], BLK[l]
            pe.wait_ge(*(o_evac.at(img, REG0) if l == 0 else out2_evac.at(img, NP2)))
            pe.sem_inc(passed, 1)
            with pe.Fori(0, R) as i:
                for q in range(2):
                    pe.wait_ge(*om_evac[l].at(img, 2 * i + q - 1))
                    for a in range(2):
                        lhs = o0t[:, a, q, :] if l == 0 else p2s[:, a, q::2]
                        m = pe.matmul(bank[:, 2 + q, 0:n], lhsT=lhs, rhs=att[:, a, bass.ds(i * n, n)], start=a == 0, stop=a == 1)
                    m.then_inc(om_mm[l].sem, 1)

        def pe_layer1(pe, img):
            def conv(i, which, q):
                d, done = ((diag, g_mm), (diag_g1, g1_mm))[which]
                for h in range(2):
                    for t in range(TAPS):
                        m = pe.matmul(bank[:, 2 * q + h, 0:E1 // 2], lhsT=d[:, t, q, :],
                                      rhs=xnp[:, q, bass.ds(i * ROWS1 + h * (ROWS1 // 2) + t // 3, ROWS1 // 2), t % 3:t % 3 + W],
                                      start=t == 0, stop=t == TAPS - 1)
                m.then_inc(done.sem, 1)

            def piece(i, n):
                if n == 2:
                    pe.wait_ge(*ax_evac.at(img, 2 * i + 2))
                conv(i, n // 2, n % 2)

            def shift(src, first, second):
                for h in range(2):
                    e = slice(h * (E1 // 2), (h + 1) * (E1 // 2))
                    pe.matmul(bank[:, 4 + h, 0:E1 // 2], lhsT=mat[:, first, :], rhs=src[:, 1, e], start=True, stop=True)
                    m = pe.matmul(bank[:, 6 + h, 0:E1 // 2], lhsT=mat[:, second, :], rhs=src[:, 0, e], start=True, stop=True)
                return m

            def chunk(i, ahead):
                pe.wait_ge(*ay_evac.at(img, 2 * i + 2))
                shift(ay1, 4, 5).then_inc(e_diff.sem, 1)
                pe.wait_ge(*h_set.at(img, i + 1))
                for k in range(STEPS):
                    if k > 0:
                        pe.wait_ge(*h_ready.at(img, STEPS * i + k))
                    shift((hA, hB)[k % 2], 2, 3).then_inc(shifted.sem, 1)
                    if ahead and k < 4:
                        piece(i + 1, k)

            pe.wait_ge(*diag_made[2].at(img, 1))
            for n in range(4):
                piece(0, n)
            with pe.Fori(0, CH1 - 1) as i:
                chunk(i, True)
            chunk(CH1 - 1, False)

        def pe_attend2(pe, img):
            def score(u, s, nth):
                pe.wait_ge(*kq2_in[s].at(img, 144 * nth))
                pe.wait_ge(*logit2.at(img, u - 1))
                for i in range(2):
                    for a in range(2):
                        m = pe.matmul(bank[64 * i:64 * i + 64, s, 0:KEYS2], lhsT=q2g[:, s, i, a, :], rhs=k2g[:, s, i, :, a, :], start=a == 0, stop=a == 1)
                m.then_inc(scored2.sem, 1)

            def pair(u, v, ahead, nth_v):
                s = v % 2
                if ahead is not None:
                    score(u + 1, 1 - s, ahead)
                pe.wait_ge(*out2_evac.at(img, u - 1))
                for a in range(2):
                    for t in range(TAPS):
                        pe.matmul(bank[:, 4 + s, 2 * a * TOK2:2 * (a + 1) * TOK2], lhsT=diag[:, t, a, :],
                                  rhs=v2_view(a, (t // 3 - 1) * 8 + t % 3 - 1)[:, bass.ds(2 * u, 2), 0:S2, 0:S2], start=a == 0 and t == 0, stop=False)
                pe.wait_ge(*weighted2.at(img, u + 1))
                pe.wait_ge(*pt2_evac.at(img, u - 1))
                for c in range(2):
                    t = pe.transpose(bank[0:HK2, 2 + s, c * P:(c + 1) * P], w2p[:, s, c * HK2:(c + 1) * HK2], ident)
                t.then_inc(turned2.sem, 1)
                pe.wait_ge(*v2_in[v].at(img, 128 * nth_v))
                pe.wait_ge(*pt2_evac.at(img, u + 1))
                pe.sem_inc(passed, 1)
                for a in range(2):
                    for i in range(2):
                        for c in range(2):
                            m = pe.matmul(bank[:, 4 + s, (2 * a + i) * TOK2:(2 * a + i + 1) * TOK2], lhsT=v2g[0:HK2, v, i, c, a * P:(a + 1) * P],
                                          rhs=pt2[0:HK2, s, c, 64 * i:64 * i + TOK2], start=False, stop=(a, i, c) == (1, 1, 1))
                m.then_inc(pv2_done.sem, 1)

            pe.wait_ge(*diag_made[3].at(img, 1))
            pe.wait_ge(*v_padded[1].at(img, R2))
            pe.sem_inc(passed, 1)
            score(0, 0, 1)
            with pe.Fori(0, NP2 // VS - 1) as n:
                for v in range(VS):
                    pair(VS * n + v, v, 2 * n + (v + 1) // 2 + 1, n + 1)
            for v in range(VS):
                u = NP2 - VS + v
                pair(u, v, (u + 1) // 2 + 1 if v < VS - 1 else None, NP2 // VS)

        def pe_layer3(pe, img):
            for k in range(3):
                pe.wait_ge(*part_made[k].at(img, 2))
            pe.sem_inc(passed, 1)

            def chunk(g, b):
                pe.wait_ge(*c3_added.at(img, 2 * g - 2))
                n = 0
                for k in (2, 1, 0):
                    for t in range(TAPS):
                        for q in range(2):
                            for o in range(2):
                                m = pe.matmul(bank[:, b + o, 0:CHUNK], lhsT=w3s[:, t, q, o::2],
                                              rhs=parts[k][:, q, bass.ds(8 * g + t // 3, 8), t % 3:t % 3 + W], start=n == 0, stop=n == 6 * TAPS - 1)
                            n += 1
                m.then_inc(c3_mm.sem, 1)

            with pe.Fori(0, CHUNKS // 2) as i:
                chunk(2 * i, 0)
                chunk(2 * i + 1, 2)
            chunk(CHUNKS - 1, 0)

        def pe_store(pe, img):
            pe.wait_ge(*res_done.at(img, LAYERS))
            for g in range(CHUNKS):
                for k2 in range(2):
                    b = 4 + (2 * g + k2) % 4
                    if g >= 2:
                        pe.wait_ge(*y_evac.at(img, 2 * g + k2 - 3))
                    for k in range(2):
                        for q in range(2):
                            o = g * CHUNK + (2 * k2 + k) * TOK
                            t = pe.transpose(bank[0:TOK, b, k * C + q * P:k * C + (q + 1) * P], res[:, q, o:o + TOK], ident)
                    t.then_inc(y_turned.sem, 1)

        def act_gn(act, img, n):
            act.wait_ge(*gn_var.at(img, n + 1))
            act.activation(gm[:, 2:3], gm[:, 1:2], ACT.Sqrt).then_inc(gn_sqrt.sem, 1)
            act.wait_ge(*gn_coef.at(img, n + 1))
            act.activation(xnp[:, 1, 1:H + 1, 1:W + 1], res[:, 1, :].rearrange("p (y x) -> p y x", x=W), ACT.Identity,
                           bias=gm[:, 4:5], scale=gm[:, 3:4]).then_inc(xn_a.sem, 1)

        def act_project(act, img, l):
            R, T, n = RR[l], (TOK0, TOK2)[l], BLK[l]
            bias = (bias0, bias2)[l]
            if l == 1:
                act_gate(act, img)
            with act.Fori(0, R) as i:
                for m in range(3):
                    kind, a = m // 2, m % 2
                    act.wait_ge(*qkv_mm[l].at(img, 6 * i + m + 1))
                    if m == 0:
                        act.wait_ge(*qk_out[l].at(img, 32 * i))
                    act.activation(qks[l][:, kind, :, a, :], bank[:, m, 0:n].rearrange("p (w t) -> p w t", w=R), ACT.Identity,
                                   bias=bias[:, kind, a:a + 1]).then_inc(qk_evac_a[l].sem, 1)
                for u in range(4):
                    act.wait_ge(*v_turned[l].at(img, 4 * i + u + 1))
                    if u == 0:
                        act.wait_ge(*v_out[l].at(img, 16 * i))
                    w1 = min(2 * u + 2, R)
                    act.activation(vtk[0:T, 2 * u:w1], bank[0:T, 6 + u % 2, 0:(w1 - 2 * u) * C].rearrange("p (w c) -> p w c", c=C),
                                   ACT.Copy).then_inc(vtk_evac[l].sem, 1)

        def act_gate(act, img):
            act.wait_ge(*hid_mm.at(img, 1))
            act.activation(hid[0:REG2, :], bank[0:REG2, 5, 0:REG2], ACT.Relu, bias=wg2s[:, 2:3]).then_inc(hid_relu.sem, 1)
            act.wait_ge(*gate_neg.at(img, 1))
            act.activation(sig[0:REG2, 2:4], sig[0:REG2, 2:4], ACT.Exp).then_inc(gate_exp.sem, 1)
            act.wait_ge(*gate_one.at(img, 1))
            act.activation(sig[0:REG2, 2:4], sig[0:REG2, 2:4], ACT.Ln).then_inc(gate_ln.sem, 1)
            act.wait_ge(*dist_done.at(img, 1))
            act.activation(gauss[0:REG2, :], gauss[0:REG2, :], ACT.Exp, scale=-0.5, accum_out=gsum[0:REG2, 0:1]).then_inc(gauss_exp.sem, 1)

        def act_attend2(act, img):
            def exp(u, s):
                act.wait_ge(*logit2.at(img, u + 1))
                act.wait_ge(*weighted2.at(img, u - 1))
                act.activation(e2[:, s], lg2[:, s], ACT.Exp, bias=max2[:, s:s + 1], scale=SCALE2, accum_out=z2[:, s:s + 1]).then_inc(exped2.sem, 1)

            def pair(u, s, last=False):
                if not last:
                    exp(u + 1, 1 - s)
                act.wait_ge(*turned2.at(img, u + 1))
                act.activation(pt2[0:HK2, s], bank[0:HK2, 2 + s, 0:2 * P].rearrange("p (c n) -> p c n", c=2), ACT.Copy).then_inc(pt2_evac.sem, 1)
                act.wait_ge(*pv2_done.at(img, u + 1))
                for a in range(2):
                    m = act.activation(att[:, a, bass.ds(u * HK2, HK2)], bank[:, 4 + s, 2 * a * TOK2:2 * (a + 1) * TOK2], ACT.Identity,
                                       bias=dw2_b[:, a:a + 1])
                m.then_inc(out2_evac.sem, 1)

            act.wait_ge(*v_padded[1].at(img, R2))
            act.wait_ge(*qk_out[1].at(img, 32 * R2))
            act.wait_ge(*v_out[1].at(img, 16 * R2))
            exp(0, 0)
            with act.Fori(0, NP2 // 2 - 1) as n:
                pair(2 * n, 0)
                pair(2 * n + 1, 1)
            pair(NP2 - 2, 0)
            pair(NP2 - 1, 1, last=True)

        def act_layer3(act, img):
            for q in range(2):
                act.activation(parts[0][:, q], xnp[:, q], ACT.Copy).then_inc(part_made[0].sem, 1)
            for q in range(2):
                act.wait_ge(*rest_made.at(img, q + 1))
                act.activation(parts[1][:, q], xnp[:, q], ACT.Copy).then_inc(part_made[1].sem, 1)

        def act_attend0(act, img):
            def copy(r, s, j):
                act.wait_ge(*scored.at(img, r * TILES + j + 1))
                act.activation(sc_sb[:, s, j, :], bank[:, j, 0:KEYS0], ACT.Copy, scale=SCALE0).then_inc(s_copied.sem, 1)

            def exps(r, s, j):
                act.wait_ge(*topped.at(img, r * TILES + j + 1))
                act.wait_ge(*p_turned.at(img, r * TILES + j - 3))
                act.activation(ebest[:, j], best[:, s, j, :], ACT.Exp, bias=nmax[:, s, j:j + 1], accum_out=zsum[:, s, j:j + 1])
                act.activation(er[:, j, :], rem[:, j, :], ACT.Exp, bias=nmax[:, s, j:j + 1])
                act.activation(ee[:, j, :], sc_sb[:, s, j, :], ACT.Exp, bias=nmax[:, s, j:j + 1]).then_inc(exped.sem, 1)

            def evac(r, j):
                act.wait_ge(*p_turned.at(img, r * TILES + j + 1))
                act.activation(pt[:, j % 2], bank[:, 4, 0:2 * P].rearrange("p (c n) -> p c n", c=2), ACT.Copy).then_inc(pt_evac.sem, 1)

            def out_evac(r):
                act.wait_ge(*o_turned.at(img, r + 1))
                act.activation(att[:, :, bass.ds(r * TOK0, TOK0)], bank[:, 4, 2 * P:3 * P].rearrange("p (a t) -> p a t", a=2), ACT.Copy).then_inc(o_evac.sem, 1)

            def evac_lepe(row, a):
                act.wait_ge(*lepe_mm.at(img, 2 * row + a + 1))
                act.activation(att[:, a, bass.ds(row * BLK[0], BLK[0])], bank[:, 7, 0:BLK[0]], ACT.Identity, bias=lepe_b[:, a:a + 1]).then_inc(lepe_evac.sem, 1)

            def region(r, s, first=False, second=False, last=False):
                if not first:
                    evac(r - 1, TILES - 1)
                if not first and not second:
                    out_evac(r - 2)
                for j in range(TILES):
                    if not last and j % 2 == 0:
                        copy(r + 1, 1 - s, j)
                        copy(r + 1, 1 - s, j + 1)
                    exps(r, s, j)
                    if j > 0:
                        evac(r, j - 1)

            act.wait_ge(*v_padded[0].at(img, R0))
            act.wait_ge(*qk_out[0].at(img, 32 * R0))
            act.wait_ge(*v_out[0].at(img, 16 * R0))
            evac_lepe(0, 0)
            for j in range(TILES):
                copy(0, 0, j)
            evac_lepe(0, 1)
            region(0, 0, first=True)
            evac_lepe(1, 0)

            def lap(i, first=False, last=False):
                for n in range(1, 2 * VS + 1):
                    region(2 * VS * i + n, n % 2, second=first and n == 1, last=last and n == 2 * VS)
                    if n == max(SECOND_HALF):
                        evac_lepe(i + 1, 1)
                    if n == max(FIRST_HALF) and not last:
                        evac_lepe(i + 2, 0)
            lap(0, first=True)
            with act.Fori(1, LAPS - 1) as i:
                lap(i)
            lap(LAPS - 1, last=True)
            evac(REG0 - 1, TILES - 1)
            out_evac(REG0 - 2)
            out_evac(REG0 - 1)

        def act_output(act, img, l):
            R, n = RR[l], BLK[l]
            b = (out0_b, proj_b)[l]
            with act.Fori(0, R) as i:
                for q in range(2):
                    act.wait_ge(*om_mm[l].at(img, 2 * i + q + 1))
                    act.wait_ge(*om_added[l].at(img, 2 * i + q - 1))
                    act.activation(otmp[:, 0, q, 0:n], bank[:, 2 + q, 0:n], ACT.Identity, bias=b[:, q:q + 1]).then_inc(om_evac[l].sem, 1)

        def act_layer1(act, img):
            for q in range(2):
                m = act.activation(VP0[:, q, 1:H + 1, 1:W + 1], res[:, q, :].rearrange("p (y x) -> p y x", x=W), ACT.Identity,
                                   bias=gm[:, 4:5], scale=gm[:, 3:4])
            m.then_inc(mirror_in.sem, 1)

            def evac_conv(i, which):
                mm, out_, done = ((g_mm, ax1, ax_evac), (g1_mm, ay1, ay_evac))[which]
                for q in range(2):
                    act.wait_ge(*mm.at(img, 2 * i + q + 1))
                    act.activation(out_[:, q].rearrange("p (h n) -> p h n", h=2), bank[:, 2 * q:2 * q + 2, 0:E1 // 2], ACT.Relu,
                                   bias=bnc[:, which, q, 1:2], scale=bnc[:, which, q, 0:1]).then_inc(done.sem, 1)

            def chunk(i, ahead):
                act.wait_ge(*y1_added.at(img, i))
                evac_conv(i, 1)
                for n, (src, dst) in enumerate(((hA, cpx), (hB, cpy))):
                    act.wait_ge(*sobel_done.at(img, 2 * i + n + 1))
                    act.activation(dst, src, ACT.Square, scale=0.5).then_inc(squared.sem, 1)
                act.wait_ge(*coef_done.at(img, i + 1))
                rows = xnp[:, :, bass.ds(i * ROWS1 + 1, ROWS1), 1:W + 1]
                act.activation(hA.rearrange("p q (y x) -> p q y x", x=W), rows, ACT.Copy)
                act.activation(hB.rearrange("p q (y x) -> p q y x", x=W), rows, ACT.Copy).then_inc(h_set.sem, 1)
                if ahead:
                    evac_conv(i + 1, 0)
                act.wait_ge(*h_ready.at(img, STEPS * i + STEPS))
                for q in range(2):
                    m = act.activation(acc[:, q], hB[:, q], ACT.Relu, bias=bnc[:, 2, q, 1:2], scale=bnc[:, 2, q, 0:1])
                m.then_inc(y1_ready.sem, 1)

            evac_conv(0, 0)
            with act.Fori(0, CH1 - 1) as i:
                chunk(i, True)
            chunk(CH1 - 1, False)

        def act_store(act, img):
            for g in range(CHUNKS):
                for k2 in range(2):
                    act.wait_ge(*y_turned.at(img, 2 * g + k2 + 1))
                    if g >= 2 and k2 == 0:
                        act.wait_ge(*y_out[g % 2].at(img, 16 * (g // 2)))
                    act.activation(tok[0:TOK, g % 2, 2 * k2:2 * k2 + 2].rearrange("p k (c q) -> p k q c", q=2),
                                   bank[0:TOK, 4 + (2 * g + k2) % 4, :].rearrange("p (k q c) -> p k q c", k=2, q=2), ACT.Copy).then_inc(y_evac.sem, 1)

        def dve_gn(dve, img, n, eps):
            for q in range(2):
                for g in range(CHUNKS):
                    dve.bn_stats(stats[:, q, g, :], res[:, q, g * CHUNK:(g + 1) * CHUNK])
            dve.drain()
            for q in range(2):
                dve.bn_aggr(mv[:, q, :], stats[:, q].rearrange("p g s -> p (g s)"))
            dve.drain()
            dve.tensor_copy(ms[:, :, 0], mv[:, :, 0])
            dve.tensor_tensor(ms[:, :, 1], mv[:, :, 0], mv[:, :, 0], ALU.mult)
            dve.drain()
            dve.tensor_tensor(ms[:, :, 1], ms[:, :, 1], mv[:, :, 1], ALU.add)
            dve.drain().then_inc(gn_ms.sem, 1)
            dve.wait_ge(*gn_grp.at(img, n + 1))
            dve.tensor_copy(grp[:, :, :], bank[:, 7, 0:4].rearrange("p (q s) -> p q s", q=2))
            dve.drain()
            dve.tensor_tensor(gm[:, 0:2], grp[:, 0, :], grp[:, 1, :], ALU.add)
            dve.drain()
            dve.tensor_tensor(gm[:, 5:6], gm[:, 0:1], gm[:, 0:1], ALU.mult)
            dve.drain()
            dve.tensor_tensor(gm[:, 1:2], gm[:, 1:2], gm[:, 5:6], ALU.subtract)
            dve.drain()
            dve.tensor_scalar(gm[:, 1:2], gm[:, 1:2], 0.0, eps, ALU.max, ALU.add)
            dve.drain().then_inc(gn_var.sem, 1)
            dve.wait_ge(*gn_sqrt.at(img, n + 1))
            dve.reciprocal(gm[:, 3:4], gm[:, 2:3])
            dve.drain()
            dve.tensor_scalar(gm[:, 4:5], gm[:, 0:1], gm[:, 3:4], -1.0, ALU.mult, ALU.mult)
            dve.drain().then_inc(gn_coef.sem, 1)
            dve.tensor_scalar(xnp[:, 0, 1:H + 1, 1:W + 1], res[:, 0, :].rearrange("p (y x) -> p y x", x=W),
                              gm[:, 3:4], gm[:, 4:5], ALU.mult, ALU.add).then_inc(xn_v.sem, 1)
            dve.wait_ge(*xn_v.at(img, n + 1))
            dve.wait_ge(*xn_a.at(img, n + 1))
            dve.sem_inc(passed, 1)

        def dve_diag(dve, k, w, dst=None):
            d = diag if dst is None else dst
            for t in range(TAPS):
                for a in range(2):
                    dve.tensor_scalar(d[:, t, a, :], ident, w[:, a, t:t + 1], None, ALU.mult)
            dve.drain().then_inc(diag_made[k].sem, 1)

        def dve_project(dve, img, l):
            R, T, n, s = RR[l], (TOK0, TOK2)[l], BLK[l], SS[l]
            for q in range(2):
                dve.tensor_reduce(pool_a[l][:, q], xnp[:, q, 1:H + 1, 1:W + 1].rearrange("p y (w x) -> p y w x", x=s), AX.X, ALU.add)
            dve.drain()
            pa, pm = pool_a[l], pool_m[l]
            for q in range(2):
                dve.tensor_reduce(pm[:, q].rearrange("p (v w) -> p v w", v=R), pa[:, q].rearrange("p (v y) w -> p v w y", y=s), AX.X, ALU.add)
            dve.drain()
            dve.tensor_scalar(pm, pm, 1.0 / (s * s), None, ALU.mult)
            dve.drain().then_inc(pooled[l].sem, 1)
            dve.wait_ge(*qkr_mm[l].at(img, 1))
            bias = (bias0, bias2)[l]
            for kind in range(2):
                for a in range(2):
                    o = (2 * kind + a) * 64
                    dve.tensor_scalar(qkr[l][:, kind, a], bank[:, 6, o:o + R * R], bias[:, kind, a:a + 1], None, ALU.add)
            dve.drain().then_inc(qkr_evac[l].sem, 1)
            dve.wait_ge(*aff_mm[l].at(img, 1))
            dve.tensor_scalar(aff[0:R * R, 0:R * R], bank[0:R * R, 7, 0:R * R], (1.0, SCALE2)[l], None, ALU.mult)
            dve.drain()
            dve.max(v8[0:R * R], aff[0:R * R, 0:R * R])
            dve.drain()
            dve.max_index(i8[0:R * R], v8[0:R * R], aff[0:R * R, 0:R * R])
            dve.drain().then_inc(idx_found[l].sem, 1)
            if l == 1:
                dve_gate(dve, img)
            with dve.Fori(0, R) as i:
                for m in range(3, 6):
                    kind, a = m // 2, m % 2
                    dve.wait_ge(*qkv_mm[l].at(img, 6 * i + m + 1))
                    if kind == 1:
                        dve.wait_ge(*qk_out[l].at(img, 32 * i))
                        dst = qks[l][:, 1, :, a, :]
                    else:
                        if m == 4:
                            dve.wait_ge(*v_padded[l].at(img, i))
                            dve.wait_ge(*v_turned[l].at(img, 4 * i))
                        dst = vrow[:, a, 0:n].rearrange("p (w t) -> p w t", w=R)
                    dve.tensor_scalar(dst, bank[:, m, 0:n].rearrange("p (w t) -> p w t", w=R), bias[:, kind, a:a + 1], None, ALU.add).then_inc(qkv_evac_v[l].sem, 1)

        def dve_gate(dve, img):
            g = sig[0:REG2]
            dve.wait_ge(*gate_mm.at(img, 1))
            dve.tensor_copy(g[:, 0:2], bank[0:REG2, 4, 0:2])
            dve.drain()
            dve.scalar_tensor_tensor(g[:, 2:4], g[:, 0:2], -1.0, g[:, 0:2], ALU.mult, ALU.min)
            dve.drain().then_inc(gate_neg.sem, 1)
            dve.wait_ge(*gate_exp.at(img, 1))
            dve.tensor_scalar(g[:, 2:4], g[:, 2:4], 1.0, None, ALU.add)
            dve.drain().then_inc(gate_one.sem, 1)
            dve.wait_ge(*gate_ln.at(img, 1))
            dve.scalar_tensor_tensor(g[:, 0:2], g[:, 0:2], 0.0, g[:, 2:4], ALU.max, ALU.add)
            dve.drain()
            dve.tensor_scalar(g[:, 0:2], g[:, 0:2], 0.5, None, ALU.add)
            dve.drain()
            dve.tensor_tensor(g[:, 2:4], g[:, 0:2], g[:, 0:2], ALU.mult)
            dve.drain()
            dve.reciprocal(g[:, 4:6], g[:, 2:4])
            dve.drain()
            dve.tensor_scalar(gauss[0:REG2, :], posd_s[:, 0], g[:, 4:5], None, ALU.mult)
            dve.drain()
            dve.scalar_tensor_tensor(gauss[0:REG2, :], posd_s[:, 1], g[:, 5:6], gauss[0:REG2, :], ALU.mult, ALU.add)
            dve.tensor_copy(idx_f[0:REG2, 0:TOPK], i8[0:REG2, 0:TOPK])
            dve.drain().then_inc(dist_done.sem, 1)
            dve.wait_ge(*gauss_exp.at(img, 1))
            dve.tensor_scalar(gsum[0:REG2, 0:1], gsum[0:REG2, 0:1], 1e-6, None, ALU.add)
            dve.drain()
            dve.reciprocal(gsum[0:REG2, 1:2], gsum[0:REG2, 0:1])
            dve.drain()
            dve.tensor_scalar(gauss[0:REG2, :], gauss[0:REG2, :], gsum[0:REG2, 1:2], None, ALU.mult)
            dve.drain()
            for t in range(TOPK):
                dve.scalar_tensor_tensor(hid[0:REG2, :], posd_s[:, 2], idx_f[0:REG2, t:t + 1], gauss[0:REG2, :], ALU.is_equal, ALU.mult,
                                         accum_out=gwt[0:REG2, t:t + 1])
                dve.drain()
            dve.memset(q2g_flat, 0.0)
            dve.drain().then_inc(q2_zeroed.sem, 1)
            dve.drain().then_inc(gwt_done.sem, 1)

        def dve_attend2(dve, img):
            def gw(u):
                return gws[:, bass.ds(u, 1), :].rearrange("p u t -> p (u t)").unsqueeze(2).to_broadcast([P, TOPK, TOK2])

            v3 = lambda a: a.rearrange("p (t n) -> p t n", t=TOPK)

            def logits(u, s):
                dve.wait_ge(*scored2.at(img, u + 1))
                dve.wait_ge(*exped2.at(img, u - 1))
                dve.tensor_tensor(v3(lg2[:, s]), v3(bank[:, s, 0:KEYS2]), gw(u), ALU.mult)
                dve.drain()
                dve.reduce_max(max2[:, s:s + 1], lg2[:, s], AX.X)
                dve.drain()
                dve.tensor_scalar(max2[:, s:s + 1], max2[:, s:s + 1], -SCALE2, None, ALU.mult).then_inc(logit2.sem, 1)

            def weights(u, s):
                dve.wait_ge(*exped2.at(img, u + 1))
                dve.reciprocal(rz2[:, s:s + 1], z2[:, s:s + 1])
                dve.drain()
                dve.wait_ge(*turned2.at(img, u - 1))
                dve.scalar_tensor_tensor(v3(w2p[:, s]), v3(e2[:, s]), rz2[:, s:s + 1], gw(u), ALU.mult, ALU.mult).then_inc(weighted2.sem, 1)

            dve.wait_ge(*v_padded[1].at(img, R2))
            dve.wait_ge(*qk_out[1].at(img, 32 * R2))
            dve.wait_ge(*v_out[1].at(img, 16 * R2))
            dve.wait_ge(*gw_in.at(img, 32))
            logits(0, 0)
            with dve.Fori(0, NP2 // 2 - 1) as n:
                logits(2 * n + 1, 1)
                weights(2 * n, 0)
                logits(2 * n + 2, 0)
                weights(2 * n + 1, 1)
            logits(NP2 - 1, 1)
            weights(NP2 - 2, 0)
            weights(NP2 - 1, 1)

        def dve_layer3(dve, img):
            for q in range(2):
                dve.wait_ge(*part_made[0].at(img, q + 1))
                dve.tensor_tensor(xnp[:, q], xnp[:, q], parts[0][:, q], ALU.subtract)
                dve.drain().then_inc(rest_made.sem, 1)
            for q in range(2):
                dve.wait_ge(*part_made[1].at(img, q + 1))
                dve.tensor_tensor(parts[2][:, q], xnp[:, q], parts[1][:, q], ALU.subtract)
                dve.drain().then_inc(part_made[2].sem, 1)

            def chunk(g, b):
                dve.wait_ge(*c3_mm.at(img, g + 1))
                for o in range(2):
                    r = res[:, o, bass.ds(g * CHUNK, CHUNK)]
                    dve.tensor_tensor(r, r, bank[:, b + o, 0:CHUNK], ALU.add).then_inc(c3_added.sem, 1)

            with dve.Fori(0, CHUNKS // 2) as i:
                chunk(2 * i, 0)
                chunk(2 * i + 1, 2)
            chunk(CHUNKS - 1, 0)
            dve.drain().then_inc(res_done.sem, 1)

        def dve_attend0(dve, img):
            def pair(r, s, h):
                j0 = 2 * h
                dve.wait_ge(*s_copied.at(img, r * TILES + j0 + 2))
                dve.wait_ge(*exped.at(img, (r - 1) * TILES + j0 + 2))
                dve.sem_inc(passed, 1)
                n = 0
                for k in range(4):
                    for j in (j0, j0 + 1):
                        src = sc_sb[:, s, j] if k == 0 else rem[:, j]
                        if k > 0:
                            dve.wait_ge(topk_step, n - 1)
                        dve.max(best[:, s, j, 8 * k:8 * k + 8], src).then_inc(topk_step, 1)
                        n += 1
                    for j in (j0, j0 + 1):
                        src = sc_sb[:, s, j] if k == 0 else rem[:, j]
                        dve.wait_ge(topk_step, n - 1)
                        ins = dve.match_replace(rem[:, j], best[:, s, j, 8 * k:8 * k + 8], src, REMOVED)
                        ins.then_inc(topk_step, 1)
                        n += 1
                dve.tensor_scalar(nmax[:, s, j0:j0 + 2], best[:, s, j0:j0 + 2, 0], -1.0, None, ALU.mult).then_inc(topped.sem, 2)
                dve.wait_ge(topk_step, n)
                dve.sem_clear(topk_step)

            def norm(r, s):
                dve.wait_ge(*exped.at(img, (r + 1) * TILES))
                dve.reciprocal(rz[:, s], zsum[:, s])
                dve.drain()
                dve.wait_ge(*pv_done.at(img, r + 1))
                dve.wait_ge(*o_turned.at(img, r))
                dve.tensor_tensor(osb[:, :, :], bank[:, 5 + s, 0:P].rearrange("p (j d) -> p j d", j=TILES),
                                  rz[:, s].unsqueeze(2).to_broadcast([P, TILES, HD]), ALU.mult).then_inc(o_norm.sem, 1)

            def region(r, s, first=False):
                pair(r, s, 0)
                pair(r, s, 1)
                if not first:
                    norm(r - 1, 1 - s)

            dve.wait_ge(*v_padded[0].at(img, R0))
            dve.wait_ge(*qk_out[0].at(img, 32 * R0))
            dve.wait_ge(*v_out[0].at(img, 16 * R0))
            region(0, 0, first=True)
            with dve.Fori(0, 24) as i:
                region(2 * i + 1, 1)
                region(2 * i + 2, 0)
            norm(48, 0)

        def tt(eng, out_, a, b, op):
            eng.tensor_tensor(out_, a, b, op)
            eng.drain()

        def dve_bn(dve):
            dve.tensor_scalar(bns[:, :, 3:12:4], bns[:, :, 3:12:4], BN_EPS, None, ALU.add)
            dve.drain().then_inc(bn_var.sem, 1)
            dve.wait_ge(bn_sqrt.sem, 1)
            dve.reciprocal(bns[:, :, 3:12:4], bns[:, :, 3:12:4])
            dve.drain()
            for n in range(3):
                k = 4 * n
                tt(dve, bnc[:, n, :, 0:1], bns[:, :, k:k + 1], bns[:, :, k + 3:k + 4], ALU.mult)
                tt(dve, bnc[:, n, :, 1:2], bns[:, :, k + 2:k + 3], bnc[:, n, :, 0:1], ALU.mult)
                tt(dve, bnc[:, n, :, 1:2], bns[:, :, k + 1:k + 2], bnc[:, n, :, 1:2], ALU.subtract)
                if n < 2:
                    dve.tensor_scalar(bnc[:, n], bnc[:, n], DT, None, ALU.mult)
                    dve.drain()
            dve.drain().then_inc(bn_ready.sem, 1)

        def dve_layer1(dve, img):
            def rolled(op, out_, coef, h, by):
                o, c, v = (a.rearrange("p q (y x) -> p (q y) x", x=W) for a in (out_, coef, h))
                if by > 0:
                    dve.tensor_tensor(o[:, :, 1:W], c[:, :, 1:W], v[:, :, 0:W - 1], op)
                    dve.tensor_tensor(o[:, :, 0:1], c[:, :, 0:1], v[:, :, W - 1:W], op)
                else:
                    dve.tensor_tensor(o[:, :, 0:W - 1], c[:, :, 0:W - 1], v[:, :, 1:W], op)
                    dve.tensor_tensor(o[:, :, W - 1:W], c[:, :, W - 1:W], v[:, :, 0:1], op)
                dve.drain()

            def banks(b):
                return bank[:, b:b + 2, 0:E1 // 2]

            def halves(a):
                return a.rearrange("p (h n) -> p h n", h=2)

            def sobel(i, out_, tmp, across):
                def d(k):
                    if across:
                        return [VP0[:, :, bass.ds(i * ROWS1 + k, ROWS1), x:x + W] for x in (2, 0)]
                    return [VP0[:, :, bass.ds(i * ROWS1 + y, ROWS1), k:k + W] for y in (2, 0)]
                v4 = lambda a: a.rearrange("p q (y x) -> p q y x", x=W)
                tt(dve, v4(out_), *d(1), ALU.subtract)
                tt(dve, v4(tmp), *d(0), ALU.subtract)
                dve.scalar_tensor_tensor(out_, out_, 2.0, tmp, ALU.mult, ALU.add)
                dve.drain()
                tt(dve, v4(tmp), *d(2), ALU.subtract)
                tt(dve, out_, out_, tmp, ALU.add)
                dve.drain().then_inc(sobel_done.sem, 1)

            def stt(out_, a, scalar, b, op0, op1):
                dve.scalar_tensor_tensor(out_, a, scalar, b, op0, op1)
                dve.drain()

            def coefficients(i):
                sobel(i, hA, acc, True)
                sobel(i, hB, prod, False)
                dve.wait_ge(*squared.at(img, 2 * i + 2))
                tt(dve, cmx, cpx, cpy, ALU.mult)
                tt(dve, cmy, cpx, cpy, ALU.add)
                stt(acc, cmy, 1.0 + 2 * DT, cmx, ALU.mult, ALU.add)
                dve.tensor_scalar(acc, acc, 1.0 + 4 * DT, None, ALU.add)
                dve.drain()
                dve.reciprocal(cE, acc)
                stt(cmx, cmx, 1.0, cmy, ALU.add, ALU.add)
                tt(dve, hB, cmx, cE, ALU.mult)
                dve.tensor_scalar(cE, cE, 2 * DT, None, ALU.mult)
                dve.tensor_scalar(c0, hB, 2.0, -1.0, ALU.mult, ALU.add)
                dve.drain()
                stt(cpx, cpx, 1.0, cE, ALU.add, ALU.mult)
                stt(cpy, cpy, 1.0, cE, ALU.add, ALU.mult)
                dve.wait_ge(*ax_evac.at(img, 2 * i + 2))
                tt(dve, acc, ax1, hB, ALU.mult)
                tt(dve, cmx, cpx, acc, ALU.subtract)
                tt(dve, cpx, cpx, acc, ALU.add)
                dve.wait_ge(*ay_evac.at(img, 2 * i + 2))
                tt(dve, acc, ay1, hB, ALU.mult)
                tt(dve, cmy, cpy, acc, ALU.subtract)
                tt(dve, cpy, cpy, acc, ALU.add)
                o, v = (a.rearrange("p q (y x) -> p (q y) x", x=W) for a in (hA, ax1))
                dve.tensor_tensor(o[:, :, 1:W - 1], v[:, :, 0:W - 2], v[:, :, 2:W], ALU.subtract)
                dve.tensor_tensor(o[:, :, 0:1], v[:, :, W - 1:W], v[:, :, 1:2], ALU.subtract)
                dve.tensor_tensor(o[:, :, W - 1:W], v[:, :, W - 2:W - 1], v[:, :, 0:1], ALU.subtract)
                dve.drain()
                dve.wait_ge(*e_diff.at(img, i + 1))
                for q in range(2):
                    dve.tensor_tensor(halves(hA[:, q]), halves(hA[:, q]), banks(4 + 2 * q), ALU.add)
                dve.drain()
                stt(cE, hA, -1.0, hB, ALU.mult, ALU.mult)
                for q in range(2):
                    dve.scalar_tensor_tensor(cF[:, q].rearrange("p (y x) -> p y x", x=W), hB[:, q].rearrange("p (y x) -> p y x", x=W), 2 * DT,
                                             xnp[:, q, bass.ds(i * ROWS1 + 1, ROWS1), 1:W + 1], ALU.mult, ALU.mult)
                dve.drain().then_inc(coef_done.sem, 1)

            with dve.Fori(0, CH1) as i:
                if True:
                    coefficients(i)
                dve.wait_ge(*h_set.at(img, i + 1))
                for k in range(STEPS):
                    h, hn = (hA, hB) if k % 2 == 0 else (hB, hA)
                    rolled(ALU.mult, acc, cmx, h, 1)
                    rolled(ALU.mult, prod, cpx, h, -1)
                    tt(dve, acc, acc, prod, ALU.add)
                    dve.wait_ge(*shifted.at(img, STEPS * i + k + 1))
                    dve.tensor_tensor(halves(prod[:, 0]), halves(cmy[:, 0]), banks(4), ALU.mult)
                    dve.tensor_tensor(prod[:, 1], cmy[:, 1], h[:, 0], ALU.mult)
                    dve.drain()
                    tt(dve, acc, acc, prod, ALU.add)
                    dve.tensor_tensor(prod[:, 0], cpy[:, 0], h[:, 1], ALU.mult)
                    dve.tensor_tensor(halves(prod[:, 1]), halves(cpy[:, 1]), banks(6), ALU.mult)
                    dve.drain()
                    tt(dve, acc, acc, prod, ALU.add)
                    dve.wait_ge(*own_part.at(img, STEPS * i + k + 1))
                    tt(dve, hn, hn, acc, ALU.add)
                    dve.drain().then_inc(h_ready.sem, 1)
                dve.wait_ge(*y1_ready.at(img, i + 1))
                r = res[:, :, bass.ds(i * E1, E1)]
                dve.tensor_tensor(r, r, acc, ALU.add).then_inc(y1_added.sem, 1)
            dve.drain().then_inc(res_done.sem, 1)

        def pool_project(pool, img, l):
            R, n = RR[l], BLK[l]
            with pool.Fori(0, R) as i:
                pool.wait_ge(*qkv_evac_v[l].at(img, 3 * i + 3))
                for a in range(2):
                    if l == 0:
                        dst = region_view(VP0[:, a, 1:H + 1, 1:W + 1], 0, i)
                        src = vrow[:, a, 0:n].rearrange("p (w y x) -> p w y x", w=R, y=S0)
                    else:
                        dst = v2_view(a, 0)[:, bass.ds(i * R2, R2), 0:S2, 0:S2]
                        src = vrow[:, a, 0:n].rearrange("p (w y x) -> p w y x", w=R, y=S2)
                    pool.tensor_copy(dst, src)
                pool.drain().then_inc(v_padded[l].sem, 1)

        def pool_attend0(pool, img):
            with pool.Fori(0, REG0) as r:
                for j in range(TILES):
                    pool.wait_ge(*exped.at(img, r * TILES + j + 1))
                    pool.tensor_tensor(ee[:, j, :], ee[:, j, :], er[:, j, :], ALU.subtract).then_inc(kept.sem, 1)

        def pool_layer1(pool, img):
            pool.wait_ge(*mirror_in.at(img, 1))
            pool.sem_inc(passed, 1)
            for to, of in ((0, 2), (H + 1, H - 1)):
                pool.tensor_copy(VP0[:, :, to, 1:W + 1], VP0[:, :, of, 1:W + 1])
            pool.drain()
            for to, of in ((0, 2), (W + 1, W - 1)):
                pool.tensor_copy(VP0[:, :, :, to], VP0[:, :, :, of])
            pool.drain().then_inc(mirrored.sem, 1)
            with pool.Fori(0, CH1) as i:
                pool.wait_ge(*h_set.at(img, i + 1))
                for k in range(STEPS):
                    h, hn = (hA, hB) if k % 2 == 0 else (hB, hA)
                    if k > 0:
                        pool.wait_ge(*h_ready.at(img, STEPS * i + k))
                    pool.tensor_tensor(ay1, cE, h, ALU.mult)
                    if k > 0:
                        pool.wait_ge(*shifted.at(img, STEPS * i + k))
                    tt(pool, hn, hn, c0, ALU.mult)
                    tt(pool, hn, hn, cF, ALU.add)
                    pool.tensor_tensor(hn, hn, ay1, ALU.add)
                    pool.drain().then_inc(own_part.sem, 1)

        def pool_output(pool, img, l):
            R, n, s = RR[l], BLK[l], SS[l]
            with pool.Fori(0, R) as i:
                for q in range(2):
                    pool.wait_ge(*om_evac[l].at(img, 2 * i + q + 1))
                    v = region_view(res[:, q, :].rearrange("p (y x) -> p y x", x=W), l, i)
                    pool.tensor_tensor(v, v, otmp[:, 0, q, 0:n].rearrange("p (w y x) -> p w y x", w=R, y=s), ALU.add).then_inc(om_added[l].sem, 1)
            pool.drain().then_inc(res_done.sem, 1)

        @block.sync
        def _(sp):
            def const(dst, src):
                sp.dma_start(dst, src).then_inc(const_in.sem, 16)
            const(mat[:, :, :], mats)
            for kind in range(3):
                for a in range(2):
                    for j in range(4):
                        o = kind * C + 64 * j + 32 * a
                        sp.dma_start(w0raw[32 * j:32 * j + 32, 2 * kind + a, :], w0_qkv[o:o + 32, :]).then_inc(wraw_in.sem, 16)
                        sp.dma_start(bias0[32 * j:32 * j + 32, kind, a:a + 1], b0_qkv[o:o + 32].rearrange("(p o) -> p o", o=1)).then_inc(wraw_in.sem, 16)
            for q in range(2):
                for a in range(2):
                    sp.dma_start(o0raw[:, q, a * P:(a + 1) * P].rearrange("p (j d) -> p j d", j=4),
                                 w0_out.rearrange("(p q) (j a d) -> p q a j d", q=2, j=4, a=2)[:, q, a]).then_inc(wraw_in.sem, 16)
            for a in range(2):
                for j in range(4):
                    o = 64 * j + 32 * a
                    sp.dma_start(lepe_w[32 * j:32 * j + 32, a, :], w0_lepe[o:o + 32].rearrange("c i y x -> c (i y x)")).then_inc(wraw_in.sem, 16)
                    sp.dma_start(small[32 * j:32 * j + 32, a:a + 1], b0_lepe[o:o + 32].rearrange("(p o) -> p o", o=1)).then_inc(wraw_in.sem, 16)
            sp.dma_start(small[:, 2:4], b0_out.rearrange("(p q) -> p q", q=2)).then_inc(wraw_in.sem, 16)

            sp.dma_start(w2s[:, :, :], w2_qkv.rearrange("(p q) o -> p q o", q=2)).then_inc(const_in.sem, 16)
            sp.dma_start(p2s[:, :, :], w2_proj.rearrange("(a p) o -> p a o", a=2)).then_inc(const_in.sem, 16)
            sp.dma_start(wg1s[:, :, :], w2_g1.rearrange("(a p) h -> p a h", a=2)).then_inc(const_in.sem, 16)
            sp.dma_start(wg2s[:, 0:2], w2_g2).then_inc(const_in.sem, 16)
            sp.dma_start(wg2s[:, 2:3], b2_g1.rearrange("(p o) -> p o", o=1)).then_inc(const_in.sem, 16)
            sp.dma_start(bg2s[:, 0:2], b2_g2.rearrange("(o g) -> o g", o=1)).then_inc(const_in.sem, 16)
            sp.dma_start(posd_s[:, :, :], posd).then_inc(const_in.sem, 16)
            sp.dma_start(small[:, 6:8], b2_proj.rearrange("(p q) -> p q", q=2)).then_inc(const_in.sem, 16)
            sp.dma_start(w3raw.rearrange("p (t q f) -> p t q f", t=TAPS, q=2), w3.rearrange("y x (p q) f -> p (y x) q f", q=2)).then_inc(const_in.sem, 16)
            with nc.allow_non_contiguous_dma("parameters of single channels"):
                for a in range(2):
                    for kind in range(3):
                        sp.dma_start(bias2[:, kind, a:a + 1], b2_qkv.rearrange("(k a p o) -> k a p o", k=3, a=2, o=1)[kind, a]).then_inc(const_in.sem, 16)
                    sp.dma_start(dw2_w[:, a, :], w2_dw.rearrange("y x o (a p) -> a p (o y x)", a=2)[a]).then_inc(const_in.sem, 16)
                    sp.dma_start(small[:, 4 + a:5 + a], b2_dw.rearrange("(a p o) -> a p o", a=2, o=1)[a]).then_inc(const_in.sem, 16)
                for w, src in ((g_w, w1_g), (g1_w, w1_g1)):
                    for q in range(2):
                        sp.dma_start(w[:, q, :], src.rearrange("y x (p q) -> q p (y x)", q=2)[q]).then_inc(const_in.sem, 16)
                for q in range(2):
                    sp.dma_start(bns[:, q, :], bn1.rearrange("n (p q) -> q p n", q=2)[q]).then_inc(const_in.sem, 16)
            with sp.Fori(0, B) as img:
                sp.wait_ge(zeroed.sem, 1)
                sp.wait_ge(w3_made.sem, 1)
                for g in range(CHUNKS):
                    s = g % 2
                    if g >= 2:
                        sp.wait_ge(*x_turned.at(img, 2 * (g - 1)))
                    sp.dma_start(tok[0:TOK, s], x[img, 8 * g:8 * g + 8].rearrange("(k y) x c -> (y x) k c", k=4)).then_inc(x_in[s].sem, 16)
                sp_project(sp, img, 0)
                sp_gather0(sp, img)
                if LAYERS > 2:
                    sp.sem_inc(passed, 1)
                    sp_project(sp, img, 1)
                    sp_gather2(sp, img)
                sp_store(sp, img)

        @block.tensor
        def _(pe):
            pe.wait_ge(const_in.sem, CONSTS)
            pe.wait_ge(wraw_in.sem, 16 * (48 + 4 + 16 + 1))
            for m in range(6):
                for q in range(2):
                    t = pe.transpose(bank[:, m, q * P:(q + 1) * P], w0raw[:, m, q::2], ident)
            for q in range(2):
                for a in range(2):
                    t = pe.transpose(bank[:, 6 + q, a * P:(a + 1) * P], o0raw[:, q, a * P:(a + 1) * P], ident)
            t.then_inc(w_turned.sem, 1)
            pe.wait_ge(w_copied.sem, 1)

            with pe.Fori(0, B) as img:
                pe.wait_ge(zeroed.sem, 1)
                for g in range(CHUNKS):
                    pe.wait_ge(*x_in[g % 2].at(img, 16 * (g // 2 + 1)))
                    for q in range(2):
                        b = (2 * g + q) % 8
                        if g >= 4:
                            pe.wait_ge(*(x_evac_a, x_evac_v)[q].at(img, g - 3))
                        for k in range(4):
                            t = pe.transpose(bank[:, b, k * TOK:(k + 1) * TOK], tok[0:TOK, g % 2, k, q::2], mat[0:TOK, 0, 0:TOK])
                        t.then_inc(x_turned.sem, 1)
                pe_gn(pe, img, 0)
                pe_project(pe, img, 0)
                pe_attend0(pe, img)
                pe_output(pe, img, 0)
                if LAYERS > 1:
                    pe_gn(pe, img, 1)
                    pe_layer1(pe, img)
                if LAYERS > 2:
                    pe_gn(pe, img, 2)
                    pe_project(pe, img, 1)
                    pe_attend2(pe, img)
                    pe_output(pe, img, 1)
                if LAYERS > 3:
                    pe_gn(pe, img, 3)
                    pe_layer3(pe, img)
                pe_store(pe, img)

        @block.scalar
        def _(act):
            act.wait_ge(bn_var.sem, 1)
            act.activation(bns[:, :, 3:12:4], bns[:, :, 3:12:4], ACT.Sqrt).then_inc(bn_sqrt.sem, 1)
            act.wait_ge(bn_ready.sem, 1)
            act.wait_ge(w3_half.sem, 1)
            act.activation(w3s[:, :, :, :].rearrange("p t q f -> p (t q f)"), w3raw, ACT.Sign).then_inc(w3_made.sem, 1)
            with act.Fori(0, B) as img:
                for g in range(CHUNKS):
                    act.wait_ge(*x_turned.at(img, 2 * g + 1))
                    act.activation(res[:, 0, g * CHUNK:(g + 1) * CHUNK], bank[:, (2 * g) % 8, 0:CHUNK], ACT.Copy).then_inc(x_evac_a.sem, 1)
                act_gn(act, img, 0)
                act_project(act, img, 0)
                act_attend0(act, img)
                act_output(act, img, 0)
                if LAYERS > 1:
                    act_gn(act, img, 1)
                    act_layer1(act, img)
                if LAYERS > 2:
                    act_gn(act, img, 2)
                    act_project(act, img, 1)
                    act_attend2(act, img)
                    act_output(act, img, 1)
                if LAYERS > 3:
                    act_gn(act, img, 3)
                    act.wait_ge(*xn_v.at(img, 4))
                    act.wait_ge(*xn_a.at(img, 4))
                    act_layer3(act, img)
                act_store(act, img)

        @block.vector
        def _(dve):
            dve.wait_ge(w_turned.sem, 1)
            for m in range(6):
                dve.tensor_copy(w0t[:, :, m // 2, m % 2, :], bank[:, m, 0:2 * P].rearrange("p (q n) -> p q n", q=2))
            for q in range(2):
                dve.tensor_copy(o0t[:, :, q, :], bank[:, 6 + q, 0:2 * P].rearrange("p (a n) -> p a n", a=2))
            dve.drain()
            dve.memset(xnp[:, :, :, :], 0.0)
            dve.drain().then_inc(w_copied.sem, 1)
            dve.drain().then_inc(zeroed.sem, 1)
            dve.wait_ge(const_in.sem, CONSTS)
            dve_bn(dve)
            dve.tensor_copy(w3half, w3raw)
            dve.drain()
            dve.tensor_copy(w3raw, w3half)
            dve.drain()
            dve.tensor_scalar(w3raw, w3raw, -1.0, 1.0, ALU.max, ALU.min)
            dve.memset(bg2s[:, 2:2 + REG2], 1.0)
            dve.drain().then_inc(w3_half.sem, 1)
            dve.wait_ge(w3_made.sem, 1)
            with dve.Fori(0, B) as img:
                for g in range(CHUNKS):
                    dve.wait_ge(*x_turned.at(img, 2 * g + 2))
                    dve.tensor_copy(res[:, 1, g * CHUNK:(g + 1) * CHUNK], bank[:, (2 * g + 1) % 8, 0:CHUNK]).then_inc(x_evac_v.sem, 1)
                dve.drain()
                dve.wait_ge(*x_evac_a.at(img, CHUNKS))
                dve_gn(dve, img, 0, 1e-5)
                dve_diag(dve, 0, lepe_w)
                dve_project(dve, img, 0)
                dve_attend0(dve, img)
                if LAYERS > 1:
                    dve_diag(dve, 1, g_w)
                    dve_diag(dve, 2, g1_w, diag_g1)
                    dve.wait_ge(*res_done.at(img, 1))
                    dve_gn(dve, img, 1, 1e-5)
                    dve.wait_ge(*mirrored.at(img, 1))
                    dve.sem_inc(passed, 1)
                    dve_layer1(dve, img)
                if LAYERS > 2:
                    dve_gn(dve, img, 2, 1e-5)
                    dve_diag(dve, 3, dw2_w)
                    dve_project(dve, img, 1)
                    dve_attend2(dve, img)
                if LAYERS > 3:
                    dve.wait_ge(*res_done.at(img, 3))
                    dve_gn(dve, img, 3, 1e-5)
                    dve_layer3(dve, img)

        @block.gpsimd
        def _(pool):
            for st in CREDITS:
                pool.sem_inc(st.sem, st.credit)
            with pool.Fori(0, B) as img:
                pool.wait_ge(*res_done.at(img, 0))
                pool.sem_inc(passed, 1)
                pool.memset(vpad[:, :], 0.0)
                pool.drain()
                pool_project(pool, img, 0)
                pool_attend0(pool, img)
                pool_output(pool, img, 0)
                if LAYERS > 1:
                    pool_layer1(pool, img)
                if LAYERS > 2:
                    pool.wait_ge(*res_done.at(img, 2))
                    pool.sem_inc(passed, 1)
                    pool.memset(vpad[:, :], 0.0)
                    pool.drain()
                    pool_project(pool, img, 1)
                    pool_gather2(pool, img)
                    pool_output(pool, img, 1)


_BN1 = [f"L1_conv_{n}_{k}" for n in ("g", "g1", "out") for k in ("gamma", "beta", "mean", "var")]
_INS = ["x", "L0_conv_qkv_w", "L0_conv_qkv_b", "L0_conv_lepe_w", "L0_conv_lepe_b", "L0_conv_out_w", "L0_conv_out_b",
        "L1_conv_wg", "L1_conv_wg1", "L2_conv_w_qkv", "L2_conv_b_qkv", "L2_conv_w_g1", "L2_conv_b_g1", "L2_conv_w_g2",
        "L2_conv_b_g2", "L2_conv_dw_kernel", "L2_conv_dw_bias", "L2_conv_w_proj", "L2_conv_b_proj", "L3_conv_w"]


def shape_constants():
    mats = np.zeros((P, 6, P), np.float32)
    p = np.arange(P)
    mats[p, 0, p] = 1.0
    mats[:, 1, :] = (p[:, None] // 4 == p[None, :] // 4) / 8.0
    mats[(p - 1) % P, 2, p] = 1.0
    mats[(p + 1) % P, 3, p] = 1.0
    mats[:, 4] = mats[:, 2] - mats[:, 0]
    mats[:, 5] = mats[:, 0] - mats[:, 3]
    w = np.arange(REG2)
    posd = np.zeros((REG2, 3, REG2), np.float32)
    posd[:, 0] = (w[None, :] % R2 - w[:, None] % R2) ** 2
    posd[:, 1] = (w[None, :] // R2 - w[:, None] // R2) ** 2
    posd[:, 2] = w[None, :]
    return mats, posd


def kernel(LAYERS=4, **inputs):
    import concourse.bacc as _bacc
    from concourse.bass_utils import run_bass_kernel_spmd as _run

    nc = _bacc.Bacc("TRN2", target_bir_lowering=False, num_devices=1)
    arrays = {n: np.ascontiguousarray(inputs[n]) for n in _INS}
    arrays["bn1"] = np.stack([np.asarray(inputs[n]) for n in _BN1])
    arrays["mats"], arrays["posd"] = shape_constants()
    ap = {n: nc.dram_tensor(f"in_{n}", a.shape, mybir.dt.from_np(a.dtype), kind="ExternalInput").ap() for n, a in arrays.items()}
    out = nc.dram_tensor("out_x", arrays["x"].shape, F32, kind="ExternalOutput").ap()
    names = _INS[:9] + ["bn1"] + _INS[9:] + ["mats", "posd"]
    build_blocks(nc, *[ap[n] for n in names], out, **({} if LAYERS == 4 else {"LAYERS": LAYERS}))
    r = _run(nc, [{f"in_{n}": a for n, a in arrays.items()}], core_ids=[0])
    return r.results[0]["out_x"]
```

```python
from contextlib import ExitStack

import numpy as np

import concourse.bass as bass
from concourse import mybir

ALU = mybir.AluOpType
ACT = mybir.ActivationFunctionType
AX = mybir.AxisListType
F32 = mybir.dt.float32
BF16 = mybir.dt.bfloat16
F16 = mybir.dt.float16
U32 = mybir.dt.uint32
SP, POOL = mybir.EngineType.SP, mybir.EngineType.Pool

P = 128
H = W = 56
C = 256
N = H * W
PW = W + 2
PN = (H + 2) * PW
TAPS = 9
CHUNK = 448
CHUNKS = N // CHUNK
TOK = 112

R0, S0 = 7, 8
REG0, TOK0 = R0 * R0, S0 * S0
TOPK = 4
HD = 32
TILES = 4
KEYS0 = TOPK * TOK0
KEPT = KEYS0 // 8
LAYERS = 4
VS = 4
LAPS = (REG0 - 1) // (2 * VS)
SECOND_HALF = {1: range(0, 3), 2: range(3, 6), 3: range(6, 9)}
FIRST_HALF = {4: range(0, 2), 5: range(2, 4), 6: range(4, 6), 7: range(6, 8), 8: range(8, 9)}
REMOVED = -1.0e30
SCALE0 = float(C) ** -0.5
ORDER = (4, 5, 0, 1, 2, 3)
VECTOR = (4, 5, 3)
R2, S2 = 8, 7
REG2, TOK2 = R2 * R2, S2 * S2
KEYS2 = TOPK * TOK2
HK2 = 2 * TOK2
SCALE2 = float(C // 8) ** -0.5
VW2 = 64
VOFF2 = 16
DT = 0.2
STEPS = 5
BN_EPS = 0.001
ROWS1 = 14
CH1 = H // ROWS1
E1 = ROWS1 * W


class Stage:

    def __init__(self, sem, per, credit=0):
        self.sem, self.per, self.credit = sem, per, credit

    def at(self, img, k):
        return self.sem, img * self.per + (k + self.credit)


def build_blocks(nc, x, w0_qkv, b0_qkv, w0_lepe, b0_lepe, w0_out, b0_out,
                 w1_g, w1_g1, bn1,
                 w2_qkv, b2_qkv, w2_g1, b2_g1, w2_g2, b2_g2, w2_dw, b2_dw, w2_proj, b2_proj,
                 w3, mats, posd, out):
    B = x.shape[0]
    with ExitStack() as ctx:
        stages = []

        def sb(name, shape, dt=F32):
            return ctx.enter_context(nc.sbuf_tensor(name, shape, dt))

        def dram(name, shape, dt=F32):
            return nc.dram_tensor(name, shape, dt, kind="Internal").ap()

        def stage(name, per, credit=0):
            stages.append(Stage(ctx.enter_context(nc.semaphore(name)), per, credit))
            return stages[-1]

        q_dram = dram("q_dram", [P, REG0, 2, TOK0])
        k_dram = dram("k_dram", [P, REG0, 2, TOK0])
        v_dram = dram("v_dram", [REG0, TOK0, C])
        q2_dram = dram("q2_dram", [P, REG2, 2, TOK2])
        k2_dram = dram("k2_dram", [P, REG2, 2, TOK2])
        v2_dram = dram("v2_dram", [REG2, TOK2, C])
        idx0_dram = dram("idx0_dram", [REG0, TOPK], U32)
        idx2_dram = dram("idx2_dram", [REG2, TOPK], U32)
        gw_dram = dram("gw_dram", [REG2, TOPK])

        bank = ctx.enter_context(nc.psum_tensor("bank", [P, 8, 512], F32))

        res = sb("res", [P, 2, N])
        xnp = sb("xnp", [P, 2, H + 2, PW])
        vpad = sb("vpad", [P, 2 * PN + 2 * E1])
        att = sb("att", [P, 2, N])
        w0t = sb("w0t", [P, 2, 3, 2, P])
        o0t = sb("o0t", [P, 2, 2, P])
        w2s = sb("w2s", [P, 2, 3 * C])
        p2s = sb("p2s", [P, 2, C])
        diag = sb("diag", [P, TAPS, 2, P])
        mat = sb("mat", [P, 6, P])
        w3s = sb("w3s", [P, TAPS, 2, C], BF16)
        wg1s = sb("wg1s", [P, 2, REG2])
        wg2s = sb("wg2s", [REG2, 4])
        bg2s = sb("bg2s", [1, 2 + REG2])
        posd_s = sb("posd_s", [REG2, 3, REG2])
        diag_g1 = sb("diag_g1", [P, TAPS, 2, P])
        bias0 = sb("bias0", [P, 3, 2])
        bias2 = sb("bias2", [P, 3, 2])
        small = sb("small", [P, 64])
        lepe_w = sb("lepe_w", [P, 2, TAPS])
        dw2_w = sb("dw2_w", [P, 2, TAPS])
        g_w = sb("g_w", [P, 2, TAPS])
        g1_w = sb("g1_w", [P, 2, TAPS])
        bns = sb("bns", [P, 2, 12])
        bnc = sb("bnc", [P, 3, 2, 2])
        stats = sb("stats", [P, 2, R2, 6])
        mv = sb("mv", [P, 2, 2])
        ms = sb("ms", [P, 2, 2])
        grp = sb("grp", [P, 2, 2])
        gm = sb("gm", [P, 8])
        SC = 13056
        scratch = sb("scratch", [P, SC])

        ident = mat[:, 0, :]
        lepe_b, out0_b = small[:, 0:2], small[:, 2:4]
        dw2_b, proj_b = small[:, 4:6], small[:, 6:8]

        top = [0]

        def carve(n, **shape):
            assert top[0] + n <= SC, (top[0], n)
            v = scratch[:, top[0]:top[0] + n]
            top[0] += n
            return v

        top[0] = 0
        tok = carve(2 * 4 * C).rearrange("p (s k c) -> p s k c", s=2, k=4)
        ysum = carve(2 * 2 * CHUNK).rearrange("p (s q n) -> p s q n", s=2, q=2)
        tok_in = carve(CHUNKS * 4 * C).rearrange("p (s k c) -> p s k c", s=CHUNKS, k=4)
        top[0] = 0
        qks_flat = carve(2 * R0 * 2 * TOK0)
        qks = [qks_flat[:, 0:2 * R * 2 * T].rearrange("p (k w a t) -> p k w a t", k=2, w=R, a=2) for R, T in ((R0, TOK0), (R2, TOK2))]
        vrow = carve(2 * CHUNK).rearrange("p (a n) -> p a n", a=2)
        vtk = carve(R2 * C).rearrange("p (w c) -> p w c", w=R2)
        pool_flat, mean_flat, qkr_flat = carve(2 * H * R2), carve(2 * REG2), carve(4 * REG2)
        pool_a = [pool_flat[:, 0:2 * H * R].rearrange("p (q y w) -> p q y w", q=2, y=H) for R in (R0, R2)]
        pool_m = [mean_flat[:, 0:2 * R * R].rearrange("p (q r) -> p q r", q=2) for R in (R0, R2)]
        qkr = [qkr_flat[:, 0:4 * R * R].rearrange("p (k a r) -> p k a r", k=2, a=2) for R in (R0, R2)]
        aff = carve(REG2)
        v8 = carve(8)
        i8 = carve(8).bitcast(U32)
        idx_row = carve(REG2 * TOPK).bitcast(U32)
        base_attn = top[0]
        qg = carve(2 * 2 * TOK0).rearrange("p (s a t) -> p s a t", s=2, a=2)
        kg = carve(2 * TOPK * 2 * TOK0).rearrange("p (s t a n) -> p s t a n", s=2, t=TOPK, a=2)
        vg = carve(VS * 2 * C).rearrange("p (s c n) -> p s c n", s=VS, c=2)
        sc_sb = carve(2 * TILES * KEYS0).rearrange("p (s j n) -> p s j n", s=2, j=TILES)
        top[0] = 0
        rem = carve(TILES * KEYS0).rearrange("p (j n) -> p j n", j=TILES)
        ee = carve(TILES * KEYS0).rearrange("p (j n) -> p j n", j=TILES)
        er = carve(TILES * KEYS0).rearrange("p (j n) -> p j n", j=TILES)
        pt = carve(2 * 2 * P).rearrange("p (s c n) -> p s c n", s=2, c=2)
        best = carve(2 * TILES * KEPT).rearrange("p (s j n) -> p s j n", s=2, j=TILES)
        ebest = carve(TILES * KEPT).rearrange("p (j n) -> p j n", j=TILES)
        nmax = carve(2 * TILES).rearrange("p (s j) -> p s j", s=2)
        zsum = carve(2 * TILES).rearrange("p (s j) -> p s j", s=2)
        rz = carve(2 * TILES).rearrange("p (s j) -> p s j", s=2)
        osb = carve(TILES * HD).rearrange("p (j d) -> p j d", j=TILES)
        assert top[0] <= base_attn - REG2 * TOPK, (top[0], base_attn)
        top[0] = base_attn
        hid = carve(REG2)
        sig = carve(16)
        gauss = carve(REG2)
        idx_f = carve(8)
        gsum = carve(2)
        gwt = carve(TOPK)
        gws = carve((REG2 // 2) * TOPK).rearrange("p (u t) -> p u t", t=TOPK)
        q2g_flat = carve(2 * 2 * 2 * 64)
        q2g = q2g_flat.rearrange("p (s i a t) -> p s i a t", s=2, i=2, a=2)
        k2g = carve(2 * 2 * TOPK * 2 * TOK2).rearrange("p (s i t a n) -> p s i t a n", s=2, i=2, t=TOPK, a=2)
        v2g = carve(VS * 2 * 2 * C).rearrange("p (s i c n) -> p s i c n", s=VS, i=2, c=2)
        top[0] = 0
        lg2 = carve(2 * KEYS2).rearrange("p (s n) -> p s n", s=2)
        e2 = carve(2 * KEYS2).rearrange("p (s n) -> p s n", s=2)
        w2p = carve(2 * KEYS2).rearrange("p (s n) -> p s n", s=2)
        pt2 = carve(2 * 2 * P).rearrange("p (s c n) -> p s c n", s=2, c=2)
        max2, z2, rz2 = carve(2), carve(2), carve(2)
        assert top[0] <= base_attn - REG2 * TOPK
        vp16 = vpad[:, 0:2 * PN].bitcast(BF16)
        parts = [v.rearrange("p (q y x) -> p q y x", q=2, y=H + 2) for v in
                 (vp16[:, 0:2 * PN], vp16[:, 2 * PN:4 * PN], att[:, :, :].rearrange("p a n -> p (a n)")[:, 0:PN].bitcast(BF16))]
        w3raw = scratch[:, 0:TAPS * 2 * C]
        w3half = scratch[:, TAPS * 2 * C:TAPS * 3 * C].bitcast(F16)
        top[0] = 0
        otmp = carve(2 * 2 * CHUNK).rearrange("p (s q n) -> p s q n", s=2, q=2)

        top[0] = 0
        A1 = 2 * E1
        arrays1 = [carve(A1) for _ in range(8)] + [att[:, :, :].rearrange("p a n -> p (a n)")[:, k * A1:(k + 1) * A1] for k in range(4)] + [vpad[:, 2 * PN:2 * PN + A1]]
        c0, cE, cmx, cpx, cmy, cpy, cF, hA, hB, acc, prod, ax1, ay1 = [a.rearrange("p (q n) -> p q n", q=2) for a in arrays1]

        diff_x = scratch[:, 2 * A1:2 * A1 + 2 * (ROWS1 + 2) * W].rearrange("p (q y x) -> p q y x", q=2, x=W)
        diff_y = scratch[:, 0:2 * ROWS1 * PW].rearrange("p (q y x) -> p q y x", q=2, x=PW)

        V2A = VOFF2 + REG2 * VW2 + 16
        def v2_view(a, shift):
            o = a * V2A + VOFF2 + shift
            return vpad[:, o:o + REG2 * VW2].rearrange("p (w y x) -> p w y x", y=8, x=8)

        VP0 = vpad[:, 0:2 * PN].rearrange("p (a y x) -> p a y x", a=2, y=H + 2)

        passed = ctx.enter_context(nc.semaphore("passed"))
        const_in = stage("const_in", 0)
        wraw_in = stage("wraw_in", 0)
        w_turned = stage("w_turned", 0)
        w_copied = stage("w_copied", 0)
        zeroed = stage("zeroed", 0)
        x_in = [stage(f"x_in{g}", 16) for g in range(CHUNKS)]
        x_turned = stage("x_turned", 2 * CHUNKS)
        x_evac_a = stage("x_evac_a", CHUNKS)
        x_evac_v = stage("x_evac_v", CHUNKS)
        gn_ms = stage("gn_ms", LAYERS)
        gn_grp = stage("gn_grp", LAYERS)
        gn_var = stage("gn_var", LAYERS)
        gn_sqrt = stage("gn_sqrt", LAYERS)
        gn_coef = stage("gn_coef", LAYERS)
        xn_a = stage("xn_a", LAYERS)
        xn_v = stage("xn_v", LAYERS)
        res_done = stage("res_done", LAYERS, 1)
        bn_sqrt = stage("bn_sqrt", 0)
        bn_ready = stage("bn_ready", 0)
        bn_var = stage("bn_var", 0)
        mirror_in = stage("mirror_in", 1)
        mirrored = stage("mirrored", 1)
        g_mm = stage("g_mm", 2 * CH1)
        g1_mm = stage("g1_mm", 2 * CH1)
        ax_evac = stage("ax_evac", 2 * CH1)
        ay_evac = stage("ay_evac", 2 * CH1)
        sobel_done = stage("sobel_done", 2 * CH1)
        squared = stage("squared", 2 * CH1)
        gy_begun = stage("gy_begun", CH1)
        e_diff = stage("e_diff", CH1)
        e_evac = stage("e_evac", CH1)
        e_added = stage("e_added", CH1)
        s_made = stage("s_made", CH1)
        n_made = stage("n_made", CH1)
        r_made = stage("r_made", CH1)
        r_scaled = stage("r_scaled", CH1)
        d_made = stage("d_made", CH1)
        ay_scaled = stage("ay_scaled", CH1)
        e_scaled = stage("e_scaled", CH1)
        d_scaled = stage("d_scaled", CH1)
        coef_done = stage("coef_done", CH1)
        h_set = stage("h_set", CH1)
        h_ready = stage("h_ready", CH1 * STEPS)
        shifted = stage("shifted", CH1 * STEPS)
        own_part = stage("own_part", CH1 * STEPS)
        y1_ready = stage("y1_ready", CH1)
        NR = (R0, R2)
        qkv_mm = [stage(f"qkv_mm{l}", 6 * NR[l]) for l in range(2)]
        qk_evac_a = [stage(f"qk_evac_a{l}", 3 * NR[l], 4) for l in range(2)]
        qkv_evac_v = [stage(f"qkv_evac_v{l}", 3 * NR[l], 4) for l in range(2)]
        v_padded = [stage(f"v_padded{l}", NR[l], 1) for l in range(2)]
        v_turned = [stage(f"v_turned{l}", 4 * NR[l], 1) for l in range(2)]
        vtk_evac = [stage(f"vtk_evac{l}", 4 * NR[l], 4) for l in range(2)]
        qk_out = [stage(f"qk_out{l}", 32 * NR[l], 1) for l in range(2)]
        v_out = [stage(f"v_out{l}", 16 * NR[l], 1) for l in range(2)]
        pooled = [stage(f"pooled{l}", 1) for l in range(2)]
        qkr_mm = [stage(f"qkr_mm{l}", 1) for l in range(2)]
        qkr_evac = [stage(f"qkr_evac{l}", 1) for l in range(2)]
        aff_mm = [stage(f"aff_mm{l}", 1) for l in range(2)]
        idx_found = [stage(f"idx_found{l}", 1) for l in range(2)]
        idx_out = [stage(f"idx_out{l}", 16) for l in range(2)]
        idx_in = [stage(f"idx_in{l}", 16) for l in range(2)]
        kq_in = [stage(f"kq_in{s}", 16 * 5 * (25 - s)) for s in range(2)]
        v_in = [stage(f"v_in{s}", 16 * 4 * len(range(s, REG0, VS))) for s in range(VS)]
        NT = REG0 * TILES
        scored = stage("scored", NT)
        s_copied = stage("s_copied", NT, 4)
        topk_step = ctx.enter_context(nc.semaphore("topk_step"))
        topped = stage("topped", NT)
        exped = stage("exped", NT, 4)
        kept = stage("kept", NT)
        p_turned = stage("p_turned", NT, 4)
        pt_evac = stage("pt_evac", NT, 4)
        pv_done = stage("pv_done", REG0)
        o_norm = stage("o_norm", REG0)
        o_turned = stage("o_turned", REG0, 1)
        o_evac = stage("o_evac", REG0, 2)
        lepe_mm = stage("lepe_mm", 2 * R0)
        lepe_evac = stage("lepe_evac", 2 * R0, 1)
        hid_mm = stage("hid_mm", 1)
        hid_relu = stage("hid_relu", 1)
        gate_mm = stage("gate_mm", 1)
        gate_neg = stage("gate_neg", 1)
        gate_exp = stage("gate_exp", 1)
        gate_one = stage("gate_one", 1)
        gate_ln = stage("gate_ln", 1)
        dist_done = stage("dist_done", 1)
        gauss_exp = stage("gauss_exp", 1)
        gwt_done = stage("gwt_done", 1)
        gw_out = stage("gw_out", 16)
        gw_in = stage("gw_in", 32)
        q2_zeroed = stage("q2_zeroed", 1)
        NP2 = REG2 // 2
        kq2_in = [stage(f"kq2_in{s}", 16 * 9 * NP2 // 2) for s in range(2)]
        v2_in = [stage(f"v2_in{s}", 16 * 8 * NP2 // VS) for s in range(VS)]
        scored2 = stage("scored2", NP2)
        logit2 = stage("logit2", NP2, 2)
        exped2 = stage("exped2", NP2, 2)
        weighted2 = stage("weighted2", NP2, 2)
        turned2 = stage("turned2", NP2, 2)
        pt2_evac = stage("pt2_evac", NP2, 2)
        pv2_done = stage("pv2_done", NP2)
        out2_evac = stage("out2_evac", NP2, 2)
        w3_half = stage("w3_half", 0)
        w3_made = stage("w3_made", 0)
        part_made = [stage(f"part_made{k}", 2) for k in range(3)]
        rest_made = stage("rest_made", 2)
        c3_mm = stage("c3_mm", CHUNKS)
        c3_added = stage("c3_added", 2 * CHUNKS, 3)
        diag_made = [stage(f"diag_made{k}", 1) for k in range(4)]
        om_mm = [stage(f"om_mm{l}", 2 * NR[l]) for l in range(2)]
        om_evac = [stage(f"om_evac{l}", 2 * NR[l], 4) for l in range(2)]
        om_added = [stage(f"om_added{l}", 2 * NR[l], 4) for l in range(2)]
        y_turned = stage("y_turned", 2 * CHUNKS, 3)
        y_evac = stage("y_evac", 2 * CHUNKS, 4)
        y_out = [stage(f"y_out{s}", 16 * (4 - s), 1) for s in range(2)]

        wraw = xnp[:, :, :, :].rearrange("p q y x -> p (q y x)")
        w0raw = wraw[:, 0:6 * C].rearrange("p (m c) -> p m c", m=6)
        o0raw = wraw[:, 6 * C:8 * C].rearrange("p (m c) -> p m c", m=2)

        BLK = (S0 * S0 * R0, S2 * S2 * R2)
        SS, RR = (S0, S2), (R0, R2)

        def region_view(img3, l, row):
            s = SS[l]
            return img3[:, bass.ds(row * s, s), :].rearrange("p y (w x) -> p w y x", x=s)

        CREDITS = [st for st in stages if st.credit]
        CONSTS = 16 * (7 + 9 + 10)
        block = ctx.enter_context(nc.Block())

        def sp_project(sp, img, l):
            R, T = RR[l], (TOK0, TOK2)[l]
            qd, kd, vd = ((q_dram, k_dram, v_dram), (q2_dram, k2_dram, v2_dram))[l]
            with sp.Fori(0, R) as i:
                sp.wait_ge(*qk_evac_a[l].at(img, 3 * i + 3))
                sp.sem_inc(passed, 1)
                sp.wait_ge(*qkv_evac_v[l].at(img, 3 * i + 3))
                sp.dma_start(qd[:, bass.ds(i * R, R)], qks[l][:, 0]).then_inc(qk_out[l].sem, 16)
                sp.dma_start(kd[:, bass.ds(i * R, R)], qks[l][:, 1]).then_inc(qk_out[l].sem, 16)
                sp.wait_ge(*vtk_evac[l].at(img, 4 * i + 4))
                sp.dma_start(vd[bass.ds(i * R, R)].rearrange("w t c -> t w c"), vtk[0:T, 0:R]).then_inc(v_out[l].sem, 16)
            idd = (idx0_dram, idx2_dram)[l]
            sp.wait_ge(*idx_found[l].at(img, 1))
            sp.dma_start(idd[:, :], i8[0:R * R, 0:TOPK]).then_inc(idx_out[l].sem, 16)
            sp.wait_ge(*idx_out[l].at(img, 16))
            sp.dma_start(idx_row[0:1, 0:R * R * TOPK], idd.rearrange("(o r) t -> o (r t)", o=1)).then_inc(idx_in[l].sem, 16)
            sp.wait_ge(*idx_in[l].at(img, 16))
            sp.wait_ge(*qk_out[l].at(img, 32 * R))
            sp.wait_ge(*v_out[l].at(img, 16 * R))

        def numbers(engine, at, n, limit):
            return nc.values_load_multi_w_load_instructions(idx_row[0:1, bass.ds(at, n)], engines=(engine,), min_val=0, max_val=limit - 1)[1]

        def sp_gather0(sp, img):
            def gather(r, s, v, wait, wait_v):
                ids = numbers(SP, r * TOPK, TOPK, REG0)
                if wait:
                    sp.wait_ge(*scored.at(img, (r - 1) * TILES))
                sp.dma_start(qg[:, s], q_dram[:, bass.ds(r, 1)].rearrange("p r a t -> p (r a) t")).then_inc(kq_in[s].sem, 16)
                for t in range(TOPK):
                    sp.dma_start(kg[:, s, t], k_dram[:, bass.ds(ids[t], 1)].rearrange("p r a t -> p (r a) t")).then_inc(kq_in[s].sem, 16)
                if wait_v:
                    sp.wait_ge(*pv_done.at(img, r - VS + 1))
                for t in range(TOPK):
                    sp.dma_start(vg[64 * (t % 2):64 * (t % 2) + 64, v, t // 2], v_dram[bass.ds(ids[t], 1)].rearrange("r t c -> (r t) c")).then_inc(v_in[v].sem, 16)
            sp.sem_inc(passed, 1)
            for r in range(VS):
                gather(r, r % 2, r, r >= 2, False)
            with sp.Fori(1, REG0 // VS) as i:
                for v in range(VS):
                    gather(VS * i + v, v % 2, v, True, True)
            gather(REG0 - 1, 0, 0, True, True)

        def sp_gather2(sp, img):
            sp.wait_ge(*gwt_done.at(img, 1))
            sp.dma_start(gw_dram, gwt[0:REG2, :]).then_inc(gw_out.sem, 16)
            sp.wait_ge(*gw_out.at(img, 16))
            for i in range(2):
                sp.dma_start(gws[64 * i:64 * i + 64], gw_dram.rearrange("(o w i) t -> i o w t", i=2, o=1)[i].to_broadcast([64, NP2, TOPK])).then_inc(gw_in.sem, 16)
            sp.wait_ge(*q2_zeroed.at(img, 1))

            def gather(u, s, wait):
                sp.sem_inc(passed, 1)
                ids = numbers(SP, 2 * u * TOPK, 2 * TOPK, REG2)
                if wait:
                    sp.wait_ge(*scored2.at(img, u - 1))
                sp.dma_start(q2g[:, s, :, :, 0:TOK2].rearrange("p i a t -> p (i a) t"), q2_dram[:, bass.ds(2 * u, 2)].rearrange("p r a t -> p (r a) t")).then_inc(kq2_in[s].sem, 16)
                for i in range(2):
                    for t in range(TOPK):
                        sp.dma_start(k2g[:, s, i, t], k2_dram[:, bass.ds(ids[i * TOPK + t], 1)].rearrange("p r a t -> p (r a) t")).then_inc(kq2_in[s].sem, 16)


            gather(0, 0, False)
            gather(1, 1, False)
            with sp.Fori(1, NP2 // 2) as n:
                gather(2 * n, 0, True)
                gather(2 * n + 1, 1, True)

        def pool_gather2(pool, img):
            def gather(u, s, wait):
                ids = numbers(POOL, 2 * u * TOPK, 2 * TOPK, REG2)
                if wait:
                    pool.wait_ge(*pv2_done.at(img, u - VS + 1))
                for i in range(2):
                    for t in range(TOPK):
                        pool.dma_start(v2g[TOK2 * (t % 2):TOK2 * (t % 2) + TOK2, s, i, t // 2],
                                     v2_dram[bass.ds(ids[i * TOPK + t], 1)].rearrange("r t c -> (r t) c")).then_inc(v2_in[s].sem, 16)
            pool.wait_ge(*v_out[1].at(img, 16 * R2))
            pool.wait_ge(*idx_in[1].at(img, 16))
            pool.sem_inc(passed, 1)
            for v in range(VS):
                gather(v, v, False)
            with pool.Fori(1, NP2 // VS) as n:
                for v in range(VS):
                    gather(VS * n + v, v, True)

        def sp_store(sp, img):
            def rows(g, s):
                sp.wait_ge(*y_evac.at(img, 2 * g + 2))
                sp.dma_start(out[img, bass.ds(8 * g, 8)].rearrange("(k y) x c -> (y x) k c", k=4), tok[0:TOK, s]).then_inc(y_out[s].sem, 16)
            with sp.Fori(0, CHUNKS // 2) as i:
                rows(2 * i, 0)
                rows(2 * i + 1, 1)
            rows(CHUNKS - 1, 0)
            sp.wait_ge(*y_out[0].at(img, 64))
            sp.sem_inc(passed, 1)
            sp.wait_ge(*y_out[1].at(img, 48))
            sp.sem_inc(passed, 1)

        def pe_gn(pe, img, n):
            pe.wait_ge(*gn_ms.at(img, n + 1))
            pe.matmul(bank[:, 7, 0:4], lhsT=mat[:, 1, :], rhs=ms[:, :, :].rearrange("p q s -> p (q s)"), start=True, stop=True).then_inc(gn_grp.sem, 1)
            pe.wait_ge(*xn_a.at(img, n + 1))
            pe.wait_ge(*xn_v.at(img, n + 1))

        def weight(l, q, kind, a):
            return w0t[:, q, kind, a, :] if l == 0 else w2s[:, q, kind * C + a * P:kind * C + (a + 1) * P]

        def pe_project(pe, img, l):
            R, T, n = RR[l], (TOK0, TOK2)[l], BLK[l]
            def routing():
                pe.wait_ge(*pooled[l].at(img, 1))
                for kind in range(2):
                    for a in range(2):
                        o = (2 * kind + a) * 64
                        for q in range(2):
                            m = pe.matmul(bank[:, 6, o:o + R * R], lhsT=weight(l, q, kind, a), rhs=pool_m[l][:, q, :], start=q == 0, stop=q == 1)
                m.then_inc(qkr_mm[l].sem, 1)
                pe.wait_ge(*qkr_evac[l].at(img, 1))
                for a in range(2):
                    m = pe.matmul(bank[0:R * R, 7, 0:R * R], lhsT=qkr[l][:, 0, a], rhs=qkr[l][:, 1, a], start=a == 0, stop=a == 1)
                m.then_inc(aff_mm[l].sem, 1)
                if l == 1:
                    for a in range(2):
                        m = pe.matmul(bank[0:REG2, 6, 256:256 + REG2], lhsT=wg1s[:, a, :], rhs=qkr[1][:, 0, a], start=a == 0, stop=a == 1)
                    m.then_inc(hid_mm.sem, 1)
                    pe.wait_ge(*hid_relu.at(img, 1))
                    pe.sem_inc(passed, 1)
                    pe.matmul(bank[0:REG2, 6, 320:322], lhsT=hid[0:REG2, :], rhs=wg2s[:, 0:2], start=True, stop=False)
                    pe.matmul(bank[0:REG2, 6, 320:322], lhsT=bg2s[:, 2:2 + REG2], rhs=bg2s[:, 0:2], start=False, stop=True).then_inc(gate_mm.sem, 1)
                    pe.wait_ge(*gate_neg.at(img, 1))
                    pe.sem_inc(passed, 1)
                pe.wait_ge(*idx_found[l].at(img, 1))
                pe.sem_inc(passed, 1)

            def project(i):
                for m in ORDER:
                    kind, a = m // 2, m % 2
                    if m < 3:
                        pe.wait_ge(*qk_evac_a[l].at(img, 3 * i + m - 2))
                    else:
                        pe.wait_ge(*qkv_evac_v[l].at(img, 3 * i + VECTOR.index(m) - 2))
                    for q in range(2):
                        mm = pe.matmul(bank[:, m, 0:n], lhsT=weight(l, q, kind, a),
                                       rhs=region_view(xnp[:, q, 1:H + 1, 1:W + 1], l, i), start=q == 0, stop=q == 1)
                    mm.then_inc(qkv_mm[l].sem, 1)

            def turn(i):
                pe.wait_ge(*qkv_evac_v[l].at(img, 3 * i + 2))
                for u in range(4):
                    pe.wait_ge(*vtk_evac[l].at(img, 4 * i + u - 1))
                    pe.sem_inc(passed, 1)
                    for w in range(2 * u, min(2 * u + 2, R)):
                        for a in range(2):
                            t = pe.transpose(bank[0:T, 6 + u % 2, (w % 2) * C + a * P:(w % 2) * C + (a + 1) * P],
                                             vrow[:, a, w * T:(w + 1) * T], ident)
                    t.then_inc(v_turned[l].sem, 1)

            project(0)
            routing()
            turn(0)
            with pe.Fori(1, R) as i:
                project(i)
                turn(i)

        def pe_attend0(pe, img):
            def score(r, s, j):
                pe.wait_ge(*s_copied.at(img, r * TILES + j - 3))
                for a in range(2):
                    m = pe.matmul(bank[64 * a:64 * a + 64, j, 0:KEYS0], lhsT=qg[32 * j:32 * j + 32, s, a, :],
                                  rhs=kg[32 * j:32 * j + 32, s, :, a, :], start=True, stop=True)
                m.then_inc(scored.sem, 1)

            def turn(r, j):
                pe.wait_ge(*kept.at(img, r * TILES + j + 1))
                pe.wait_ge(*pt_evac.at(img, r * TILES + j))
                if j == 0:
                    pe.wait_ge(*o_evac.at(img, r - 1))
                for c in range(2):
                    t = pe.transpose(bank[:, 4, c * P:(c + 1) * P], ee[:, j, c * P:(c + 1) * P], ident)
                t.then_inc(p_turned.sem, 1)

            def values(r, s, v, j):
                pe.wait_ge(*pt_evac.at(img, r * TILES + j + 1))
                for a in range(2):
                    for c in range(2):
                        m = pe.matmul(bank[64 * a:64 * a + 64, 5 + s, j * HD:(j + 1) * HD],
                                      lhsT=pt[:, j % 2, c, a * 64:a * 64 + 64],
                                      rhs=vg[:, v, c, a * P + 32 * j:a * P + 32 * j + HD], start=c == 0, stop=c == 1)
                if j == TILES - 1:
                    m.then_inc(pv_done.sem, 1)

            def turn_out(r):
                pe.wait_ge(*o_norm.at(img, r + 1))
                pe.wait_ge(*lepe_evac.at(img, 2 * (r // R0) + 2))
                pe.sem_inc(passed, 1)
                pe.matmul(bank[:, 4, 2 * P:3 * P], lhsT=ident, rhs=att[:, :, bass.ds(r * TOK0, TOK0)], start=True, stop=False)
                pe.matmul(bank[:, 4, 2 * P:3 * P], lhsT=osb[:, :, :].rearrange("p j d -> p (j d)"), rhs=ident, start=False, stop=True).then_inc(o_turned.sem, 1)

            def lepe(row, a, taps, wait=True):
                if taps[0] == 0:
                    pe.wait_ge(*lepe_evac.at(img, 2 * row + a))
                for t in taps:
                    m = pe.matmul(bank[:, 7, 0:BLK[0]], lhsT=diag[:, t, a, :], rhs=region_view(VP0[:, a, t // 3:t // 3 + H, t % 3:t % 3 + W], 0, row),
                                  start=t == 0, stop=t == TAPS - 1)
                if taps[-1] == TAPS - 1:
                    m.then_inc(lepe_mm.sem, 1)

            def region(r, v, nth_next, nth, first=False, second=False, last=False, ahead=None):
                s = v % 2
                if not first:
                    values(r - 1, 1 - s, (v - 1) % VS, TILES - 1)
                if not first and not second:
                    turn_out(r - 2)
                if not last:
                    pe.wait_ge(*kq_in[1 - s].at(img, 80 * nth_next))
                    for j in range(TILES):
                        score(r + 1, 1 - s, j)
                for j in range(TILES):
                    turn(r, j)
                    if j > 0:
                        if j == 1:
                            pe.wait_ge(*v_in[v].at(img, 64 * nth))
                        values(r, s, v, j - 1)
                    if j == 1 and ahead:
                        lepe(*ahead)

            def lap(i, first=False, last=False):
                for n in range(1, 2 * VS + 1):
                    if n in SECOND_HALF:
                        ahead = (i + 1, 1, SECOND_HALF[n])
                    else:
                        ahead = None if last else (i + 2, 0, FIRST_HALF[n])
                    region(2 * VS * i + n, n % VS, VS * i + (n + 1) // 2 + 1, 2 * i + n // VS + 1, second=first and n == 1,
                           last=last and n == 2 * VS, ahead=ahead)

            pe.wait_ge(*diag_made[0].at(img, 1))
            pe.wait_ge(*v_padded[0].at(img, R0))
            pe.wait_ge(*vtk_evac[0].at(img, 4 * R0))
            pe.sem_inc(passed, 1)
            lepe(0, 0, range(TAPS))
            pe.wait_ge(*kq_in[0].at(img, 80))
            for j in range(TILES):
                score(0, 0, j)
            lepe(0, 1, range(TAPS))
            region(0, 0, 1, 1, first=True, ahead=(1, 0, range(TAPS)))
            lap(0, first=True)
            with pe.Fori(1, LAPS - 1) as i:
                lap(i)
            lap(LAPS - 1, last=True)
            values(REG0 - 1, 0, 0, TILES - 1)
            turn_out(REG0 - 2)
            pe.wait_ge(*o_evac.at(img, REG0 - 1))
            turn_out(REG0 - 1)

        def pe_output(pe, img, l):
            R, n = RR[l], BLK[l]
            pe.wait_ge(*(o_evac.at(img, REG0) if l == 0 else out2_evac.at(img, NP2)))
            pe.sem_inc(passed, 1)
            with pe.Fori(0, R) as i:
                for q in range(2):
                    pe.wait_ge(*om_evac[l].at(img, 2 * i + q - 1))
                    for a in range(2):
                        lhs = o0t[:, a, q, :] if l == 0 else p2s[:, a, q::2]
                        m = pe.matmul(bank[:, 2 + q, 0:n], lhsT=lhs, rhs=att[:, a, bass.ds(i * n, n)], start=a == 0, stop=a == 1)
                    m.then_inc(om_mm[l].sem, 1)

        def pe_layer1(pe, img):
            def conv(i, which, q):
                d, done = ((diag, g_mm), (diag_g1, g1_mm))[which]
                for h in range(2):
                    for t in range(TAPS):
                        m = pe.matmul(bank[:, 2 * q + h, 0:E1 // 2], lhsT=d[:, t, q, :],
                                      rhs=xnp[:, q, bass.ds(i * ROWS1 + h * (ROWS1 // 2) + t // 3, ROWS1 // 2), t % 3:t % 3 + W],
                                      start=t == 0, stop=t == TAPS - 1)
                m.then_inc(done.sem, 1)

            def piece(i, n):
                if n == 2:
                    pe.wait_ge(*ax_evac.at(img, 2 * i + 2))
                conv(i, n // 2, n % 2)

            def shift(src, first, second):
                for h in range(2):
                    e = slice(h * (E1 // 2), (h + 1) * (E1 // 2))
                    pe.matmul(bank[:, 4 + h, 0:E1 // 2], lhsT=mat[:, first, :], rhs=src[:, 1, e], start=True, stop=True)
                    m = pe.matmul(bank[:, 6 + h, 0:E1 // 2], lhsT=mat[:, second, :], rhs=src[:, 0, e], start=True, stop=True)
                return m

            def chunk(i, ahead):
                pe.wait_ge(*ay_evac.at(img, 2 * i + 2))
                shift(ay1, 4, 5).then_inc(e_diff.sem, 1)
                pe.wait_ge(*h_set.at(img, i + 1))
                pe.wait_ge(*e_evac.at(img, i + 1))
                pe.sem_inc(passed, 1)
                for k in range(STEPS):
                    if k > 0:
                        pe.wait_ge(*h_ready.at(img, STEPS * i + k))
                    shift((hA, hB)[k % 2], 2, 3).then_inc(shifted.sem, 1)
                    if ahead and k < 4:
                        piece(i + 1, k)

            pe.wait_ge(*diag_made[2].at(img, 1))
            for n in range(4):
                piece(0, n)
            with pe.Fori(0, CH1 - 1) as i:
                chunk(i, True)
            chunk(CH1 - 1, False)

        def pe_attend2(pe, img):
            def score(u, s, nth):
                pe.wait_ge(*kq2_in[s].at(img, 144 * nth))
                pe.wait_ge(*logit2.at(img, u - 1))
                for i in range(2):
                    for a in range(2):
                        m = pe.matmul(bank[64 * i:64 * i + 64, s, 0:KEYS2], lhsT=q2g[:, s, i, a, :], rhs=k2g[:, s, i, :, a, :], start=a == 0, stop=a == 1)
                m.then_inc(scored2.sem, 1)

            def pair(u, v, ahead, nth_v):
                s = v % 2
                if ahead is not None:
                    score(u + 1, 1 - s, ahead)
                pe.wait_ge(*out2_evac.at(img, u - 1))
                for a in range(2):
                    for t in range(TAPS):
                        pe.matmul(bank[:, 4 + s, 2 * a * TOK2:2 * (a + 1) * TOK2], lhsT=diag[:, t, a, :],
                                  rhs=v2_view(a, (t // 3 - 1) * 8 + t % 3 - 1)[:, bass.ds(2 * u, 2), 0:S2, 0:S2], start=a == 0 and t == 0, stop=False)
                pe.wait_ge(*weighted2.at(img, u + 1))
                pe.wait_ge(*pt2_evac.at(img, u - 1))
                for c in range(2):
                    t = pe.transpose(bank[0:HK2, 2 + s, c * P:(c + 1) * P], w2p[:, s, c * HK2:(c + 1) * HK2], ident)
                t.then_inc(turned2.sem, 1)
                pe.wait_ge(*v2_in[v].at(img, 128 * nth_v))
                pe.wait_ge(*pt2_evac.at(img, u + 1))
                pe.sem_inc(passed, 1)
                for a in range(2):
                    for i in range(2):
                        for c in range(2):
                            m = pe.matmul(bank[:, 4 + s, (2 * a + i) * TOK2:(2 * a + i + 1) * TOK2], lhsT=v2g[0:HK2, v, i, c, a * P:(a + 1) * P],
                                          rhs=pt2[0:HK2, s, c, 64 * i:64 * i + TOK2], start=False, stop=(a, i, c) == (1, 1, 1))
                m.then_inc(pv2_done.sem, 1)

            pe.wait_ge(*diag_made[3].at(img, 1))
            pe.wait_ge(*v_padded[1].at(img, R2))
            pe.sem_inc(passed, 1)
            score(0, 0, 1)
            with pe.Fori(0, NP2 // VS - 1) as n:
                for v in range(VS):
                    pair(VS * n + v, v, 2 * n + (v + 1) // 2 + 1, n + 1)
            for v in range(VS):
                u = NP2 - VS + v
                pair(u, v, (u + 1) // 2 + 1 if v < VS - 1 else None, NP2 // VS)

        def pe_layer3(pe, img):
            def chunk(g, b, first=False):
                pe.wait_ge(*c3_added.at(img, 2 * g - 2))
                n = 0
                for k in range(3):
                    if first:
                        pe.wait_ge(*part_made[k].at(img, 2))
                        pe.sem_inc(passed, 1)
                    for t in range(TAPS):
                        for q in range(2):
                            for o in range(2):
                                m = pe.matmul(bank[:, b + o, 0:CHUNK], lhsT=w3s[:, t, q, o::2],
                                              rhs=parts[k][:, q, bass.ds(8 * g + t // 3, 8), t % 3:t % 3 + W], start=n == 0, stop=n == 6 * TAPS - 1)
                            n += 1
                m.then_inc(c3_mm.sem, 1)

            def turn(g, s):
                pe.wait_ge(*c3_added.at(img, 2 * g + 2))
                pe.sem_inc(passed, 1)
                for k2 in range(2):
                    pe.wait_ge(*y_evac.at(img, 2 * g + k2 - 3))
                    pe.sem_inc(passed, 1)
                    for k in range(2):
                        for q in range(2):
                            o = (2 * k2 + k) * TOK
                            t = pe.transpose(bank[0:TOK, 4 + 2 * s + k2, k * C + q * P:k * C + (q + 1) * P], ysum[:, s, q, o:o + TOK], ident)
                    t.then_inc(y_turned.sem, 1)

            chunk(0, 0, first=True)
            with pe.Fori(0, CHUNKS // 2) as i:
                chunk(2 * i + 1, 2)
                turn(2 * i, 0)
                chunk(2 * i + 2, 0)
                turn(2 * i + 1, 1)
            turn(CHUNKS - 1, 0)

        def act_gn(act, img, n):
            act.wait_ge(*gn_var.at(img, n + 1))
            act.activation(gm[:, 2:3], gm[:, 1:2], ACT.Sqrt).then_inc(gn_sqrt.sem, 1)
            act.wait_ge(*gn_coef.at(img, n + 1))
            act.activation(xnp[:, 1, 1:H + 1, 1:W + 1], res[:, 1, :].rearrange("p (y x) -> p y x", x=W), ACT.Identity,
                           bias=gm[:, 4:5], scale=gm[:, 3:4]).then_inc(xn_a.sem, 1)

        def act_project(act, img, l):
            R, T, n = RR[l], (TOK0, TOK2)[l], BLK[l]
            bias = (bias0, bias2)[l]

            def queries(i):
                for m in range(3):
                    kind, a = m // 2, m % 2
                    act.wait_ge(*qkv_mm[l].at(img, 6 * i + ORDER.index(m) + 1))
                    if m == 0:
                        act.wait_ge(*qk_out[l].at(img, 32 * i))
                    act.activation(qks[l][:, kind, :, a, :], bank[:, m, 0:n].rearrange("p (w t) -> p w t", w=R), ACT.Identity,
                                   bias=bias[:, kind, a:a + 1]).then_inc(qk_evac_a[l].sem, 1)

            def values(i):
                for u in range(4):
                    act.wait_ge(*v_turned[l].at(img, 4 * i + u + 1))
                    if u == 0:
                        act.wait_ge(*v_out[l].at(img, 16 * i))
                    w1 = min(2 * u + 2, R)
                    act.activation(vtk[0:T, 2 * u:w1], bank[0:T, 6 + u % 2, 0:(w1 - 2 * u) * C].rearrange("p (w c) -> p w c", c=C),
                                   ACT.Copy).then_inc(vtk_evac[l].sem, 1)

            queries(0)
            if l == 1:
                act.wait_ge(*hid_mm.at(img, 1))
                act.activation(hid[0:REG2, :], bank[0:REG2, 6, 256:256 + REG2], ACT.Relu, bias=wg2s[:, 2:3]).then_inc(hid_relu.sem, 1)
            values(0)
            if l == 1:
                act_gate(act, img)
            with act.Fori(1, R) as i:
                queries(i)
                values(i)

        def act_gate(act, img):
            act.wait_ge(*gate_neg.at(img, 1))
            act.activation(sig[0:REG2, 2:4], sig[0:REG2, 2:4], ACT.Exp).then_inc(gate_exp.sem, 1)
            act.wait_ge(*gate_one.at(img, 1))
            act.activation(sig[0:REG2, 2:4], sig[0:REG2, 2:4], ACT.Ln).then_inc(gate_ln.sem, 1)
            act.wait_ge(*dist_done.at(img, 1))
            act.activation(gauss[0:REG2, :], gauss[0:REG2, :], ACT.Exp, scale=-0.5, accum_out=gsum[0:REG2, 0:1]).then_inc(gauss_exp.sem, 1)

        def act_attend2(act, img):
            def exp(u, s):
                act.wait_ge(*logit2.at(img, u + 1))
                act.wait_ge(*weighted2.at(img, u - 1))
                act.activation(e2[:, s], lg2[:, s], ACT.Exp, bias=max2[:, s:s + 1], scale=SCALE2, accum_out=z2[:, s:s + 1]).then_inc(exped2.sem, 1)

            def pair(u, s, last=False):
                if not last:
                    exp(u + 1, 1 - s)
                act.wait_ge(*turned2.at(img, u + 1))
                act.activation(pt2[0:HK2, s], bank[0:HK2, 2 + s, 0:2 * P].rearrange("p (c n) -> p c n", c=2), ACT.Copy).then_inc(pt2_evac.sem, 1)
                act.wait_ge(*pv2_done.at(img, u + 1))
                for a in range(2):
                    m = act.activation(att[:, a, bass.ds(u * HK2, HK2)], bank[:, 4 + s, 2 * a * TOK2:2 * (a + 1) * TOK2], ACT.Identity,
                                       bias=dw2_b[:, a:a + 1])
                m.then_inc(out2_evac.sem, 1)

            act.wait_ge(*v_padded[1].at(img, R2))
            act.wait_ge(*qk_out[1].at(img, 32 * R2))
            act.wait_ge(*v_out[1].at(img, 16 * R2))
            exp(0, 0)
            with act.Fori(0, NP2 // 2 - 1) as n:
                pair(2 * n, 0)
                pair(2 * n + 1, 1)
            pair(NP2 - 2, 0)
            pair(NP2 - 1, 1, last=True)

        def act_layer3(act, img):
            for q in range(2):
                act.activation(parts[0][:, q], xnp[:, q], ACT.Copy).then_inc(part_made[0].sem, 1)
            for q in range(2):
                act.wait_ge(*rest_made.at(img, q + 1))
                act.activation(parts[1][:, q], xnp[:, q], ACT.Copy).then_inc(part_made[1].sem, 1)

        def act_attend0(act, img):
            def copy(r, s, j):
                act.wait_ge(*scored.at(img, r * TILES + j + 1))
                act.activation(sc_sb[:, s, j, :], bank[:, j, 0:KEYS0], ACT.Copy, scale=SCALE0).then_inc(s_copied.sem, 1)

            def exps(r, s, j):
                act.wait_ge(*topped.at(img, r * TILES + j + 1))
                act.wait_ge(*p_turned.at(img, r * TILES + j - 3))
                act.activation(ebest[:, j], best[:, s, j, :], ACT.Exp, bias=nmax[:, s, j:j + 1], accum_out=zsum[:, s, j:j + 1])
                act.activation(er[:, j, :], rem[:, j, :], ACT.Exp, bias=nmax[:, s, j:j + 1])
                act.activation(ee[:, j, :], sc_sb[:, s, j, :], ACT.Exp, bias=nmax[:, s, j:j + 1]).then_inc(exped.sem, 1)

            def evac(r, j):
                act.wait_ge(*p_turned.at(img, r * TILES + j + 1))
                act.activation(pt[:, j % 2], bank[:, 4, 0:2 * P].rearrange("p (c n) -> p c n", c=2), ACT.Copy).then_inc(pt_evac.sem, 1)

            def out_evac(r):
                act.wait_ge(*o_turned.at(img, r + 1))
                act.activation(att[:, :, bass.ds(r * TOK0, TOK0)], bank[:, 4, 2 * P:3 * P].rearrange("p (a t) -> p a t", a=2), ACT.Copy).then_inc(o_evac.sem, 1)

            def evac_lepe(row, a):
                act.wait_ge(*lepe_mm.at(img, 2 * row + a + 1))
                act.activation(att[:, a, bass.ds(row * BLK[0], BLK[0])], bank[:, 7, 0:BLK[0]], ACT.Identity, bias=lepe_b[:, a:a + 1]).then_inc(lepe_evac.sem, 1)

            def region(r, s, first=False, second=False, last=False):
                if not first:
                    evac(r - 1, TILES - 1)
                if not first and not second:
                    out_evac(r - 2)
                for j in range(TILES):
                    exps(r, s, j)
                    if j > 0:
                        evac(r, j - 1)
                    if not last and j % 2 == 1:
                        copy(r + 1, 1 - s, j - 1)
                        copy(r + 1, 1 - s, j)

            act.wait_ge(*v_padded[0].at(img, R0))
            act.wait_ge(*qk_out[0].at(img, 32 * R0))
            act.wait_ge(*v_out[0].at(img, 16 * R0))
            evac_lepe(0, 0)
            for j in range(TILES):
                copy(0, 0, j)
            evac_lepe(0, 1)
            region(0, 0, first=True)
            evac_lepe(1, 0)

            def lap(i, first=False, last=False):
                for n in range(1, 2 * VS + 1):
                    region(2 * VS * i + n, n % 2, second=first and n == 1, last=last and n == 2 * VS)
                    if n == max(SECOND_HALF):
                        evac_lepe(i + 1, 1)
                    if n == max(FIRST_HALF) and not last:
                        evac_lepe(i + 2, 0)
            lap(0, first=True)
            with act.Fori(1, LAPS - 1) as i:
                lap(i)
            lap(LAPS - 1, last=True)
            evac(REG0 - 1, TILES - 1)
            out_evac(REG0 - 2)
            out_evac(REG0 - 1)

        def act_output(act, img, l):
            R, n = RR[l], BLK[l]
            b = (out0_b, proj_b)[l]
            with act.Fori(0, R) as i:
                for q in range(2):
                    act.wait_ge(*om_mm[l].at(img, 2 * i + q + 1))
                    act.wait_ge(*om_added[l].at(img, 2 * i + q - 1))
                    act.activation(otmp[:, 0, q, 0:n], bank[:, 2 + q, 0:n], ACT.Identity, bias=b[:, q:q + 1]).then_inc(om_evac[l].sem, 1)

        def act_layer1(act, img):
            for q in range(2):
                m = act.activation(VP0[:, q, 1:H + 1, 1:W + 1], res[:, q, :].rearrange("p (y x) -> p y x", x=W), ACT.Identity,
                                   bias=gm[:, 4:5], scale=gm[:, 3:4])
            m.then_inc(mirror_in.sem, 1)

            def evac_conv(i, which):
                mm, out_, done = ((g_mm, ax1, ax_evac), (g1_mm, ay1, ay_evac))[which]
                for q in range(2):
                    act.wait_ge(*mm.at(img, 2 * i + q + 1))
                    act.activation(out_[:, q].rearrange("p (h n) -> p h n", h=2), bank[:, 2 * q:2 * q + 2, 0:E1 // 2], ACT.Relu,
                                   bias=bnc[:, which, q, 1:2], scale=bnc[:, which, q, 0:1]).then_inc(done.sem, 1)

            def rows(i):
                return xnp[:, :, bass.ds(i * ROWS1 + 1, ROWS1), 1:W + 1]

            def finish(i):
                act.wait_ge(*h_ready.at(img, STEPS * i + STEPS))
                for q in range(2):
                    m = act.activation(acc[:, q], hB[:, q], ACT.Relu, bias=bnc[:, 2, q, 1:2], scale=bnc[:, 2, q, 0:1])
                m.then_inc(y1_ready.sem, 1)

            def chunk(i, first=False, last=False):
                if not first:
                    finish(i - 1)
                    evac_conv(i, 1)
                for n, (src, dst) in enumerate(((prod, cpx), (cmy, cpy))):
                    act.wait_ge(*sobel_done.at(img, 2 * i + n + 1))
                    act.activation(dst, src, ACT.Square, scale=0.5).then_inc(squared.sem, 1)
                if first:
                    evac_conv(i, 1)
                act.wait_ge(*e_diff.at(img, i + 1))
                for q in range(2):
                    m = act.activation(hB[:, q].rearrange("p (h n) -> p h n", h=2), bank[:, 4 + 2 * q:6 + 2 * q, 0:E1 // 2], ACT.Copy, scale=-1.0)
                m.then_inc(e_evac.sem, 1)
                act.activation(hA.rearrange("p q (y x) -> p q y x", x=W), rows(i), ACT.Copy)
                act.wait_ge(*e_added.at(img, i + 1))
                act.sem_inc(passed, 1)
                act.activation(hB.rearrange("p q (y x) -> p q y x", x=W), rows(i), ACT.Copy).then_inc(h_set.sem, 1)
                act.wait_ge(*r_made.at(img, i + 1))
                act.activation(acc, cE, ACT.Copy, scale=2 * DT).then_inc(r_scaled.sem, 1)
                act.wait_ge(*d_made.at(img, i + 1))
                act.activation(c0, prod, ACT.Copy, scale=2.0, bias=-1.0)
                act.wait_ge(*e_scaled.at(img, i + 1))
                act.activation(cF, prod, ACT.Copy, scale=2 * DT).then_inc(d_scaled.sem, 1)
                act.wait_ge(*coef_done.at(img, i + 1))
                if not last:
                    evac_conv(i + 1, 0)

            evac_conv(0, 0)
            chunk(0, first=True)
            with act.Fori(1, CH1 - 1) as i:
                chunk(i)
            chunk(CH1 - 1, last=True)
            finish(CH1 - 1)

        def act_store(act, img):
            def rows(g, s):
                act.wait_ge(*y_out[s].at(img, 16 * (g // 2)))
                for k2 in range(2):
                    act.wait_ge(*y_turned.at(img, 2 * g + k2 + 1))
                    act.activation(tok[0:TOK, s, 2 * k2:2 * k2 + 2].rearrange("p k (c q) -> p k q c", q=2),
                                   bank[0:TOK, 4 + 2 * s + k2, :].rearrange("p (k q c) -> p k q c", k=2, q=2), ACT.Copy).then_inc(y_evac.sem, 1)
            with act.Fori(0, CHUNKS // 2) as i:
                rows(2 * i, 0)
                rows(2 * i + 1, 1)
            rows(CHUNKS - 1, 0)

        def dve_gn(dve, img, n, eps, pieces=None):
            if pieces is None:
                pieces = CHUNKS
                for q in range(2):
                    for g in range(CHUNKS):
                        dve.bn_stats(stats[:, q, g, :], res[:, q, g * CHUNK:(g + 1) * CHUNK])
            dve.drain()
            for q in range(2):
                dve.bn_aggr(mv[:, q, :], stats[:, q, 0:pieces].rearrange("p g s -> p (g s)"))
            dve.drain()
            dve.tensor_copy(ms[:, :, 0], mv[:, :, 0])
            dve.tensor_tensor(ms[:, :, 1], mv[:, :, 0], mv[:, :, 0], ALU.mult)
            dve.drain()
            dve.tensor_tensor(ms[:, :, 1], ms[:, :, 1], mv[:, :, 1], ALU.add)
            dve.drain().then_inc(gn_ms.sem, 1)
            dve.wait_ge(*gn_grp.at(img, n + 1))
            dve.tensor_copy(grp[:, :, :], bank[:, 7, 0:4].rearrange("p (q s) -> p q s", q=2))
            dve.drain()
            dve.tensor_tensor(gm[:, 0:2], grp[:, 0, :], grp[:, 1, :], ALU.add)
            dve.drain()
            dve.tensor_tensor(gm[:, 5:6], gm[:, 0:1], gm[:, 0:1], ALU.mult)
            dve.drain()
            dve.tensor_tensor(gm[:, 1:2], gm[:, 1:2], gm[:, 5:6], ALU.subtract)
            dve.drain()
            dve.tensor_scalar(gm[:, 1:2], gm[:, 1:2], 0.0, eps, ALU.max, ALU.add)
            dve.drain().then_inc(gn_var.sem, 1)
            dve.wait_ge(*gn_sqrt.at(img, n + 1))
            dve.reciprocal(gm[:, 3:4], gm[:, 2:3])
            dve.drain()
            dve.tensor_scalar(gm[:, 4:5], gm[:, 0:1], gm[:, 3:4], -1.0, ALU.mult, ALU.mult)
            dve.drain().then_inc(gn_coef.sem, 1)
            dve.tensor_scalar(xnp[:, 0, 1:H + 1, 1:W + 1], res[:, 0, :].rearrange("p (y x) -> p y x", x=W),
                              gm[:, 3:4], gm[:, 4:5], ALU.mult, ALU.add).then_inc(xn_v.sem, 1)
            dve.wait_ge(*xn_v.at(img, n + 1))
            dve.wait_ge(*xn_a.at(img, n + 1))
            dve.sem_inc(passed, 1)

        def dve_diag(dve, k, w, dst=None):
            d = diag if dst is None else dst
            for t in range(TAPS):
                for a in range(2):
                    dve.tensor_scalar(d[:, t, a, :], ident, w[:, a, t:t + 1], None, ALU.mult)
            dve.drain().then_inc(diag_made[k].sem, 1)

        def dve_project(dve, img, l):
            R, T, n, s = RR[l], (TOK0, TOK2)[l], BLK[l], SS[l]
            for q in range(2):
                dve.tensor_reduce(pool_a[l][:, q], xnp[:, q, 1:H + 1, 1:W + 1].rearrange("p y (w x) -> p y w x", x=s), AX.X, ALU.add)
            dve.drain()
            pa, pm = pool_a[l], pool_m[l]
            for q in range(2):
                dve.tensor_reduce(pm[:, q].rearrange("p (v w) -> p v w", v=R), pa[:, q].rearrange("p (v y) w -> p v w y", y=s), AX.X, ALU.add)
            dve.drain()
            dve.tensor_scalar(pm, pm, 1.0 / (s * s), None, ALU.mult)
            dve.drain().then_inc(pooled[l].sem, 1)
            bias = (bias0, bias2)[l]

            def evacuate(i):
                for m in VECTOR:
                    kind, a = m // 2, m % 2
                    dve.wait_ge(*qkv_mm[l].at(img, 6 * i + ORDER.index(m) + 1))
                    if kind == 1:
                        dve.wait_ge(*qk_out[l].at(img, 32 * i))
                        dst = qks[l][:, 1, :, a, :]
                    else:
                        if m == 4:
                            dve.wait_ge(*v_padded[l].at(img, i))
                            dve.wait_ge(*v_turned[l].at(img, 4 * i))
                        dst = vrow[:, a, 0:n].rearrange("p (w t) -> p w t", w=R)
                    dve.tensor_scalar(dst, bank[:, m, 0:n].rearrange("p (w t) -> p w t", w=R), bias[:, kind, a:a + 1], None, ALU.add).then_inc(qkv_evac_v[l].sem, 1)

            evacuate(0)
            dve.wait_ge(*qkr_mm[l].at(img, 1))
            for kind in range(2):
                for a in range(2):
                    o = (2 * kind + a) * 64
                    dve.tensor_scalar(qkr[l][:, kind, a], bank[:, 6, o:o + R * R], bias[:, kind, a:a + 1], None, ALU.add)
            dve.drain().then_inc(qkr_evac[l].sem, 1)
            dve.wait_ge(*aff_mm[l].at(img, 1))
            dve.tensor_scalar(aff[0:R * R, 0:R * R], bank[0:R * R, 7, 0:R * R], (1.0, SCALE2)[l], None, ALU.mult)
            dve.drain()
            dve.max(v8[0:R * R], aff[0:R * R, 0:R * R])
            dve.drain()
            dve.max_index(i8[0:R * R], v8[0:R * R], aff[0:R * R, 0:R * R])
            dve.drain().then_inc(idx_found[l].sem, 1)
            if l == 1:
                dve_gate(dve, img)
            dve_diag(dve, *((0, lepe_w), (3, dw2_w))[l])
            with dve.Fori(1, R) as i:
                evacuate(i)

        def dve_gate(dve, img):
            g = sig[0:REG2]
            dve.wait_ge(*gate_mm.at(img, 1))
            dve.tensor_copy(g[:, 0:2], bank[0:REG2, 6, 320:322])
            dve.drain()
            dve.scalar_tensor_tensor(g[:, 2:4], g[:, 0:2], -1.0, g[:, 0:2], ALU.mult, ALU.min)
            dve.drain().then_inc(gate_neg.sem, 1)
            dve.wait_ge(*gate_exp.at(img, 1))
            dve.tensor_scalar(g[:, 2:4], g[:, 2:4], 1.0, None, ALU.add)
            dve.drain().then_inc(gate_one.sem, 1)
            dve.wait_ge(*gate_ln.at(img, 1))
            dve.scalar_tensor_tensor(g[:, 0:2], g[:, 0:2], 0.0, g[:, 2:4], ALU.max, ALU.add)
            dve.drain()
            dve.tensor_scalar(g[:, 0:2], g[:, 0:2], 0.5, None, ALU.add)
            dve.drain()
            dve.tensor_tensor(g[:, 2:4], g[:, 0:2], g[:, 0:2], ALU.mult)
            dve.drain()
            dve.reciprocal(g[:, 4:6], g[:, 2:4])
            dve.drain()
            dve.tensor_scalar(gauss[0:REG2, :], posd_s[:, 0], g[:, 4:5], None, ALU.mult)
            dve.drain()
            dve.scalar_tensor_tensor(gauss[0:REG2, :], posd_s[:, 1], g[:, 5:6], gauss[0:REG2, :], ALU.mult, ALU.add)
            dve.tensor_copy(idx_f[0:REG2, 0:TOPK], i8[0:REG2, 0:TOPK])
            dve.drain().then_inc(dist_done.sem, 1)
            dve.wait_ge(*gauss_exp.at(img, 1))
            dve.tensor_scalar(gsum[0:REG2, 0:1], gsum[0:REG2, 0:1], 1e-6, None, ALU.add)
            dve.drain()
            dve.reciprocal(gsum[0:REG2, 1:2], gsum[0:REG2, 0:1])
            dve.drain()
            dve.tensor_scalar(gauss[0:REG2, :], gauss[0:REG2, :], gsum[0:REG2, 1:2], None, ALU.mult)
            dve.drain()
            for t in range(TOPK):
                dve.scalar_tensor_tensor(hid[0:REG2, :], posd_s[:, 2], idx_f[0:REG2, t:t + 1], gauss[0:REG2, :], ALU.is_equal, ALU.mult,
                                         accum_out=gwt[0:REG2, t:t + 1])
                dve.drain()
            dve.memset(q2g_flat, 0.0)
            dve.drain().then_inc(q2_zeroed.sem, 1)
            dve.drain().then_inc(gwt_done.sem, 1)

        def dve_attend2(dve, img):
            def gw(u):
                return gws[:, bass.ds(u, 1), :].rearrange("p u t -> p (u t)").unsqueeze(2).to_broadcast([P, TOPK, TOK2])

            v3 = lambda a: a.rearrange("p (t n) -> p t n", t=TOPK)

            def logits(u, s):
                dve.wait_ge(*scored2.at(img, u + 1))
                dve.wait_ge(*exped2.at(img, u - 1))
                dve.tensor_tensor(v3(lg2[:, s]), v3(bank[:, s, 0:KEYS2]), gw(u), ALU.mult)
                dve.drain()
                dve.reduce_max(max2[:, s:s + 1], lg2[:, s], AX.X)
                dve.drain()
                dve.tensor_scalar(max2[:, s:s + 1], max2[:, s:s + 1], -SCALE2, None, ALU.mult).then_inc(logit2.sem, 1)

            def weights(u, s):
                dve.wait_ge(*exped2.at(img, u + 1))
                dve.reciprocal(rz2[:, s:s + 1], z2[:, s:s + 1])
                dve.drain()
                dve.wait_ge(*turned2.at(img, u - 1))
                dve.scalar_tensor_tensor(v3(w2p[:, s]), v3(e2[:, s]), rz2[:, s:s + 1], gw(u), ALU.mult, ALU.mult).then_inc(weighted2.sem, 1)

            dve.wait_ge(*v_padded[1].at(img, R2))
            dve.wait_ge(*qk_out[1].at(img, 32 * R2))
            dve.wait_ge(*v_out[1].at(img, 16 * R2))
            dve.wait_ge(*gw_in.at(img, 32))
            logits(0, 0)
            with dve.Fori(0, NP2 // 2 - 1) as n:
                logits(2 * n + 1, 1)
                weights(2 * n, 0)
                logits(2 * n + 2, 0)
                weights(2 * n + 1, 1)
            logits(NP2 - 1, 1)
            weights(NP2 - 2, 0)
            weights(NP2 - 1, 1)

        def dve_layer3(dve, img):
            for q in range(2):
                dve.wait_ge(*part_made[0].at(img, q + 1))
                dve.tensor_tensor(xnp[:, q], xnp[:, q], parts[0][:, q], ALU.subtract)
                dve.drain().then_inc(rest_made.sem, 1)
            for q in range(2):
                dve.wait_ge(*part_made[1].at(img, q + 1))
                dve.tensor_tensor(parts[2][:, q], xnp[:, q], parts[1][:, q], ALU.subtract)
                dve.drain().then_inc(part_made[2].sem, 1)

            def chunk(g, b):
                dve.wait_ge(*y_turned.at(img, 2 * g - 2))
                dve.wait_ge(*c3_mm.at(img, g + 1))
                for o in range(2):
                    dve.tensor_tensor(ysum[:, b // 2, o], res[:, o, bass.ds(g * CHUNK, CHUNK)], bank[:, b + o, 0:CHUNK], ALU.add).then_inc(c3_added.sem, 1)

            with dve.Fori(0, CHUNKS // 2) as i:
                chunk(2 * i, 0)
                chunk(2 * i + 1, 2)
            chunk(CHUNKS - 1, 0)
            dve.drain().then_inc(res_done.sem, 1)

        def dve_attend0(dve, img):
            def pair(r, s, h):
                j0 = 2 * h
                dve.wait_ge(*s_copied.at(img, r * TILES + j0 + 2))
                dve.wait_ge(*exped.at(img, (r - 1) * TILES + j0 + 2))
                dve.sem_inc(passed, 1)
                n = 0
                for k in range(4):
                    for j in (j0, j0 + 1):
                        src = sc_sb[:, s, j] if k == 0 else rem[:, j]
                        if k > 0:
                            dve.wait_ge(topk_step, n - 1)
                        dve.max(best[:, s, j, 8 * k:8 * k + 8], src).then_inc(topk_step, 1)
                        n += 1
                    for j in (j0, j0 + 1):
                        src = sc_sb[:, s, j] if k == 0 else rem[:, j]
                        dve.wait_ge(topk_step, n - 1)
                        ins = dve.match_replace(rem[:, j], best[:, s, j, 8 * k:8 * k + 8], src, REMOVED)
                        ins.then_inc(topk_step, 1)
                        n += 1
                dve.tensor_scalar(nmax[:, s, j0:j0 + 2], best[:, s, j0:j0 + 2, 0], -1.0, None, ALU.mult).then_inc(topped.sem, 2)
                dve.wait_ge(topk_step, n)
                dve.sem_clear(topk_step)

            def norm(r, s):
                dve.wait_ge(*exped.at(img, (r + 1) * TILES))
                dve.reciprocal(rz[:, s], zsum[:, s])
                dve.drain()
                dve.wait_ge(*pv_done.at(img, r + 1))
                dve.wait_ge(*o_turned.at(img, r))
                dve.tensor_tensor(osb[:, :, :], bank[:, 5 + s, 0:P].rearrange("p (j d) -> p j d", j=TILES),
                                  rz[:, s].unsqueeze(2).to_broadcast([P, TILES, HD]), ALU.mult).then_inc(o_norm.sem, 1)

            def region(r, s, first=False):
                pair(r, s, 0)
                pair(r, s, 1)
                if not first:
                    norm(r - 1, 1 - s)

            dve.wait_ge(*v_padded[0].at(img, R0))
            dve.wait_ge(*qk_out[0].at(img, 32 * R0))
            dve.wait_ge(*v_out[0].at(img, 16 * R0))
            region(0, 0, first=True)
            with dve.Fori(0, 24) as i:
                region(2 * i + 1, 1)
                region(2 * i + 2, 0)
            norm(48, 0)

        def dve_output(dve, img, l):
            R, n, s = RR[l], BLK[l], SS[l]
            with dve.Fori(0, R) as i:
                for q in range(2):
                    dve.wait_ge(*om_evac[l].at(img, 2 * i + q + 1))
                    v = region_view(res[:, q, :].rearrange("p (y x) -> p y x", x=W), l, i)
                    dve.tensor_tensor(v, v, otmp[:, 0, q, 0:n].rearrange("p (w y x) -> p w y x", w=R, y=s), ALU.add).then_inc(om_added[l].sem, 1)
                    dve.drain()
                    dve.bn_stats(stats[:, q, bass.ds(i, 1), :].rearrange("p o s -> p (o s)"), res[:, q, bass.ds(i * n, n)])
            dve.drain().then_inc(res_done.sem, 1)

        def tt(eng, out_, a, b, op):
            eng.tensor_tensor(out_, a, b, op)
            eng.drain()

        def dve_bn(dve):
            dve.tensor_scalar(bns[:, :, 3:12:4], bns[:, :, 3:12:4], BN_EPS, None, ALU.add)
            dve.drain().then_inc(bn_var.sem, 1)
            dve.wait_ge(bn_sqrt.sem, 1)
            dve.reciprocal(bns[:, :, 3:12:4], bns[:, :, 3:12:4])
            dve.drain()
            for n in range(3):
                k = 4 * n
                tt(dve, bnc[:, n, :, 0:1], bns[:, :, k:k + 1], bns[:, :, k + 3:k + 4], ALU.mult)
                tt(dve, bnc[:, n, :, 1:2], bns[:, :, k + 2:k + 3], bnc[:, n, :, 0:1], ALU.mult)
                tt(dve, bnc[:, n, :, 1:2], bns[:, :, k + 1:k + 2], bnc[:, n, :, 1:2], ALU.subtract)
                if n < 2:
                    dve.tensor_scalar(bnc[:, n], bnc[:, n], DT, None, ALU.mult)
                    dve.drain()
            dve.drain().then_inc(bn_ready.sem, 1)

        def dve_layer1(dve, img):
            def rolled(op, out_, coef, h, by):
                o, c, v = (a.rearrange("p q (y x) -> p (q y) x", x=W) for a in (out_, coef, h))
                if by > 0:
                    dve.tensor_tensor(o[:, :, 1:W], c[:, :, 1:W], v[:, :, 0:W - 1], op)
                    dve.tensor_tensor(o[:, :, 0:1], c[:, :, 0:1], v[:, :, W - 1:W], op)
                else:
                    dve.tensor_tensor(o[:, :, 0:W - 1], c[:, :, 0:W - 1], v[:, :, 1:W], op)
                    dve.tensor_tensor(o[:, :, W - 1:W], c[:, :, W - 1:W], v[:, :, 0:1], op)
                dve.drain()

            def banks(b):
                return bank[:, b:b + 2, 0:E1 // 2]

            def halves(a):
                return a.rearrange("p (h n) -> p h n", h=2)

            def stt(out_, a, scalar, b, op0, op1):
                dve.scalar_tensor_tensor(out_, a, scalar, b, op0, op1)
                dve.drain()

            def sobel(i):
                y0 = i * ROWS1
                tt(dve, diff_x, VP0[:, :, bass.ds(y0, ROWS1 + 2), 2:W + 2], VP0[:, :, bass.ds(y0, ROWS1 + 2), 0:W], ALU.subtract)
                d = [diff_x[:, :, k:k + ROWS1].rearrange("p q y x -> p q (y x)") for k in range(3)]
                stt(prod, d[1], 2.0, d[0], ALU.mult, ALU.add)
                dve.tensor_tensor(prod, prod, d[2], ALU.add).then_inc(sobel_done.sem, 1)
                dve.wait_ge(*gy_begun.at(img, i + 1))
                dve.scalar_tensor_tensor(cmy.rearrange("p q (y x) -> p (q y) x", x=W), diff_y.rearrange("p q y x -> p (q y) x")[:, :, 1:W + 1], 2.0,
                                         cF.rearrange("p q (y x) -> p (q y) x", x=W), ALU.mult, ALU.add).then_inc(sobel_done.sem, 1)

            def join(i):
                dve.wait_ge(*y1_ready.at(img, i + 1))
                r = res[:, :, bass.ds(i * E1, E1)]
                dve.tensor_tensor(r, r, acc, ALU.add)

            def coefficients(i, first=False):
                sobel(i)
                if not first:
                    join(i - 1)
                    dve.drain()
                dve.wait_ge(*squared.at(img, 2 * i + 2))
                dve.tensor_tensor(cmx, cpx, cpy, ALU.mult)
                dve.tensor_tensor(cmy, cpx, cpy, ALU.add)
                dve.drain().then_inc(s_made.sem, 1)
                stt(acc, cmy, 1.0 + 2 * DT, cmx, ALU.mult, ALU.add)
                dve.tensor_scalar(acc, acc, 1.0 + 4 * DT, None, ALU.add)
                dve.drain()
                dve.reciprocal(cE, acc)
                dve.drain().then_inc(r_made.sem, 1)
                dve.wait_ge(*n_made.at(img, i + 1))
                stt(prod, prod, 1.0, cE, ALU.add, ALU.mult)
                dve.drain().then_inc(d_made.sem, 1)
                dve.wait_ge(*r_scaled.at(img, i + 1))
                stt(cpx, cpx, 1.0, acc, ALU.add, ALU.mult)
                stt(cpy, cpy, 1.0, acc, ALU.add, ALU.mult)
                dve.wait_ge(*ax_evac.at(img, 2 * i + 2))
                tt(dve, cmy, ax1, prod, ALU.mult)
                tt(dve, cmx, cpx, cmy, ALU.subtract)
                tt(dve, cpx, cpx, cmy, ALU.add)
                dve.wait_ge(*ay_scaled.at(img, i + 1))
                tt(dve, cmy, cpy, ay1, ALU.subtract)
                tt(dve, cpy, cpy, ay1, ALU.add)
                dve.drain().then_inc(coef_done.sem, 1)
                dve.wait_ge(*e_scaled.at(img, i + 1))
                dve.wait_ge(*d_scaled.at(img, i + 1))

            def chunk(i, first=False):
                coefficients(i, first)
                dve.wait_ge(*h_set.at(img, i + 1))
                for k in range(STEPS):
                    h, hn = (hA, hB) if k % 2 == 0 else (hB, hA)
                    rolled(ALU.mult, acc, cmx, h, 1)
                    rolled(ALU.mult, prod, cpx, h, -1)
                    tt(dve, acc, acc, prod, ALU.add)
                    dve.wait_ge(*shifted.at(img, STEPS * i + k + 1))
                    dve.tensor_tensor(halves(prod[:, 0]), halves(cmy[:, 0]), banks(4), ALU.mult)
                    dve.tensor_tensor(prod[:, 1], cmy[:, 1], h[:, 0], ALU.mult)
                    dve.drain()
                    tt(dve, acc, acc, prod, ALU.add)
                    dve.tensor_tensor(prod[:, 0], cpy[:, 0], h[:, 1], ALU.mult)
                    dve.tensor_tensor(halves(prod[:, 1]), halves(cpy[:, 1]), banks(6), ALU.mult)
                    dve.drain()
                    tt(dve, acc, acc, prod, ALU.add)
                    dve.wait_ge(*own_part.at(img, STEPS * i + k + 1))
                    tt(dve, hn, hn, acc, ALU.add)
                    dve.drain().then_inc(h_ready.sem, 1)

            chunk(0, first=True)
            with dve.Fori(1, CH1) as i:
                chunk(i)
            join(CH1 - 1)
            dve.drain().then_inc(res_done.sem, 1)

        def pool_project(pool, img, l):
            R, n = RR[l], BLK[l]
            with pool.Fori(0, R) as i:
                pool.wait_ge(*qkv_evac_v[l].at(img, 3 * i + 2))
                for a in range(2):
                    if l == 0:
                        dst = region_view(VP0[:, a, 1:H + 1, 1:W + 1], 0, i)
                        src = vrow[:, a, 0:n].rearrange("p (w y x) -> p w y x", w=R, y=S0)
                    else:
                        dst = v2_view(a, 0)[:, bass.ds(i * R2, R2), 0:S2, 0:S2]
                        src = vrow[:, a, 0:n].rearrange("p (w y x) -> p w y x", w=R, y=S2)
                    pool.tensor_copy(dst, src)
                pool.drain().then_inc(v_padded[l].sem, 1)

        def pool_attend0(pool, img):
            with pool.Fori(0, REG0) as r:
                for j in range(TILES):
                    pool.wait_ge(*exped.at(img, r * TILES + j + 1))
                    pool.tensor_tensor(ee[:, j, :], ee[:, j, :], er[:, j, :], ALU.subtract).then_inc(kept.sem, 1)

        def pool_layer1(pool, img):
            pool.wait_ge(*mirror_in.at(img, 1))
            pool.sem_inc(passed, 1)
            for to, of in ((0, 2), (H + 1, H - 1)):
                pool.tensor_copy(VP0[:, :, to, 1:W + 1], VP0[:, :, of, 1:W + 1])
            pool.drain()
            for to, of in ((0, 2), (W + 1, W - 1)):
                pool.tensor_copy(VP0[:, :, :, to], VP0[:, :, :, of])
            pool.drain().then_inc(mirrored.sem, 1)
            with pool.Fori(0, CH1) as i:
                y0 = i * ROWS1
                tt(pool, diff_y, VP0[:, :, bass.ds(y0 + 2, ROWS1)], VP0[:, :, bass.ds(y0, ROWS1)], ALU.subtract)
                pool.tensor_tensor(cF.rearrange("p q (y x) -> p q y x", x=W), diff_y[:, :, :, 0:W], diff_y[:, :, :, 2:W + 2], ALU.add)
                pool.drain().then_inc(gy_begun.sem, 1)
                pool.wait_ge(*sobel_done.at(img, 2 * i + 2))
                pool.wait_ge(*ax_evac.at(img, 2 * i + 2))
                o, v = (a.rearrange("p q (y x) -> p (q y) x", x=W) for a in (cF, ax1))
                pool.tensor_tensor(o[:, :, 1:W - 1], v[:, :, 2:W], v[:, :, 0:W - 2], ALU.subtract)
                pool.tensor_tensor(o[:, :, 0:1], v[:, :, 1:2], v[:, :, W - 1:W], ALU.subtract)
                pool.tensor_tensor(o[:, :, W - 1:W], v[:, :, 0:1], v[:, :, W - 2:W - 1], ALU.subtract)
                pool.drain()
                pool.wait_ge(*e_evac.at(img, i + 1))
                pool.tensor_tensor(cF, cF, hB, ALU.add)
                pool.drain().then_inc(e_added.sem, 1)
                pool.wait_ge(*s_made.at(img, i + 1))
                pool.tensor_tensor(prod, cmx, cmy, ALU.add)
                pool.drain().then_inc(n_made.sem, 1)
                pool.wait_ge(*d_made.at(img, i + 1))
                pool.tensor_tensor(ay1, ay1, prod, ALU.mult)
                pool.drain().then_inc(ay_scaled.sem, 1)
                pool.wait_ge(*r_scaled.at(img, i + 1))
                pool.tensor_tensor(cE, cF, prod, ALU.mult)
                pool.drain().then_inc(e_scaled.sem, 1)
                pool.wait_ge(*d_scaled.at(img, i + 1))
                pool.tensor_tensor(cF.rearrange("p q (y x) -> p q y x", x=W), cF.rearrange("p q (y x) -> p q y x", x=W),
                                   xnp[:, :, bass.ds(y0 + 1, ROWS1), 1:W + 1], ALU.mult)
                pool.drain()
                pool.wait_ge(*coef_done.at(img, i + 1))
                pool.wait_ge(*h_set.at(img, i + 1))
                for k in range(STEPS):
                    h, hn = (hA, hB) if k % 2 == 0 else (hB, hA)
                    if k > 0:
                        pool.wait_ge(*h_ready.at(img, STEPS * i + k))
                    pool.tensor_tensor(ay1, cE, h, ALU.mult)
                    if k > 0:
                        pool.wait_ge(*shifted.at(img, STEPS * i + k))
                    tt(pool, hn, hn, c0, ALU.mult)
                    tt(pool, hn, hn, cF, ALU.add)
                    pool.tensor_tensor(hn, hn, ay1, ALU.add)
                    pool.drain().then_inc(own_part.sem, 1)

        @block.sync
        def _(sp):
            def const(dst, src):
                sp.dma_start(dst, src).then_inc(const_in.sem, 16)
            const(mat[:, :, :], mats)
            for kind in range(3):
                for a in range(2):
                    for j in range(4):
                        o = kind * C + 64 * j + 32 * a
                        sp.dma_start(w0raw[32 * j:32 * j + 32, 2 * kind + a, :], w0_qkv[o:o + 32, :]).then_inc(wraw_in.sem, 16)
                        sp.dma_start(bias0[32 * j:32 * j + 32, kind, a:a + 1], b0_qkv[o:o + 32].rearrange("(p o) -> p o", o=1)).then_inc(wraw_in.sem, 16)
            for q in range(2):
                for a in range(2):
                    sp.dma_start(o0raw[:, q, a * P:(a + 1) * P].rearrange("p (j d) -> p j d", j=4),
                                 w0_out.rearrange("(p q) (j a d) -> p q a j d", q=2, j=4, a=2)[:, q, a]).then_inc(wraw_in.sem, 16)
            for a in range(2):
                for j in range(4):
                    o = 64 * j + 32 * a
                    sp.dma_start(lepe_w[32 * j:32 * j + 32, a, :], w0_lepe[o:o + 32].rearrange("c i y x -> c (i y x)")).then_inc(wraw_in.sem, 16)
                    sp.dma_start(small[32 * j:32 * j + 32, a:a + 1], b0_lepe[o:o + 32].rearrange("(p o) -> p o", o=1)).then_inc(wraw_in.sem, 16)
            sp.dma_start(small[:, 2:4], b0_out.rearrange("(p q) -> p q", q=2)).then_inc(wraw_in.sem, 16)

            sp.dma_start(w2s[:, :, :], w2_qkv.rearrange("(p q) o -> p q o", q=2)).then_inc(const_in.sem, 16)
            sp.dma_start(p2s[:, :, :], w2_proj.rearrange("(a p) o -> p a o", a=2)).then_inc(const_in.sem, 16)
            sp.dma_start(wg1s[:, :, :], w2_g1.rearrange("(a p) h -> p a h", a=2)).then_inc(const_in.sem, 16)
            sp.dma_start(wg2s[:, 0:2], w2_g2).then_inc(const_in.sem, 16)
            sp.dma_start(wg2s[:, 2:3], b2_g1.rearrange("(p o) -> p o", o=1)).then_inc(const_in.sem, 16)
            sp.dma_start(bg2s[:, 0:2], b2_g2.rearrange("(o g) -> o g", o=1)).then_inc(const_in.sem, 16)
            sp.dma_start(posd_s[:, :, :], posd).then_inc(const_in.sem, 16)
            sp.dma_start(small[:, 6:8], b2_proj.rearrange("(p q) -> p q", q=2)).then_inc(const_in.sem, 16)
            sp.dma_start(w3raw.rearrange("p (t q f) -> p t q f", t=TAPS, q=2), w3.rearrange("y x (p q) f -> p (y x) q f", q=2)).then_inc(const_in.sem, 16)
            with nc.allow_non_contiguous_dma("parameters of single channels"):
                for a in range(2):
                    for kind in range(3):
                        sp.dma_start(bias2[:, kind, a:a + 1], b2_qkv.rearrange("(k a p o) -> k a p o", k=3, a=2, o=1)[kind, a]).then_inc(const_in.sem, 16)
                    sp.dma_start(dw2_w[:, a, :], w2_dw.rearrange("y x o (a p) -> a p (o y x)", a=2)[a]).then_inc(const_in.sem, 16)
                    sp.dma_start(small[:, 4 + a:5 + a], b2_dw.rearrange("(a p o) -> a p o", a=2, o=1)[a]).then_inc(const_in.sem, 16)
                for w, src in ((g_w, w1_g), (g1_w, w1_g1)):
                    for q in range(2):
                        sp.dma_start(w[:, q, :], src.rearrange("y x (p q) -> q p (y x)", q=2)[q]).then_inc(const_in.sem, 16)
                for q in range(2):
                    sp.dma_start(bns[:, q, :], bn1.rearrange("n (p q) -> q p n", q=2)[q]).then_inc(const_in.sem, 16)
            def load(img):
                for g in range(CHUNKS):
                    sp.dma_start(tok_in[0:TOK, g], x[img, 8 * g:8 * g + 8].rearrange("(k y) x c -> (y x) k c", k=4)).then_inc(x_in[g].sem, 16)

            sp.wait_ge(w3_made.sem, 1)
            load(0)
            with sp.Fori(0, B) as img:
                sp_project(sp, img, 0)
                sp_gather0(sp, img)
                sp.sem_inc(passed, 1)
                sp_project(sp, img, 1)
                sp_gather2(sp, img)
                sp.wait_ge(*out2_evac.at(img, NP2))
                sp.sem_inc(passed, 1)
                load((img + 1) % B)
                sp_store(sp, img)
            for g in range(CHUNKS):
                sp.wait_ge(x_in[g].sem, 16 * (B + 1))

        @block.tensor
        def _(pe):
            pe.wait_ge(const_in.sem, CONSTS)
            pe.wait_ge(wraw_in.sem, 16 * (48 + 4 + 16 + 1))
            for m in range(6):
                for q in range(2):
                    t = pe.transpose(bank[:, m, q * P:(q + 1) * P], w0raw[:, m, q::2], ident)
            for q in range(2):
                for a in range(2):
                    t = pe.transpose(bank[:, 6 + q, a * P:(a + 1) * P], o0raw[:, q, a * P:(a + 1) * P], ident)
            t.then_inc(w_turned.sem, 1)
            pe.wait_ge(w_copied.sem, 1)

            with pe.Fori(0, B) as img:
                pe.wait_ge(zeroed.sem, 1)
                pe.wait_ge(*y_evac.at(img, 0))
                pe.sem_inc(passed, 1)
                for s in range(2):
                    pe.wait_ge(*y_out[s].at(img, 0))
                    pe.sem_inc(passed, 1)
                for g in range(CHUNKS):
                    pe.wait_ge(*x_in[g].at(img, 16))
                    for q in range(2):
                        b = (2 * g + q) % 8
                        if g >= 4:
                            pe.wait_ge(*(x_evac_a, x_evac_v)[q].at(img, g - 3))
                        for k in range(4):
                            t = pe.transpose(bank[:, b, k * TOK:(k + 1) * TOK], tok_in[0:TOK, g, k, q::2], mat[0:TOK, 0, 0:TOK])
                        t.then_inc(x_turned.sem, 1)
                pe_gn(pe, img, 0)
                pe_project(pe, img, 0)
                pe_attend0(pe, img)
                pe_output(pe, img, 0)
                pe_gn(pe, img, 1)
                pe_layer1(pe, img)
                pe_gn(pe, img, 2)
                pe_project(pe, img, 1)
                pe_attend2(pe, img)
                pe_output(pe, img, 1)
                pe_gn(pe, img, 3)
                pe_layer3(pe, img)

        @block.scalar
        def _(act):
            act.wait_ge(bn_var.sem, 1)
            act.activation(bns[:, :, 3:12:4], bns[:, :, 3:12:4], ACT.Sqrt).then_inc(bn_sqrt.sem, 1)
            act.wait_ge(bn_ready.sem, 1)
            act.wait_ge(w3_half.sem, 1)
            act.activation(w3s[:, :, :, :].rearrange("p t q f -> p (t q f)"), w3raw, ACT.Sign).then_inc(w3_made.sem, 1)
            with act.Fori(0, B) as img:
                for g in range(CHUNKS):
                    act.wait_ge(*x_turned.at(img, 2 * g + 1))
                    act.activation(res[:, 0, g * CHUNK:(g + 1) * CHUNK], bank[:, (2 * g) % 8, 0:CHUNK], ACT.Copy).then_inc(x_evac_a.sem, 1)
                act_gn(act, img, 0)
                act_project(act, img, 0)
                act_attend0(act, img)
                act_output(act, img, 0)
                act_gn(act, img, 1)
                act_layer1(act, img)
                act_gn(act, img, 2)
                act_project(act, img, 1)
                act_attend2(act, img)
                act_output(act, img, 1)
                act_gn(act, img, 3)
                act.wait_ge(*xn_v.at(img, 4))
                act.wait_ge(*xn_a.at(img, 4))
                act_layer3(act, img)
                act_store(act, img)

        @block.vector
        def _(dve):
            dve.wait_ge(w_turned.sem, 1)
            for m in range(6):
                dve.tensor_copy(w0t[:, :, m // 2, m % 2, :], bank[:, m, 0:2 * P].rearrange("p (q n) -> p q n", q=2))
            for q in range(2):
                dve.tensor_copy(o0t[:, :, q, :], bank[:, 6 + q, 0:2 * P].rearrange("p (a n) -> p a n", a=2))
            dve.drain()
            dve.memset(xnp[:, :, :, :], 0.0)
            dve.drain().then_inc(w_copied.sem, 1)
            dve.drain().then_inc(zeroed.sem, 1)
            dve.wait_ge(const_in.sem, CONSTS)
            dve_bn(dve)
            dve.tensor_copy(w3half, w3raw)
            dve.drain()
            dve.tensor_copy(w3raw, w3half)
            dve.drain()
            dve.tensor_scalar(w3raw, w3raw, -1.0, 1.0, ALU.max, ALU.min)
            dve.memset(bg2s[:, 2:2 + REG2], 1.0)
            dve.drain().then_inc(w3_half.sem, 1)
            dve.wait_ge(w3_made.sem, 1)
            with dve.Fori(0, B) as img:
                for g in range(CHUNKS):
                    dve.wait_ge(*x_turned.at(img, 2 * g + 2))
                    dve.tensor_copy(res[:, 1, g * CHUNK:(g + 1) * CHUNK], bank[:, (2 * g + 1) % 8, 0:CHUNK]).then_inc(x_evac_v.sem, 1)
                    dve.wait_ge(*x_evac_a.at(img, g + 1))
                    dve.sem_inc(passed, 1)
                    dve.drain()
                    for q in range(2):
                        dve.bn_stats(stats[:, q, g, :], res[:, q, g * CHUNK:(g + 1) * CHUNK])
                dve_gn(dve, img, 0, 1e-5, pieces=CHUNKS)
                dve_project(dve, img, 0)
                dve_attend0(dve, img)
                dve_diag(dve, 1, g_w)
                dve_diag(dve, 2, g1_w, diag_g1)
                dve_output(dve, img, 0)
                dve_gn(dve, img, 1, 1e-5, pieces=R0)
                dve.wait_ge(*mirrored.at(img, 1))
                dve.sem_inc(passed, 1)
                dve_layer1(dve, img)
                dve_gn(dve, img, 2, 1e-5)
                dve_project(dve, img, 1)
                dve_attend2(dve, img)
                dve_output(dve, img, 1)
                dve_gn(dve, img, 3, 1e-5, pieces=R2)
                dve_layer3(dve, img)

        @block.gpsimd
        def _(pool):
            for st in CREDITS:
                pool.sem_inc(st.sem, st.credit)
            with pool.Fori(0, B) as img:
                pool.wait_ge(*res_done.at(img, 0))
                pool.sem_inc(passed, 1)
                pool.memset(vpad[:, :], 0.0)
                pool.drain()
                pool_project(pool, img, 0)
                pool_attend0(pool, img)
                pool_layer1(pool, img)
                pool.wait_ge(*res_done.at(img, 2))
                pool.sem_inc(passed, 1)
                pool.memset(vpad[:, :], 0.0)
                pool.drain()
                pool_project(pool, img, 1)
                pool_gather2(pool, img)


_BN1 = [f"L1_conv_{n}_{k}" for n in ("g", "g1", "out") for k in ("gamma", "beta", "mean", "var")]
_INS = ["x", "L0_conv_qkv_w", "L0_conv_qkv_b", "L0_conv_lepe_w", "L0_conv_lepe_b", "L0_conv_out_w", "L0_conv_out_b",
        "L1_conv_wg", "L1_conv_wg1", "L2_conv_w_qkv", "L2_conv_b_qkv", "L2_conv_w_g1", "L2_conv_b_g1", "L2_conv_w_g2",
        "L2_conv_b_g2", "L2_conv_dw_kernel", "L2_conv_dw_bias", "L2_conv_w_proj", "L2_conv_b_proj", "L3_conv_w"]


def shape_constants():
    mats = np.zeros((P, 6, P), np.float32)
    p = np.arange(P)
    mats[p, 0, p] = 1.0
    mats[:, 1, :] = (p[:, None] // 4 == p[None, :] // 4) / 8.0
    mats[(p - 1) % P, 2, p] = 1.0
    mats[(p + 1) % P, 3, p] = 1.0
    mats[:, 4] = mats[:, 2] - mats[:, 0]
    mats[:, 5] = mats[:, 0] - mats[:, 3]
    w = np.arange(REG2)
    posd = np.zeros((REG2, 3, REG2), np.float32)
    posd[:, 0] = (w[None, :] % R2 - w[:, None] % R2) ** 2
    posd[:, 1] = (w[None, :] // R2 - w[:, None] // R2) ** 2
    posd[:, 2] = w[None, :]
    return mats, posd


def kernel(**inputs):
    import concourse.bacc as _bacc
    from concourse.bass_utils import run_bass_kernel_spmd as _run

    nc = _bacc.Bacc("TRN2", target_bir_lowering=False, num_devices=1)
    arrays = {n: np.ascontiguousarray(inputs[n]) for n in _INS}
    arrays["bn1"] = np.stack([np.asarray(inputs[n]) for n in _BN1])
    arrays["mats"], arrays["posd"] = shape_constants()
    ap = {n: nc.dram_tensor(f"in_{n}", a.shape, mybir.dt.from_np(a.dtype), kind="ExternalInput").ap() for n, a in arrays.items()}
    out = nc.dram_tensor("out_x", arrays["x"].shape, F32, kind="ExternalOutput").ap()
    names = _INS[:9] + ["bn1"] + _INS[9:] + ["mats", "posd"]
    build_blocks(nc, *[ap[n] for n in names], out)
    r = _run(nc, [{f"in_{n}": a for n, a in arrays.items()}], core_ids=[0])
    return r.results[0]["out_x"]
```
